# Optimizing a Trainium2 kernel written in Bass

```python
import numpy as np
import jax
import jax.numpy as jnp

def _softmax(x, axis=-1):
    return jax.nn.softmax(x, axis=axis)

def _gelu(x):
    return jax.nn.gelu(x, approximate=True)

def _silu(x):
    return jax.nn.silu(x)

def _sigmoid(x):
    return jax.nn.sigmoid(x)

def _layernorm(x, axis=-1, eps=1e-05):
    m = jnp.mean(x, axis=axis, keepdims=True)
    v = jnp.var(x, axis=axis, keepdims=True)
    return (x - m) / jnp.sqrt(v + eps)

def _scatter_add(tgt, idx, src, axis=0):
    return tgt.at[idx].add(src)

def _segment_sum(src, seg, n):
    return jax.ops.segment_sum(src, seg, n)
kernel_name = 'mk_prb_d2_jaxref_r8_2c925d'

def setup_inputs(seed: int=0):
    np.random.seed(seed)
    _w = jnp.asarray

    def _L0_attn_setup():
        import jax, jax.numpy as jnp
        import numpy as np
        EMB = 128
        NH = 4
        INNER = 256
        DH = INNER // NH
        KS = 4
        QKV_BLK = 4
        NHP = INNER // QKV_BLK
        EPS = 1e-06
        LN_EPS = 1e-05

        def _headwise(x, w):
            B, S, _ = x.shape
            xh = x.reshape(B, S, NHP, QKV_BLK)
            return jnp.einsum('bshd,hod->bsho', xh, w).reshape(B, S, -1)

        def _forward(x, w_up, conv_w, conv_b, w_q, w_k, w_v, w_ig, b_ig, w_fg, b_fg, ln_w, skip, w_down):
            B, S, _ = x.shape
            x_inner = x @ w_up.T
            x_m, z = jnp.split(x_inner, 2, axis=-1)
            xc = jax.lax.conv_general_dilated(x_m.transpose(0, 2, 1), conv_w, (1,), [(KS - 1, 0)], dimension_numbers=('NCH', 'OIH', 'NCH'), feature_group_count=INNER)
            xc = (xc + conv_b[None, :, None]).transpose(0, 2, 1)
            xc = jax.nn.silu(xc)
            q = _headwise(xc, w_q)
            k = _headwise(xc, w_k)
            v = _headwise(x_m, w_v)
            ifg_in = jnp.concatenate([q, k, v], axis=-1)
            igp = (ifg_in @ w_ig.T + b_ig).transpose(0, 2, 1)
            fgp = (ifg_in @ w_fg.T + b_fg).transpose(0, 2, 1)
            qh = q.reshape(B, S, NH, DH).transpose(0, 2, 1, 3)
            kh = k.reshape(B, S, NH, DH).transpose(0, 2, 1, 3)
            vh = v.reshape(B, S, NH, DH).transpose(0, 2, 1, 3)
            log_f = jax.nn.log_sigmoid(fgp)
            lc = jnp.concatenate([jnp.zeros((B, NH, 1), x.dtype), jnp.cumsum(log_f, axis=-1)], axis=-1)
            log_fg_mat = lc[:, :, 1:, None] - lc[:, :, None, 1:]
            ltr = jnp.tril(jnp.ones((S, S), bool))
            log_fg_mat = jnp.where(ltr, log_fg_mat, -jnp.inf)
            log_D = log_fg_mat + igp[:, :, None, :]
            max_log_D = jnp.max(log_D, axis=-1, keepdims=True)
            D = jnp.exp(log_D - max_log_D)
            qk = jnp.einsum('bhsd,bhtd->bhst', qh, kh) / float(np.sqrt(DH))
            C = qk * D
            normalizer = jnp.maximum(jnp.abs(C.sum(-1, keepdims=True)), jnp.exp(-max_log_D))
            h = jnp.einsum('bhst,bhtd->bhsd', C / (normalizer + EPS), vh)
            mu = h.mean(-1, keepdims=True)
            var = h.var(-1, keepdims=True)
            hn = (h - mu) / jnp.sqrt(var + LN_EPS) * ln_w[None, :, None, :]
            h_flat = hn.transpose(0, 2, 1, 3).reshape(B, S, INNER)
            h_skip = h_flat + skip * xc
            h_state = h_skip * jax.nn.silu(z)
            return h_state @ w_down.T
        key = jax.random.key(seed)
        ks = jax.random.split(key, 10)
        B, S = (4, 256)
        small_std = float(np.sqrt(2.0 / (5.0 * EMB)))
        blk_std = float(np.sqrt(2.0 / (5.0 * QKV_BLK)))
        return {'x': jax.random.normal(ks[0], (B, S, EMB), jnp.float32), 'w_up': jax.random.normal(ks[1], (2 * INNER, EMB), jnp.float32) * small_std, 'conv_w': jax.random.normal(ks[2], (INNER, 1, KS), jnp.float32) * 0.3, 'conv_b': jnp.zeros((INNER,), jnp.float32), 'w_q': jax.random.normal(ks[3], (NHP, QKV_BLK, QKV_BLK), jnp.float32) * blk_std, 'w_k': jax.random.normal(ks[4], (NHP, QKV_BLK, QKV_BLK), jnp.float32) * blk_std, 'w_v': jax.random.normal(ks[5], (NHP, QKV_BLK, QKV_BLK), jnp.float32) * blk_std, 'w_ig': jax.random.normal(ks[6], (NH, 3 * INNER), jnp.float32) * 0.01, 'b_ig': jnp.full((NH,), -2.0, jnp.float32), 'w_fg': jnp.zeros((NH, 3 * INNER), jnp.float32), 'b_fg': jnp.linspace(3.0, 6.0, NH).astype(jnp.float32), 'ln_w': jnp.ones((NH, DH), jnp.float32), 'skip': jnp.ones((INNER,), jnp.float32), 'w_down': jax.random.normal(ks[7], (EMB, INNER), jnp.float32) * (2.0 / float(np.sqrt(INNER)))}
    _L0_attn_in = _L0_attn_setup()

    def _L0_ffn_setup():
        import jax, jax.numpy as jnp
        import numpy as np
        H = 16
        TOP_K = 2
        LN_EPS = 1e-05
        key = jax.random.key(seed)
        ks = jax.random.split(key, 8)
        B, S, E, NE = (2, 128, 128, 8)
        w = lambda k, shp: jax.random.normal(k, shp, dtype=jnp.float32) * 0.02
        return {'x': jax.random.normal(ks[0], (B, S, E), dtype=jnp.float32), 'rW1': w(ks[1], (E // 2, E)), 'rb1': jnp.zeros((E // 2,), jnp.float32), 'ln_g': jnp.ones((E // 2,), jnp.float32), 'ln_b': jnp.zeros((E // 2,), jnp.float32), 'rW2': w(ks[2], (NE, E // 2)), 'rb2': jnp.zeros((NE,), jnp.float32), 'qW': w(ks[3], (NE, E, E)), 'qb': jnp.zeros((NE, E), jnp.float32), 'kW': w(ks[4], (NE, E, E)), 'kb': jnp.zeros((NE, E), jnp.float32), 'vW': w(ks[5], (NE, E, E)), 'vb': jnp.zeros((NE, E), jnp.float32), 'oW': w(ks[6], (NE, E, E)), 'ob': jnp.zeros((NE, E), jnp.float32)}
    _L0_ffn_in = _L0_ffn_setup()

    def _L1_attn_setup():
        import jax, jax.numpy as jnp
        import numpy as np
        E = 128
        H = 16
        HD = E // H
        R = 8
        T, B = (256, 2)

        def _dora_linear(x, m, V, A, Bm, b):
            Vu = V + Bm @ A
            W = m / (jnp.linalg.norm(Vu) + 1e-08) * Vu
            return x @ W.T + b
        key = jax.random.key(seed)
        ks = jax.random.split(key, 16)
        query = jax.random.normal(ks[0], (T, B, E), dtype=jnp.float32)
        kk = jax.random.normal(ks[1], (T, B, E), dtype=jnp.float32)
        vv = jax.random.normal(ks[2], (T, B, E), dtype=jnp.float32)

        def make_dora(k1, k2, k3, k4):
            w = jax.random.normal(k1, (E, E), dtype=jnp.float32) * E ** (-0.5)
            m = jnp.linalg.norm(w)
            V = w / m
            A = jax.random.normal(k2, (R, E), dtype=jnp.float32) * E ** (-0.5)
            Bm = jax.random.normal(k3, (E, R), dtype=jnp.float32) * 0.01
            b = jax.random.normal(k4, (E,), dtype=jnp.float32) * 0.01
            return (m, V, A, Bm, b)
        mag_q, dir_q, A_q, B_q, bias_q = make_dora(ks[3], ks[4], ks[5], ks[6])
        mag_v, dir_v, A_v, B_v, bias_v = make_dora(ks[7], ks[8], ks[9], ks[10])
        k_w = jax.random.normal(ks[11], (E, E), dtype=jnp.float32) * E ** (-0.5)
        k_b = jax.random.normal(ks[12], (E,), dtype=jnp.float32) * 0.01
        out_w = jax.random.normal(ks[13], (E, E), dtype=jnp.float32) * E ** (-0.5)
        out_b = jax.random.normal(ks[14], (E,), dtype=jnp.float32) * 0.01
        return dict(query=query, key=kk, value=vv, mag_q=mag_q, dir_q=dir_q, A_q=A_q, B_q=B_q, bias_q=bias_q, mag_v=mag_v, dir_v=dir_v, A_v=A_v, B_v=B_v, bias_v=bias_v, k_w=k_w, k_b=k_b, out_w=out_w, out_b=out_b)
    _L1_attn_in = _L1_attn_setup()

    def _L1_ffn_setup():
        import jax, jax.numpy as jnp
        import numpy as np
        BLOCK = 16
        _GRID = jnp.array([0.0, 0.5, 1.0, 1.5, 2.0, 3.0, 4.0, 6.0], dtype=jnp.float32)
        _MID = jnp.array([0.25, 0.75, 1.25, 1.75, 2.5, 3.5, 5.0], dtype=jnp.float32)

        def fp4_quant_dequant(x):
            shape = x.shape
            xb = x.reshape(shape[:-1] + (shape[-1] // BLOCK, BLOCK))
            scale = jnp.max(jnp.abs(xb), axis=-1, keepdims=True) / 6.0
            scale = jnp.maximum(scale, jnp.float32(1e-12))
            xn = xb / scale
            idx = jnp.searchsorted(_MID, jnp.abs(xn))
            q = _GRID[idx] * jnp.sign(xn) * scale
            return q.reshape(shape)

        def fp4_linear(x, w):
            xq = fp4_quant_dequant(x)
            wq = fp4_quant_dequant(w)
            return jnp.einsum('bsk,nk->bsn', xq, wq)
        key = jax.random.key(seed)
        k1, k2, k3, k4 = jax.random.split(key, 4)
        H, I = (128, 352)
        x = jax.random.normal(k1, (4, 512, H), dtype=jnp.float32)
        w_gate = jax.random.normal(k2, (I, H), dtype=jnp.float32) * 0.02
        w_up = jax.random.normal(k3, (I, H), dtype=jnp.float32) * 0.02
        w_down = jax.random.normal(k4, (H, I), dtype=jnp.float32) * 0.02
        return {'x': x, 'w_gate': w_gate, 'w_up': w_up, 'w_down': w_down}
    _L1_ffn_in = _L1_ffn_setup()
    _d = {'L0_attn_x': _L0_attn_in['x'], 'L0_attn_w_up': _L0_attn_in['w_up'], 'L0_attn_conv_w': _L0_attn_in['conv_w'], 'L0_attn_conv_b': _L0_attn_in['conv_b'], 'L0_attn_w_q': _L0_attn_in['w_q'], 'L0_attn_w_k': _L0_attn_in['w_k'], 'L0_attn_w_v': _L0_attn_in['w_v'], 'L0_attn_w_ig': _L0_attn_in['w_ig'], 'L0_attn_b_ig': _L0_attn_in['b_ig'], 'L0_attn_w_fg': _L0_attn_in['w_fg'], 'L0_attn_b_fg': _L0_attn_in['b_fg'], 'L0_attn_ln_w': _L0_attn_in['ln_w'], 'L0_attn_skip': _L0_attn_in['skip'], 'L0_attn_w_down': _L0_attn_in['w_down'], 'L0_ffn_rW1': _L0_ffn_in['rW1'], 'L0_ffn_rb1': _L0_ffn_in['rb1'], 'L0_ffn_ln_g': _L0_ffn_in['ln_g'], 'L0_ffn_ln_b': _L0_ffn_in['ln_b'], 'L0_ffn_rW2': _L0_ffn_in['rW2'], 'L0_ffn_rb2': _L0_ffn_in['rb2'], 'L0_ffn_qW': _L0_ffn_in['qW'], 'L0_ffn_qb': _L0_ffn_in['qb'], 'L0_ffn_kW': _L0_ffn_in['kW'], 'L0_ffn_kb': _L0_ffn_in['kb'], 'L0_ffn_vW': _L0_ffn_in['vW'], 'L0_ffn_vb': _L0_ffn_in['vb'], 'L0_ffn_oW': _L0_ffn_in['oW'], 'L0_ffn_ob': _L0_ffn_in['ob'], 'L1_attn_key': _L1_attn_in['key'], 'L1_attn_value': _L1_attn_in['value'], 'L1_attn_mag_q': _L1_attn_in['mag_q'], 'L1_attn_dir_q': _L1_attn_in['dir_q'], 'L1_attn_A_q': _L1_attn_in['A_q'], 'L1_attn_B_q': _L1_attn_in['B_q'], 'L1_attn_bias_q': _L1_attn_in['bias_q'], 'L1_attn_mag_v': _L1_attn_in['mag_v'], 'L1_attn_dir_v': _L1_attn_in['dir_v'], 'L1_attn_A_v': _L1_attn_in['A_v'], 'L1_attn_B_v': _L1_attn_in['B_v'], 'L1_attn_bias_v': _L1_attn_in['bias_v'], 'L1_attn_k_w': _L1_attn_in['k_w'], 'L1_attn_k_b': _L1_attn_in['k_b'], 'L1_attn_out_w': _L1_attn_in['out_w'], 'L1_attn_out_b': _L1_attn_in['out_b'], 'L1_ffn_w_gate': _L1_ffn_in['w_gate'], 'L1_ffn_w_up': _L1_ffn_in['w_up'], 'L1_ffn_w_down': _L1_ffn_in['w_down']}
    _x0 = _d['L0_attn_x']
    _d['L0_attn_x'] = jax.random.normal(jax.random.fold_in(jax.random.key(seed), 1), (8, 512, 128), dtype=_x0.dtype)
    del _x0
    return _d

def reference(L0_attn_x, L0_attn_w_up, L0_attn_conv_w, L0_attn_conv_b, L0_attn_w_q, L0_attn_w_k, L0_attn_w_v, L0_attn_w_ig, L0_attn_b_ig, L0_attn_w_fg, L0_attn_b_fg, L0_attn_ln_w, L0_attn_skip, L0_attn_w_down, L0_ffn_rW1, L0_ffn_rb1, L0_ffn_ln_g, L0_ffn_ln_b, L0_ffn_rW2, L0_ffn_rb2, L0_ffn_qW, L0_ffn_qb, L0_ffn_kW, L0_ffn_kb, L0_ffn_vW, L0_ffn_vb, L0_ffn_oW, L0_ffn_ob, L1_attn_key, L1_attn_value, L1_attn_mag_q, L1_attn_dir_q, L1_attn_A_q, L1_attn_B_q, L1_attn_bias_q, L1_attn_mag_v, L1_attn_dir_v, L1_attn_A_v, L1_attn_B_v, L1_attn_bias_v, L1_attn_k_w, L1_attn_k_b, L1_attn_out_w, L1_attn_out_b, L1_ffn_w_gate, L1_ffn_w_up, L1_ffn_w_down):

    def _L0_attn_ref(x, w_up, conv_w, conv_b, w_q, w_k, w_v, w_ig, b_ig, w_fg, b_fg, ln_w, skip, w_down):
        import jax, jax.numpy as jnp
        import numpy as np
        EMB = 128
        NH = 4
        INNER = 256
        DH = INNER // NH
        KS = 4
        QKV_BLK = 4
        NHP = INNER // QKV_BLK
        EPS = 1e-06
        LN_EPS = 1e-05

        def _headwise(x, w):
            B, S, _ = x.shape
            xh = x.reshape(B, S, NHP, QKV_BLK)
            return jnp.einsum('bshd,hod->bsho', xh, w).reshape(B, S, -1)

        def _forward(x, w_up, conv_w, conv_b, w_q, w_k, w_v, w_ig, b_ig, w_fg, b_fg, ln_w, skip, w_down):
            B, S, _ = x.shape
            x_inner = x @ w_up.T
            x_m, z = jnp.split(x_inner, 2, axis=-1)
            xc = jax.lax.conv_general_dilated(x_m.transpose(0, 2, 1), conv_w, (1,), [(KS - 1, 0)], dimension_numbers=('NCH', 'OIH', 'NCH'), feature_group_count=INNER)
            xc = (xc + conv_b[None, :, None]).transpose(0, 2, 1)
            xc = jax.nn.silu(xc)
            q = _headwise(xc, w_q)
            k = _headwise(xc, w_k)
            v = _headwise(x_m, w_v)
            ifg_in = jnp.concatenate([q, k, v], axis=-1)
            igp = (ifg_in @ w_ig.T + b_ig).transpose(0, 2, 1)
            fgp = (ifg_in @ w_fg.T + b_fg).transpose(0, 2, 1)
            qh = q.reshape(B, S, NH, DH).transpose(0, 2, 1, 3)
            kh = k.reshape(B, S, NH, DH).transpose(0, 2, 1, 3)
            vh = v.reshape(B, S, NH, DH).transpose(0, 2, 1, 3)
            log_f = jax.nn.log_sigmoid(fgp)
            lc = jnp.concatenate([jnp.zeros((B, NH, 1), x.dtype), jnp.cumsum(log_f, axis=-1)], axis=-1)
            log_fg_mat = lc[:, :, 1:, None] - lc[:, :, None, 1:]
            ltr = jnp.tril(jnp.ones((S, S), bool))
            log_fg_mat = jnp.where(ltr, log_fg_mat, -jnp.inf)
            log_D = log_fg_mat + igp[:, :, None, :]
            max_log_D = jnp.max(log_D, axis=-1, keepdims=True)
            D = jnp.exp(log_D - max_log_D)
            qk = jnp.einsum('bhsd,bhtd->bhst', qh, kh) / float(np.sqrt(DH))
            C = qk * D
            normalizer = jnp.maximum(jnp.abs(C.sum(-1, keepdims=True)), jnp.exp(-max_log_D))
            h = jnp.einsum('bhst,bhtd->bhsd', C / (normalizer + EPS), vh)
            mu = h.mean(-1, keepdims=True)
            var = h.var(-1, keepdims=True)
            hn = (h - mu) / jnp.sqrt(var + LN_EPS) * ln_w[None, :, None, :]
            h_flat = hn.transpose(0, 2, 1, 3).reshape(B, S, INNER)
            h_skip = h_flat + skip * xc
            h_state = h_skip * jax.nn.silu(z)
            return h_state @ w_down.T
        return _forward(x, w_up, conv_w, conv_b, w_q, w_k, w_v, w_ig, b_ig, w_fg, b_fg, ln_w, skip, w_down)

    def _L0_ffn_ref(x, rW1, rb1, ln_g, ln_b, rW2, rb2, qW, qb, kW, kb, vW, vb, oW, ob):
        import jax, jax.numpy as jnp
        import numpy as np
        H = 16
        TOP_K = 2
        LN_EPS = 1e-05
        B, S, E = x.shape
        NE = qW.shape[0]
        Dh = E // H
        scale = 1.0 / jnp.sqrt(jnp.asarray(Dh, x.dtype))
        h = x @ rW1.T + rb1
        mu = h.mean(-1, keepdims=True)
        var = ((h - mu) ** 2).mean(-1, keepdims=True)
        h = (h - mu) * jax.lax.rsqrt(var + LN_EPS) * ln_g + ln_b
        h = jax.nn.relu(h)
        logits = h @ rW2.T + rb2
        probs = jax.nn.softmax(logits, axis=-1)
        tp, ti = jax.lax.top_k(probs, TOP_K)
        tp = tp / tp.sum(-1, keepdims=True)
        expert_mask = (jax.nn.one_hot(ti, NE, dtype=probs.dtype) * tp[..., None]).sum(-2)
        gates = jnp.moveaxis(expert_mask, -1, 0)

        def expert_step(acc, params):
            qw, qb_, kw, kb_, vw, vb_, ow, ob_, g = params
            q = (x @ qw.T + qb_).reshape(B, S, H, Dh).transpose(0, 2, 1, 3)
            k = (x @ kw.T + kb_).reshape(B, S, H, Dh).transpose(0, 2, 1, 3)
            v = (x @ vw.T + vb_).reshape(B, S, H, Dh).transpose(0, 2, 1, 3)
            scores = jnp.einsum('bhqd,bhkd->bhqk', q, k) * scale
            p = jax.nn.softmax(scores, axis=-1)
            o = jnp.einsum('bhqk,bhkd->bhqd', p, v)
            o = o.transpose(0, 2, 1, 3).reshape(B, S, E) @ ow.T + ob_
            return (acc + o * g[..., None], None)
        out, _ = jax.lax.scan(expert_step, jnp.zeros_like(x), (qW, qb, kW, kb, vW, vb, oW, ob, gates))
        return out

    def _L1_attn_ref(query, key, value, mag_q, dir_q, A_q, B_q, bias_q, mag_v, dir_v, A_v, B_v, bias_v, k_w, k_b, out_w, out_b):
        import jax, jax.numpy as jnp
        import numpy as np
        E = 128
        H = 16
        HD = E // H
        R = 8
        T, B = (256, 2)

        def _dora_linear(x, m, V, A, Bm, b):
            Vu = V + Bm @ A
            W = m / (jnp.linalg.norm(Vu) + 1e-08) * Vu
            return x @ W.T + b
        Tq, Bq, _ = query.shape
        q = _dora_linear(query, mag_q, dir_q, A_q, B_q, bias_q)
        k = query @ k_w.T + k_b
        v = _dora_linear(query, mag_v, dir_v, A_v, B_v, bias_v)
        q = q.reshape(Tq, Bq * H, HD).transpose(1, 0, 2)
        k = k.reshape(Tq, Bq * H, HD).transpose(1, 0, 2)
        v = v.reshape(Tq, Bq * H, HD).transpose(1, 0, 2)
        scale = HD ** (-0.5)
        attn = jnp.einsum('nqd,nkd->nqk', q, k) * scale
        attn = jax.nn.softmax(attn, axis=-1)
        out = jnp.einsum('nqk,nkd->nqd', attn, v)
        out = out.transpose(1, 0, 2).reshape(Tq, Bq, E)
        out = out @ out_w.T + out_b
        return out

    def _L1_ffn_ref(x, w_gate, w_up, w_down):
        import jax, jax.numpy as jnp
        import numpy as np
        BLOCK = 16
        _GRID = jnp.array([0.0, 0.5, 1.0, 1.5, 2.0, 3.0, 4.0, 6.0], dtype=jnp.float32)
        _MID = jnp.array([0.25, 0.75, 1.25, 1.75, 2.5, 3.5, 5.0], dtype=jnp.float32)

        def fp4_quant_dequant(x):
            shape = x.shape
            xb = x.reshape(shape[:-1] + (shape[-1] // BLOCK, BLOCK))
            scale = jnp.max(jnp.abs(xb), axis=-1, keepdims=True) / 6.0
            scale = jnp.maximum(scale, jnp.float32(1e-12))
            xn = xb / scale
            idx = jnp.searchsorted(_MID, jnp.abs(xn))
            q = _GRID[idx] * jnp.sign(xn) * scale
            return q.reshape(shape)

        def fp4_linear(x, w):
            xq = fp4_quant_dequant(x)
            wq = fp4_quant_dequant(w)
            return jnp.einsum('bsk,nk->bsn', xq, wq)
        gate = fp4_linear(x, w_gate)
        y = fp4_linear(x, w_up)
        h = jax.nn.silu(gate) * y
        return fp4_linear(h, w_down)
    x = L0_attn_x
    xn = _layernorm(x, axis=-1)
    x = x + _L0_attn_ref(xn, L0_attn_w_up, L0_attn_conv_w, L0_attn_conv_b, L0_attn_w_q, L0_attn_w_k, L0_attn_w_v, L0_attn_w_ig, L0_attn_b_ig, L0_attn_w_fg, L0_attn_b_fg, L0_attn_ln_w, L0_attn_skip, L0_attn_w_down) + _L0_ffn_ref(xn, L0_ffn_rW1, L0_ffn_rb1, L0_ffn_ln_g, L0_ffn_ln_b, L0_ffn_rW2, L0_ffn_rb2, L0_ffn_qW, L0_ffn_qb, L0_ffn_kW, L0_ffn_kb, L0_ffn_vW, L0_ffn_vb, L0_ffn_oW, L0_ffn_ob)
    xn = _layernorm(x, axis=-1)
    x = x + _L1_attn_ref(xn, L1_attn_key, L1_attn_value, L1_attn_mag_q, L1_attn_dir_q, L1_attn_A_q, L1_attn_B_q, L1_attn_bias_q, L1_attn_mag_v, L1_attn_dir_v, L1_attn_A_v, L1_attn_B_v, L1_attn_bias_v, L1_attn_k_w, L1_attn_k_b, L1_attn_out_w, L1_attn_out_b) + _L1_ffn_ref(xn, L1_ffn_w_gate, L1_ffn_w_up, L1_ffn_w_down)
    return x

_drawn_inputs = setup_inputs


def setup_inputs(seed=0):
    import zlib

    import numpy as np

    out = dict(_drawn_inputs(seed))
    spreads = {'L0_attn_conv_b': (0.0, 0.1),
     'L0_attn_b_ig': (-2.0, 0.2),
     'L0_attn_w_fg': (0.0, 0.1),
     'L0_attn_ln_w': (1.0, 0.2),
     'L0_attn_skip': (1.0, 0.2),
     'L0_ffn_rb1': (0.0, 0.1),
     'L0_ffn_ln_g': (1.0, 0.2),
     'L0_ffn_ln_b': (0.0, 0.341),
     'L0_ffn_rb2': (0.0, 0.1),
     'L0_ffn_qb': (0.0, 0.8),
     'L0_ffn_kb': (0.0, 2.0),
     'L0_ffn_vb': (0.0, 0.519),
     'L0_ffn_ob': (0.0, 0.1)}
    factors = {'L0_ffn_qW': 8.0,
     'L0_ffn_kW': 8.0,
     'L0_ffn_vW': 8.0,
     'L0_ffn_oW': 3.761,
     'L1_attn_bias_q': 64.0,
     'L1_attn_bias_v': 28.787,
     'L1_attn_k_b': 64.0,
     'L1_attn_out_b': 31.294,
     'L1_ffn_w_gate': 7.515,
     'L1_ffn_w_up': 7.379,
     'L1_ffn_w_down': 7.38,
     'L1_attn_A_q': 2.845,
     'L1_attn_B_q': 2.732}
    for name, (base, spread) in spreads.items():
        noise = np.random.default_rng([zlib.crc32(name.encode()), seed]).standard_normal(out[name].shape)
        drawn = base * np.exp(spread * noise) if base else spread * noise
        out[name] = jnp.asarray(drawn.astype(out[name].dtype))
    for name, factor in factors.items():
        out[name] = (out[name] * factor).astype(out[name].dtype)
    return out
```

```python
from contextlib import ExitStack

import concourse.bass as bass
from concourse import mybir

F32 = mybir.dt.float32
BF16 = mybir.dt.bfloat16
I32 = mybir.dt.int32
U32 = mybir.dt.uint32
ACT = mybir.ActivationFunctionType
ALU = mybir.AluOpType
AX = mybir.AxisListType

P = 128
NB, S, E = 8, 512, 128
SC = S // P
NCH = NB * SC
NE, NH, HD = 8, 16, 8
NT = 15
TILES = NB * NT
LN_EPS = 1e-5
KQ = 48
QPART = (0, 0, 1, 0, 1, 2)
KPART = (0, 1, 0, 2, 1, 0)
INNER, MH, MD = 256, 4, 64
FF = 352
QB = 16


class Chain:

    def __init__(self, eng, sem, base=0):
        self.eng, self.sem, self.base, self.n = eng, sem, base, 0

    def add(self, ins):
        self.n += 1
        ins.then_inc(self.sem, 1)

    def settle(self):
        self.eng.wait_ge(self.sem, self.base + self.n)

    def link(self, ins):
        self.add(ins)
        self.settle()


def tools(nc, ctx, tag):
    def sb(name, shape, dt=F32):
        return ctx.enter_context(nc.sbuf_tensor(f"{tag}_{name}", shape, dt))

    def ps(name, shape, dt=F32):
        return ctx.enter_context(nc.psum_tensor(f"{tag}_{name}", shape, dt))

    def sem(name):
        s = ctx.enter_context(nc.semaphore(f"{tag}_{name}"))
        MADE.append(s)
        return s

    MADE.clear()
    return sb, ps, sem


MADE = []


def clear(nc):
    with nc.Block() as block:
        @block.sync
        def _(sp):
            for s in MADE:
                sp.sem_clear(s)




def bc(ap, shape):
    return ap.to_broadcast(shape)


def norm_phase(nc, tag, x_dram, xn_dram, xnT_dram, identity, adds=(), sum_dram=None):
    x_v = x_dram.rearrange("b (c p) e -> p (b c) e", p=P)
    xn_v = xn_dram.rearrange("b (c p) e -> p (b c) e", p=P)
    with ExitStack() as ctx:
        sb, ps, sem = tools(nc, ctx, tag)
        x = sb("x", [P, NCH, E])
        xn = sb("xn", [P, NCH, E])
        xnT = sb("xnT", [P, NCH * P])
        ident = sb("ident", [P, P])
        stats = sb("stats", [P, NCH, 6])
        mv = sb("mv", [P, NCH, 2])
        ve = sb("ve", [P, NCH])
        half = sb("half", [P, NCH])
        rstd = sb("rstd", [P, NCH])
        tp = [ps(f"tp{i}", [P, SC * P]) for i in range(2)]
        more = [sb(f"more{i}", [P, NCH, E]) for i in range(len(adds))]
        loaded, ident_loaded, half_set, var_ready, rstd_ready, xn_ready, turned, taken, stored, own = (
            sem(n) for n in ("loaded", "ident_loaded", "half_set", "var_ready", "rstd_ready", "xn_ready",
                             "turned", "taken", "stored", "own"))
        if adds:
            clear(nc)
        block = ctx.enter_context(nc.Block())

        @block.sync
        def _(sp):
            for b in range(NB):
                sp.dma_start(x[:, b * SC:(b + 1) * SC, :], x_v[:, b * SC:(b + 1) * SC, :]).then_inc(loaded, 16)
                for t, source in zip(more, adds):
                    sp.dma_start(t[:, b * SC:(b + 1) * SC, :], source(b)).then_inc(loaded, 16)
                if b == 0:
                    sp.dma_start(ident[:, :], identity).then_inc(ident_loaded, 16)
            for b in range(NB):
                sp.wait_ge(xn_ready, (b + 1) * SC)
                if adds:
                    sp.dma_start(sum_dram.rearrange("b (c p) e -> p (b c) e", p=P)[:, b * SC:(b + 1) * SC, :],
                                 x[:, b * SC:(b + 1) * SC, :]).then_inc(stored, 16)
                sp.dma_start(xn_v[:, b * SC:(b + 1) * SC, :], xn[:, b * SC:(b + 1) * SC, :]).then_inc(stored, 16)
                sp.wait_ge(taken, b + 1)
                sp.dma_start(xnT_dram[:, b * S:(b + 1) * S], xnT[:, b * S:(b + 1) * S]).then_inc(stored, 16)
            sp.wait_ge(stored, (48 if adds else 32) * NB)

        @block.gpsimd
        def _(pool):
            pool.memset(half[:, :], -0.5).then_inc(half_set, 1)
            pool.wait_ge(half_set, 1)
            pool.wait_ge(var_ready, 1)
            pool.tensor_tensor(rstd[:, :], ve[:, :], half[:, :], ALU.pow).then_inc(rstd_ready, 1)

        @block.vector
        def _(dve):
            chain = Chain(dve, own)
            dve.wait_ge(loaded, 16 * NB * (1 + len(adds)))
            for t in more:
                chain.link(dve.tensor_tensor(x[:, :, :], x[:, :, :], t[:, :, :], ALU.add))
            for c in range(NCH):
                chain.add(dve.bn_stats(stats[:, c, :], x[:, c, :]))
            chain.settle()
            for c in range(NCH):
                chain.add(dve.bn_aggr(mv[:, c, :], stats[:, c, :]))
            chain.settle()
            dve.tensor_scalar(ve[:, :], mv[:, :, 1], LN_EPS, None, ALU.add).then_inc(var_ready, 1)
            dve.wait_ge(rstd_ready, 1)
            for c in range(NCH):
                dve.tensor_scalar(xn[:, c, :], x[:, c, :], mv[:, c, 0:1], rstd[:, c:c + 1],
                                  ALU.subtract, ALU.mult).then_inc(xn_ready, 1)

        @block.tensor
        def _(pe):
            pe.wait_ge(ident_loaded, 16)
            for b in range(NB):
                pe.wait_ge(xn_ready, (b + 1) * SC)
                if b >= 2:
                    pe.wait_ge(taken, b - 1)
                for c in range(SC):
                    last = pe.transpose(tp[b % 2][:, c * P:(c + 1) * P], xn[:, b * SC + c, :], ident[:, :])
                last.then_inc(turned, 1)

        @block.scalar
        def _(act):
            for b in range(NB):
                act.wait_ge(turned, b + 1)
                act.activation(xnT[:, b * S:(b + 1) * S], tp[b % 2][:, :], ACT.Copy).then_inc(taken, 1)


def router_phase(nc, d, xnT_dram, route_dram, texp_dram):
    with ExitStack() as ctx:
        sb, ps, sem = tools(nc, ctx, "rt")
        R = 64
        xnT = sb("xnT", [P, NCH * P])
        w1 = sb("w1", [P, R])
        b1 = sb("b1", [1, R])
        w2 = sb("w2", [R, NE])
        b2 = sb("b2", [1, NE])
        gain = sb("gain", [P, R])
        shift = sb("shift", [P, R])
        ident = sb("ident", [P, P])
        lower = sb("lower", [P, P])
        ones = sb("ones", [P, P])
        iota8 = sb("iota8", [P, NE])
        tstart = sb("tstart", [P, NT])
        bstart = sb("bstart", [P, TILES])
        h = sb("h", [P, NCH, R])
        stats = sb("stats", [P, NCH, 6])
        mv = sb("mv", [P, NCH, 2])
        ve = sb("ve", [P, NCH])
        half = sb("half", [P, NCH])
        rstd = sb("rstd", [P, NCH])
        hT = sb("hT", [R, NCH * P])
        lg = sb("lg", [P, NCH, NE])
        mx = sb("mx", [P, NCH])
        sm = sb("sm", [P, NCH])
        top = sb("top", [P, NCH, 8])
        idx = sb("idx", [P, NCH, 8], U32)
        idf = sb("idf", [P, NCH, 2])
        m1 = sb("m1", [P, NCH, NE])
        m2 = sb("m2", [P, NCH, NE])
        g1 = sb("g1", [P, NCH, NE])
        g2 = sb("g2", [P, NCH, NE])
        den = sb("den", [P, NCH])
        w = sb("w", [P, NCH, 2])
        rank = sb("rank", [P, NB, SC, NE])
        tot = sb("tot", [P, NB, SC, NE])
        cnt = sb("cnt", [P, NB, NE])
        pc = sb("pc", [P, NB, NE])
        tmp = sb("tmp", [P, NB, NE])
        off = sb("off", [P, NB, NE])
        end = sb("end", [P, NB, NE])
        cmp = sb("cmp", [P, NB, NT, NE])
        tx = sb("tx", [P, 2, TILES])
        txi = sb("txi", [P, 2, TILES], I32)
        route = sb("route", [P, NB * NE, 2 * SC])
        hp = [ps(f"hp{i}", [P, 8 * R]) for i in range(2)]
        tp = [ps(f"tp{i}", [P, 4 * P]) for i in range(2)]
        lp = ps("lp", [P, NCH * NE])
        rp = ps("rp", [P, 2 * NCH * NE])
        loaded, half_set, h_ready, h_taken, var_ready, rstd_ready, act_ready, turned, hT_taken, lg_ready, \
            sub_ready, exp_ready, mask_ready, rank_ready, table_ready, stored, own = (
                sem(n) for n in ("loaded", "half_set", "h_ready", "h_taken", "var_ready", "rstd_ready",
                                 "act_ready", "turned", "hT_taken", "lg_ready", "sub_ready", "exp_ready",
                                 "mask_ready", "rank_ready", "table_ready", "stored", "own"))
        block = ctx.enter_context(nc.Block())
        G = NCH // 8

        @block.sync
        def _(sp):
            loads = [(xnT[:, :], xnT_dram[:, :]), (w1[:, :], d["rW1T"]), (b1[:, :], d["rb1"]), (w2[:, :], d["rW2T"]),
                     (b2[:, :], d["rb2"]), (gain[:, :], d["ln_g"].partition_broadcast(P)),
                     (shift[:, :], d["ln_b"].partition_broadcast(P)), (ident[:, :], d["identity"]),
                     (lower[:, :], d["lower"]), (iota8[:, :], d["iota8"]), (tstart[:, :], d["tile_start"]),
                     (bstart[:, :], d["batch_start"])]
            for dst, src in loads:
                sp.dma_start(dst, src).then_inc(loaded, 16)
            sp.wait_ge(table_ready, 1)
            sp.dma_start(route_dram[:, :, :], route[:, :, :]).then_inc(stored, 16)
            sp.dma_start(texp_dram[:, :], txi[0:1, :, :].rearrange("p i t -> p (i t)")).then_inc(stored, 16)
            sp.wait_ge(stored, 32)

        @block.gpsimd
        def _(pool):
            pool.memset(half[:, :], -0.5).then_inc(half_set, 1)
            pool.memset(ones[:, :], 1.0).then_inc(half_set, 1)
            pool.wait_ge(half_set, 2)
            pool.wait_ge(var_ready, 1)
            pool.tensor_tensor(rstd[:, :], ve[:, :], half[:, :], ALU.pow).then_inc(rstd_ready, 1)

        @block.tensor
        def _(pe):
            pe.wait_ge(loaded, 16 * 12)
            pe.wait_ge(half_set, 2)
            for g in range(G):
                if g >= 2:
                    pe.wait_ge(h_taken, g - 1)
                for i in range(8):
                    o = hp[g % 2][:, i * R:(i + 1) * R]
                    pe.matmul(o, xnT[:, (8 * g + i) * P:(8 * g + i + 1) * P], w1[:, :], start=True, stop=False)
                    last = pe.matmul(o, ones[0:1, :], b1[:, :], start=False, stop=True)
                last.then_inc(h_ready, 1)
            for g in range(NCH // 4):
                if g == 0:
                    pe.wait_ge(act_ready, 1)
                if g >= 2:
                    pe.wait_ge(hT_taken, g - 1)
                for i in range(4):
                    last = pe.transpose(tp[g % 2][0:R, i * P:(i + 1) * P], h[:, 4 * g + i, :], ident[:, :])
                last.then_inc(turned, 1)
            pe.wait_ge(hT_taken, NCH // 4)
            for c in range(NCH):
                o = lp[:, c * NE:(c + 1) * NE]
                pe.matmul(o, hT[:, c * P:(c + 1) * P], w2[:, :], start=True, stop=False)
                last = pe.matmul(o, ones[0:1, :], b2[:, :], start=False, stop=True)
            last.then_inc(lg_ready, 1)
            pe.wait_ge(mask_ready, 1)
            mask = m1[:, :, :].rearrange("p c e -> p (c e)")
            pe.matmul(rp[:, 0:NCH * NE], lower[:, :], mask, start=True, stop=True)
            pe.matmul(rp[:, NCH * NE:2 * NCH * NE], ones[:, :], mask, start=True, stop=True).then_inc(rank_ready, 1)

        @block.scalar
        def _(act):
            for g in range(G):
                act.wait_ge(h_ready, g + 1)
                act.activation(h[:, 8 * g:8 * g + 8, :], hp[g % 2][:, :].rearrange("p (c r) -> p c r", c=8),
                               ACT.Copy).then_inc(h_taken, 1)
            for g in range(NCH // 4):
                act.wait_ge(turned, g + 1)
                act.activation(hT[:, 4 * g * P:4 * (g + 1) * P], tp[g % 2][0:R, :], ACT.Copy).then_inc(hT_taken, 1)
            act.wait_ge(sub_ready, 1)
            act.activation(g1[:, :, :], lg[:, :, :], ACT.Exp).then_inc(exp_ready, 1)

        @block.vector
        def _(dve):
            chain = Chain(dve, own)
            dve.wait_ge(loaded, 16 * 12)
            dve.wait_ge(h_taken, G)
            for c in range(NCH):
                chain.add(dve.bn_stats(stats[:, c, :], h[:, c, :]))
            chain.settle()
            for c in range(NCH):
                chain.add(dve.bn_aggr(mv[:, c, :], stats[:, c, :]))
            chain.settle()
            dve.tensor_scalar(ve[:, :], mv[:, :, 1], LN_EPS, None, ALU.add).then_inc(var_ready, 1)
            dve.wait_ge(rstd_ready, 1)
            wide = [P, NCH, R]
            chain.link(dve.tensor_tensor(h[:, :, :], h[:, :, :], bc(mv[:, :, 0:1], wide), ALU.subtract))
            chain.link(dve.tensor_tensor(h[:, :, :], h[:, :, :], bc(rstd[:, :].unsqueeze(2), wide), ALU.mult))
            chain.link(dve.tensor_tensor(h[:, :, :], h[:, :, :], bc(gain[:, :].unsqueeze(1), wide), ALU.mult))
            chain.link(dve.tensor_tensor(h[:, :, :], h[:, :, :], bc(shift[:, :].unsqueeze(1), wide), ALU.add))
            dve.tensor_scalar(h[:, :, :], h[:, :, :], 0.0, None, ALU.max).then_inc(act_ready, 1)
            dve.wait_ge(lg_ready, 1)
            lp_v = lp[:, :].rearrange("p (c e) -> p c e", e=NE)
            each = [P, NCH, NE]
            chain.link(dve.tensor_reduce(mx[:, :], lp_v, AX.X, ALU.max))
            dve.tensor_tensor(lg[:, :, :], lp_v, bc(mx[:, :].unsqueeze(2), each), ALU.subtract).then_inc(sub_ready, 1)
            dve.wait_ge(exp_ready, 1)
            chain.link(dve.tensor_reduce(sm[:, :], g1[:, :, :], AX.X, ALU.add))
            chain.link(dve.reciprocal(mx[:, :], sm[:, :]))
            chain.link(dve.tensor_tensor(g1[:, :, :], g1[:, :, :], bc(mx[:, :].unsqueeze(2), each), ALU.mult))
            for c in range(NCH):
                chain.add(dve.max(top[:, c, :], g1[:, c, :]))
            chain.settle()
            for c in range(NCH):
                chain.add(dve.max_index(idx[:, c, :], top[:, c, :], g1[:, c, :]))
            chain.settle()
            chain.link(dve.tensor_copy(idf[:, :, :], idx[:, :, 0:2]))
            chain.link(dve.tensor_tensor(den[:, :], top[:, :, 0], top[:, :, 1], ALU.add))
            chain.link(dve.reciprocal(sm[:, :], den[:, :]))
            chain.link(dve.tensor_tensor(w[:, :, :], top[:, :, 0:2], bc(sm[:, :].unsqueeze(2), [P, NCH, 2]), ALU.mult))
            iota_b = bc(iota8[:, :].unsqueeze(1), each)
            chain.link(dve.tensor_tensor(m1[:, :, :], iota_b, bc(idf[:, :, 0:1], each), ALU.is_equal))
            chain.link(dve.tensor_tensor(m2[:, :, :], iota_b, bc(idf[:, :, 1:2], each), ALU.is_equal))
            chain.link(dve.tensor_tensor(g1[:, :, :], m1[:, :, :], bc(w[:, :, 0:1], each), ALU.mult))
            chain.link(dve.tensor_tensor(g2[:, :, :], m2[:, :, :], bc(w[:, :, 1:2], each), ALU.mult))
            chain.link(dve.tensor_tensor(g1[:, :, :], g1[:, :, :], g2[:, :, :], ALU.add))
            dve.tensor_tensor(m1[:, :, :], m1[:, :, :], m2[:, :, :], ALU.add).then_inc(mask_ready, 1)
            dve.wait_ge(mask_ready, 1)
            dve.wait_ge(rank_ready, 1)
            four = "p (b c e) -> p b c e"
            chain.link(dve.tensor_copy(rank[:, :, :, :], rp[:, 0:NCH * NE].rearrange(four, b=NB, c=SC)))
            chain.link(dve.tensor_copy(tot[:, :, :, :], rp[:, NCH * NE:].rearrange(four, b=NB, c=SC)))
            chain.link(dve.tensor_copy(cnt[:, :, :], tot[:, :, 0, :]))
            for c in range(1, SC):
                chain.link(dve.tensor_tensor(rank[:, :, c, :], rank[:, :, c, :], cnt[:, :, :], ALU.add))
                chain.link(dve.tensor_tensor(cnt[:, :, :], cnt[:, :, :], tot[:, :, c, :], ALU.add))
            chain.link(dve.tensor_scalar(pc[:, :, :], cnt[:, :, :], 0.0, float(P), ALU.is_gt, ALU.mult))
            for k in range(1, SC):
                chain.link(dve.tensor_scalar(tmp[:, :, :], cnt[:, :, :], float(P * k), float(P), ALU.is_gt, ALU.mult))
                chain.link(dve.tensor_tensor(pc[:, :, :], pc[:, :, :], tmp[:, :, :], ALU.add))
            chain.link(dve.memset(off[:, :, 0:1], 0.0))
            for e in range(1, NE):
                chain.link(dve.tensor_tensor(off[:, :, e:e + 1], off[:, :, e - 1:e], pc[:, :, e - 1:e], ALU.add))
            chain.link(dve.tensor_tensor(end[:, :, :], off[:, :, :], pc[:, :, :], ALU.add))
            for c in range(SC):
                chain.add(dve.tensor_tensor(rank[:, :, c, :], rank[:, :, c, :], off[:, :, :], ALU.add))
            chain.settle()
            rank_v = rank[:, :, :, :].rearrange("p b c e -> p (b c) e")
            chain.link(dve.tensor_scalar(rank_v, rank_v, 1.0, None, ALU.add))
            chain.link(dve.tensor_tensor(rank_v, rank_v, m1[:, :, :], ALU.mult))
            route_v = route[:, :, :].rearrange("p (b e) k -> p b e k", e=NE)
            g_v = g1[:, :, :].rearrange("p (b c) e -> p b c e", c=SC)
            for c in range(SC):
                chain.add(dve.tensor_scalar(route_v[:, :, :, c], rank[:, :, c, :], -1.0, None, ALU.add))
                chain.add(dve.tensor_copy(route_v[:, :, :, SC + c], g_v[:, :, c, :]))
            for b in range(NB):
                chain.add(dve.tensor_tensor(cmp[:, b, :, :], bc(end[:, b, :].unsqueeze(1), [P, NT, NE]),
                                            bc(tstart[:, :].unsqueeze(2), [P, NT, NE]), ALU.is_le))
            chain.settle()
            chain.link(dve.tensor_reduce(tx[:, 0, :], cmp[:, :, :, :].rearrange("p b t e -> p (b t) e"), AX.X, ALU.add))
            chain.link(dve.tensor_scalar(tx[:, 1, :], tx[:, 0, :], float(NE - 1), None, ALU.min))
            chain.link(dve.tensor_tensor(tx[:, 0, :], tx[:, 1, :], bstart[:, :], ALU.add))
            dve.tensor_copy(txi[:, :, :], tx[:, :, :]).then_inc(table_ready, 1)


def kv_phase(nc, d, xnT_dram, kst_dram, v_dram):
    with ExitStack() as ctx:
        sb, ps, sem = tools(nc, ctx, "kv")
        xT = [sb(f"xT{i}", [P, S]) for i in range(2)]
        w = [sb(f"w{i}", [P, 2 * E + 1]) for i in range(2)]
        vb = [sb(f"vb{i}", [1, E]) for i in range(2)]
        ones = sb("ones", [1, P])
        k = sb("k", [P, S])
        rest = sb("rest", [P, S])
        part = [[sb(f"part{j}_{i}", [P, S], BF16) for i in range(2)] for j in range(3)]
        v = [sb(f"v{i}", [P, SC, NH, HD + 1]) for i in range(2)]
        kp = [ps(f"kp{i}", [P, S]) for i in range(2)]
        vp = [ps(f"vp{i}", [P, S]) for i in range(2)]
        ones_set, k_done, v_done, k_taken, v_taken, part0, part1, part2, rest_ready = (
            sem(n) for n in ("ones_set", "k_done", "v_done", "k_taken", "v_taken", "part0", "part1",
                             "part2", "rest_ready"))
        loaded, stored, v_stored = ([sem(f"{n}{i}") for i in range(2)] for n in ("loaded", "stored", "v_stored"))
        block = ctx.enter_context(nc.Block())
        NK = 2 * len(KPART)
        STEPS = NB * NE

        def steps(eng, body):
            for u in range(2):
                body(u, u, 0)
            with eng.Fori(1, STEPS // 2) as i:
                for u in range(2):
                    body(2 * i + u, u, i)

        def least(eng, s, value):
            if not isinstance(value, int) or value > 0:
                eng.wait_ge(s, value)

        @block.sync
        def _(sp):
            with sp.Fori(0, NB) as b:
                with sp.Fori(0, NE // 2) as i:
                    for u in range(2):
                        n = b * NE + 2 * i + u
                        column = sp.snap(b * S)
                        expert = sp.snap(2 * i + u)
                        free = sp.snap(n + 1)
                        sp.wait_ge(k_taken, free)
                        sp.wait_ge(v_taken, free)
                        sp.dma_start(xT[u][:, :], xnT_dram[:, bass.DynSlice(column, S)]).then_inc(loaded[u], 16)
                        sp.dma_start(w[u][:, :], d["wkv"][bass.DynSlice(expert, 1), :, :].rearrange("o p n -> (o p) n")).then_inc(loaded[u], 16)
                        sp.dma_start(vb[u][:, :], d["vb"][bass.DynSlice(expert, 1), :]).then_inc(loaded[u], 16)

        @block.tensor
        def _(pe):
            pe.wait_ge(ones_set, 3)

            def body(n, u, i):
                pe.wait_ge(loaded[u], 48 * i + 48)
                least(pe, k_taken, n + 1)
                pe.matmul(kp[u][:, :], w[u][:, 0:E], xT[u][:, :], start=True, stop=True).then_inc(k_done, 1)
                least(pe, v_taken, n + 1)
                for c in range(SC):
                    o = vp[u][:, c * P:(c + 1) * P]
                    pe.matmul(o, xT[u][:, c * P:(c + 1) * P], w[u][:, E:2 * E], start=True, stop=False)
                    last = pe.matmul(o, ones[:, :], vb[u][:, :], start=False, stop=True)
                last.then_inc(v_done, 1)

            steps(pe, body)

        @block.scalar
        def _(act):
            act.wait_ge(ones_set, 3)
            act.sem_inc(k_taken, 2)
            act.sem_inc(v_taken, 2)

            def body(n, u, i):
                act.wait_ge(k_done, n + 1)
                least(act, rest_ready, n)
                act.activation(k[:, :], kp[u][:, :], ACT.Identity, bias=w[u][:, 2 * E:2 * E + 1]).then_inc(k_taken, 1)
                act.wait_ge(k_taken, n + 3)
                least(act, stored[u], 16 * NK * i)
                act.activation(part[0][u][:, :], k[:, :], ACT.Copy).then_inc(part0, 1)
                act.wait_ge(v_done, n + 1)
                least(act, v_stored[u], 16 * i)
                act.activation(v[u][:, :, :, 0:HD], vp[u][:, :].rearrange("p (c h d) -> p c h d", c=SC, h=NH),
                               ACT.Copy).then_inc(v_taken, 1)

            steps(act, body)

        @block.vector
        def _(dve):
            def body(n, u, i):
                dve.wait_ge(part0, n + 1)
                least(dve, stored[u], 16 * NK * i)
                dve.tensor_tensor(rest[:, :], k[:, :], part[0][u][:, :], ALU.subtract).then_inc(rest_ready, 1)
                dve.wait_ge(rest_ready, n + 1)
                dve.tensor_copy(part[1][u][:, :], rest[:, :]).then_inc(part1, 1)
                dve.wait_ge(part1, n + 1)
                dve.tensor_tensor(part[2][u][:, :], rest[:, :], part[1][u][:, :], ALU.subtract).then_inc(part2, 1)
                dve.wait_ge(part2, n + 1)

            steps(dve, body)

        def store_body(q):
            def body(n, u, i):
                q.wait_ge(part2, n + 1)
                for s in range(2):
                    for j, kpart in enumerate(KPART):
                        row = KQ * s + HD * j
                        q.dma_start(kst_dram[bass.DynSlice(n, 1), row:row + HD, :, :].rearrange("o d p t -> (o d p) t"),
                                    part[kpart][u][64 * s:64 * s + 64, :]).then_inc(stored[u], 16)
                q.wait_ge(v_taken, n + 3)
                q.dma_start(v_dram[bass.DynSlice(n, 1), :, :, :, :].rearrange("o p c h d -> (o p) (c h d)"),
                            v[u][:, :, :, :].rearrange("p c h d -> p (c h d)")).then_inc(v_stored[u], 16)
            return body

        @block.gpsimd
        def _(pool):
            for i in range(2):
                pool.memset(v[i][:, :, :, :], 1.0).then_inc(ones_set, 1)
            pool.memset(ones[:, :], 1.0).then_inc(ones_set, 1)
            steps(pool, store_body(pool))
            for u in range(2):
                pool.wait_ge(stored[u], 16 * NK * STEPS // 2)
                pool.wait_ge(v_stored[u], 16 * STEPS // 2)


def experts_phase(nc, d, xn_dram, kst_dram, v_dram, route_dram, texp_dram, moe_dram):
    with ExitStack() as ctx:
        sb, ps, sem = tools(nc, ctx, "ex")
        M3 = 3 * NH
        SCALE = float(HD) ** -0.5
        ks = [sb(f"ks{i}", [P, NH // 2, S], BF16) for i in range(3)]
        qs = [sb(f"qs{i}", [P, NH, P], BF16) for i in range(3)]
        v = [sb(f"v{i}", [P, SC, NH, HD + 1]) for i in range(2)]
        wo = [sb(f"wo{i}", [P, E]) for i in range(3)]
        ob = [sb(f"ob{i}", [1, E]) for i in range(3)]
        wq = [sb(f"wq{i}", [P, E + 1]) for i in range(2)]
        xn = [sb(f"xn{i}", [P, SC, E]) for i in range(2)]
        rt = [sb(f"rt{i}", [P, 2 * SC]) for i in range(2)]
        rel = sb("rel", [P, SC])
        hot = [sb(f"hot{i}", [P, SC, P]) for i in range(2)]
        gated = [sb(f"gated{i}", [P, SC, P]) for i in range(3)]
        xg = sb("xg", [P, P])
        q = sb("q", [P, P])
        qrest = sb("qrest", [P, P])
        qpart = [sb(f"qpart{j}", [P, P], BF16) for j in range(3)]
        nm = sb("nm", [P, NH])
        nmrest = sb("nmrest", [P, NH])
        mpart = sb("mpart", [P, P // NH, NH], BF16)
        mT = sb("mT", [M3, P], BF16)
        ex = sb("ex", [P, 8, S])
        oT = sb("oT", [P, 4 * P])
        rec = sb("rec", [P, 4, 4])
        on = sb("on", [P, NH, HD])
        onT = sb("onT", [P, P])
        os_ = sb("os", [P, E])
        spread = sb("spread", [P, SC * P])
        acc = [sb(f"acc{i}", [P, SC, E]) for i in range(2)]
        ident = sb("ident", [P, P])
        identb = sb("identb", [P, P], BF16)
        iota = sb("iota", [P, P])
        first_slot = sb("first_slot", [P, TILES])
        keep = sb("keep", [P, TILES])
        ones = sb("ones", [1, P])
        texp = sb("texp", [1, 2 * TILES], I32)
        tb = sb("tb", [1, TILES], I32)
        SP_ = [ps(f"s{i}", [P, S]) for i in range(2)]
        ST_ = [ps(f"st{i}", [P, S]) for i in range(3)]
        O_ = ps("o", [P, 4 * P])
        A_ = ps("a", [P, 4 * P])
        B_ = ps("b", [P, 4 * P])
        names = ("consts cleared rel_ready rel_seen hot_ready gated_ready xg_done "
                 "xg_taken q_done q_taken q0 qr1 q1 q_parts q_stacked s_done max_taken nm0 nmr nm1 nm_parts mt_done mt_taken "
                 "m_stacked st_done exp_done pv_done o_taken tr_done rec_ready on_ready on_done onT_taken out_done "
                 "out_taken gt_done gt_taken sc_done acc_ready")
        sems = {n: sem(n) for n in names.split()}
        kv_loaded, wo_loaded = ([sem(f"{n}{i}") for i in range(3)] for n in ("kv_loaded", "wo_loaded"))
        v_loaded, in_loaded, acc_stored = ([sem(f"{n}{i}") for i in range(2)] for n in ("v_loaded", "in_loaded", "acc_stored"))
        block = ctx.enter_context(nc.Block())

        def least(eng, name, value):
            if not isinstance(value, int) or value > 0:
                eng.wait_ge(sems[name], value)

        now = {"i": 0}

        def uses(k, ring):
            return now["i"] * (6 // ring) + k // ring + 1

        def bodies(eng, body):
            now["i"] = 0
            for n in range(3):
                body(n, n)
            with eng.Fori(0, (TILES - 6) // 6) as i:
                now["i"] = i
                for k in range(3, 9):
                    body(6 * i + k, k, loop=True)
            now["i"] = 0
            for n in range(TILES - 3, TILES):
                body(n, n)

        def inside(n, loop):
            return loop or n < TILES

        @block.sync
        def _(sp):
            for dst, src in [(ident[:, :], d["identity"]), (iota[:, :], d["iota"]), (first_slot[:, :], d["first_slot"]),
                             (keep[:, :], d["keep"]), (texp[:, :], texp_dram[:, :]), (tb[:, :], d["tile_batch"])]:
                sp.dma_start(dst, src).then_inc(sems["consts"], 16)

            def value(n):
                return n if isinstance(n, int) else sp.snap(n)

            def stack_q(n, k):
                sp.wait_ge(sems["q_parts"], n + 1)
                for s in range(2):
                    for j, part in enumerate(QPART):
                        row = KQ * s + HD * j
                        sp.dma_start(qs[k % 3][row:row + HD, s::2, :],
                                     qpart[part][64 * s:64 * s + 64, :]).then_inc(sems["q_stacked"], 16)

            def stack_m(n, k):
                sp.wait_ge(sems["mt_taken"], n + 1)
                sp.dma_start(qs[k % 3][2 * KQ:2 * KQ + 3, :, :], mT[:, :]).then_inc(sems["m_stacked"], 16)

            def store(n, k):
                tile, added = value(n), value(n + 1)
                sp.wait_ge(sems["acc_ready"], added)
                sp.dma_start(moe_dram[bass.DynSlice(tile, 1), :, :, :].rearrange("o p c e -> (o p) (c e)"),
                             acc[k % 2][:, :, :].rearrange("p c e -> p (c e)")).then_inc(acc_stored[k % 2], 16)

            def body(n, k, loop=False):
                if inside(n + 2 if not loop else 0, loop):
                    stack_q(n + 2, k + 2)
                if inside(n + 1 if not loop else 0, loop):
                    stack_m(n + 1, k + 1)
                if loop or n > 0:
                    store(n - 1, k - 1)

            sp.wait_ge(sems["cleared"], 2)
            stack_q(0, 0)
            stack_q(1, 1)
            stack_m(0, 0)
            bodies(sp, body)
            store(TILES - 1, TILES - 1)
            for i in range(2):
                sp.wait_ge(acc_stored[i], 16 * TILES // 2)

        @block.gpsimd
        def _(pool):
            pool.memset(ones[:, :], 1.0).then_inc(sems["cleared"], 1)
            pool.wait_ge(sems["consts"], 16 * 6)

            def be_of(n):
                return pool.value_load(texp[0:1, bass.DynSlice(n, 1)], min_val=0, max_val=NB * NE - 1)

            def expert_of(n):
                return pool.value_load(texp[0:1, bass.DynSlice(TILES + n, 1)], min_val=0, max_val=NE - 1)

            def load_kv(n, k):
                be = be_of(n)
                least(pool, "st_done", 16 * (n - 2))
                pool.dma_start(ks[k % 3][0:2 * KQ, :, :].rearrange("p h t -> p (h t)"),
                               kst_dram[bass.DynSlice(be, 1), :, :, :].rearrange("o r p t -> (o r) (p t)"))\
                    .then_inc(kv_loaded[k % 3], 16)

            def load_v(n, k):
                be = be_of(n)
                e = expert_of(n)
                least(pool, "pv_done", 4 * (n - 1))
                pool.dma_start(v[k % 2][:, :, :, :].rearrange("p c h d -> p (c h d)"),
                               v_dram[bass.DynSlice(be, 1), :, :, :, :].rearrange("o p c h d -> (o p) (c h d)"))\
                    .then_inc(v_loaded[k % 2], 16)
                least(pool, "out_done", n - 2)
                pool.dma_start(wo[k % 3][:, :], d["wo"][bass.DynSlice(e, 1), :, :].rearrange("o p n -> (o p) n"))\
                    .then_inc(wo_loaded[k % 3], 16)
                pool.dma_start(ob[k % 3][:, :], d["ob"][bass.DynSlice(e, 1), :]).then_inc(wo_loaded[k % 3], 16)

            def load_in(n, k):
                be = be_of(n)
                e = expert_of(n)
                b = pool.value_load(tb[0:1, bass.DynSlice(n, 1)], min_val=0, max_val=NB - 1)
                least(pool, "q_taken", n - 1)
                least(pool, "gated_ready", n - 1)
                i = k % 2
                pool.dma_start(xn[i][:, :, :], xn_dram[bass.DynSlice(b, 1), :, :].rearrange("o (c p) e -> p (o c) e", p=P))\
                    .then_inc(in_loaded[k % 2], 16)
                pool.dma_start(wq[i][:, :], d["wq"][bass.DynSlice(e, 1), :, :].rearrange("o p n -> (o p) n"))\
                    .then_inc(in_loaded[k % 2], 16)
                pool.dma_start(rt[i][:, :], route_dram[:, bass.DynSlice(be, 1), :].rearrange("p o k -> p (o k)"))\
                    .then_inc(in_loaded[k % 2], 16)

            def one_hot(n, k):
                pool.wait_ge(in_loaded[k % 2], 48 * uses(k, 2))
                least(pool, "gated_ready", n)
                least(pool, "xg_done", n - 1)
                least(pool, "gt_done", n - 2)
                pool.tensor_tensor(rel[:, :], rt[k % 2][:, 0:SC], bc(first_slot[:, bass.DynSlice(n, 1)], [P, SC]),
                                   ALU.subtract).then_inc(sems["rel_ready"], 1)
                pool.wait_ge(sems["rel_ready"], n + 1)
                pool.sem_inc(sems["rel_seen"], 1)
                for c in range(SC):
                    last = pool.tensor_scalar(hot[k % 2][:, c, :], iota[:, :], rel[:, c:c + 1], None, ALU.is_equal)
                last.then_inc(sems["hot_ready"], 1)
                for c in range(SC):
                    last = pool.tensor_scalar(gated[k % 3][:, c, :], iota[:, :], rel[:, c:c + 1],
                                              rt[k % 2][:, SC + c:SC + c + 1], ALU.is_equal, ALU.mult)
                last.then_inc(sems["gated_ready"], 1)

            def body(n, k, loop=False):
                if inside(n + 2 if not loop else 0, loop):
                    one_hot(n + 2, k + 2)
                if inside(n + 1 if not loop else 0, loop):
                    load_v(n + 1, k + 1)
                if inside(n + 2 if not loop else 0, loop):
                    load_kv(n + 2, k + 2)
                if inside(n + 3 if not loop else 0, loop):
                    load_in(n + 3, k + 3)

            load_in(0, 0)
            load_in(1, 1)
            load_kv(0, 0)
            load_kv(1, 1)
            load_v(0, 0)
            one_hot(0, 0)
            one_hot(1, 1)
            load_in(2, 2)
            bodies(pool, body)

        @block.tensor
        def _(pe):
            def gather(n, k):
                pe.wait_ge(sems["hot_ready"], n + 1)
                pe.wait_ge(in_loaded[k % 2], 48 * uses(k, 2))
                least(pe, "mt_taken", n - 1)
                least(pe, "q_taken", n)
                for c in range(SC):
                    last = pe.matmul(A_[:, 0:P], xn[k % 2][:, c, :], hot[k % 2][:, c, :], start=(c == 0), stop=(c == SC - 1))
                last.then_inc(sems["xg_done"], 1)

            def query(n, k):
                pe.wait_ge(sems["xg_taken"], n + 1)
                pe.matmul(A_[:, 0:P], wq[k % 2][:, 0:E], xg[:, :], start=True, stop=True).then_inc(sems["q_done"], 1)

            def max_T(n, k):
                pe.wait_ge(sems["nm_parts"], n + 1)
                least(pe, "q_taken", n + 2 if not isinstance(n, int) or n + 2 <= TILES else TILES)
                pe.transpose(A_[:, 0:P // 2].bitcast(BF16), mpart[:, :, :].rearrange("p i h -> p (i h)"), identb[:, :])\
                    .then_inc(sems["mt_done"], 1)

            def score(n, k, h):
                if h == 0:
                    pe.wait_ge(sems["q_stacked"], 192 * (n + 1))
                    pe.wait_ge(kv_loaded[k % 3], 16 * uses(k, 3))
                least(pe, "max_taken", 16 * n + h - 1)
                pe.matmul(SP_[h % 2][:, :], qs[k % 3][0:2 * KQ, h, :], ks[k % 3][0:2 * KQ, h // 2, :],
                          start=True, stop=True).then_inc(sems["s_done"], 1)

            def score_T(n, k, u):
                if u == 0:
                    pe.wait_ge(sems["m_stacked"], 16 * (n + 1))
                least(pe, "exp_done", 16 * n + u - 2)
                bank = ST_[(k + u) % 3]
                for i in range(2):
                    c = 2 * (u % 2) + i
                    last = pe.matmul(bank[:, i * 2 * P:(i + 1) * 2 * P],
                                     ks[k % 3][0:2 * KQ + 3, u // 2, c * P:(c + 1) * P],
                                     qs[k % 3][0:2 * KQ + 3, u // 2 * 2:u // 2 * 2 + 2, :], start=True, stop=True)
                last.then_inc(sems["st_done"], 1)

            def values(n, k, g, c):
                if c == 0:
                    pe.wait_ge(sems["exp_done"], 16 * n + 4 * g + 4)
                    if g == 0:
                        pe.wait_ge(v_loaded[k % 2], 16 * uses(k, 2))
                        least(pe, "o_taken", n)
                for j in range(4):
                    unit = (4 * g + 2 * (j // 2) + c // 2) % 8
                    at = (c % 2) * 2 * P + (j % 2) * P
                    last = pe.matmul(O_[32 * j:32 * j + HD + 1, g * P:(g + 1) * P], v[k % 2][:, c, 4 * g + j, :],
                                     ex[:, unit, at:at + P], start=(c == 0), stop=(c == SC - 1), skip_group_check=True)
                if c == SC - 1:
                    last.then_inc(sems["pv_done"], 1)

            def turn_out(n, k):
                pe.wait_ge(sems["o_taken"], n + 1)
                least(pe, "gt_taken", n + 1)
                for g in range(4):
                    last = pe.transpose(B_[:, g * P:(g + 1) * P], oT[:, g * P:(g + 1) * P], ident[:, :])
                last.then_inc(sems["tr_done"], 1)

            def turn_norm(n, k):
                pe.wait_ge(sems["on_ready"], n + 1)
                pe.transpose(B_[:, 0:P], on[:, :, :].rearrange("p h d -> p (h d)"), ident[:, :]).then_inc(sems["on_done"], 1)

            def project(n, k):
                pe.wait_ge(sems["onT_taken"], n + 1)
                pe.wait_ge(wo_loaded[k % 3], 32 * uses(k, 3))
                pe.matmul(B_[:, 0:E], onT[:, :], wo[k % 3][:, :], start=True, stop=False)
                pe.matmul(B_[:, 0:E], ones[:, :], ob[k % 3][:, :], start=False, stop=True).then_inc(sems["out_done"], 1)

            def scatter(n, k):
                pe.wait_ge(sems["out_taken"], n + 1)
                pe.wait_ge(sems["gt_taken"], n + 1)
                for c in range(SC):
                    last = pe.matmul(B_[:, c * P:(c + 1) * P], spread[:, c * P:(c + 1) * P], os_[:, :], start=True, stop=True)
                last.then_inc(sems["sc_done"], 1)

            def turn_gated(n, k):
                pe.wait_ge(sems["gated_ready"], n + 1)
                least(pe, "acc_ready", n)
                for c in range(SC):
                    last = pe.transpose(B_[:, c * P:(c + 1) * P], gated[k % 3][:, c, :], ident[:, :])
                last.then_inc(sems["gt_done"], 1)

            def body(n, k, loop=False):
                more, later = loop or n + 1 < TILES, loop or n + 2 < TILES
                before = loop or n > 0
                for g in range(4):
                    for i in range(4):
                        score_T(n, k, 4 * g + i)
                        if more:
                            score(n + 1, k + 1, 4 * g + i)
                        if g:
                            values(n, k, g - 1, i)
                    if g == 0 and before:
                        turn_out(n - 1, k - 1)
                    if g == 1 and before:
                        turn_norm(n - 1, k - 1)
                    if g == 1 and later:
                        gather(n + 2, k + 2)
                    if g == 2 and before:
                        project(n - 1, k - 1)
                    if g == 2 and later:
                        query(n + 2, k + 2)
                    if g == 3 and before:
                        scatter(n - 1, k - 1)
                if more:
                    max_T(n + 1, k + 1)
                for i in range(4):
                    values(n, k, 3, i)
                turn_gated(n, k)

            pe.wait_ge(sems["consts"], 16 * 6)
            pe.wait_ge(sems["cleared"], 2)
            gather(0, 0)
            query(0, 0)
            gather(1, 1)
            query(1, 1)
            for h in range(NH):
                score(0, 0, h)
            max_T(0, 0)
            bodies(pe, body)
            n, k = TILES - 1, TILES - 1
            turn_out(n, k)
            turn_norm(n, k)
            project(n, k)
            scatter(n, k)

        @block.scalar
        def _(act):
            def take_xg(n, k):
                act.wait_ge(sems["xg_done"], n + 1)
                least(act, "q_done", n)
                act.activation(xg[:, :], A_[:, 0:P], ACT.Copy).then_inc(sems["xg_taken"], 1)

            def take_max(n, k):
                act.wait_ge(sems["mt_done"], n + 1)
                least(act, "m_stacked", 16 * n)
                act.activation(mT[:, :], A_[0:M3, 0:P // 2].bitcast(BF16), ACT.Copy).then_inc(sems["mt_taken"], 1)

            def exps(n, k, u):
                act.wait_ge(sems["st_done"], 16 * n + u + 1)
                if u % 4 == 0:
                    least(act, "pv_done", 4 * n + u // 4 - 1)
                act.activation(ex[:, u % 8, :], ST_[(k + u) % 3][:, :], ACT.Exp).then_inc(sems["exp_done"], 1)

            def take_out(n, k):
                act.wait_ge(sems["pv_done"], 4 * n + 4)
                least(act, "tr_done", n)
                act.activation(oT[:, :], O_[:, :], ACT.Copy).then_inc(sems["o_taken"], 1)

            def take_norm(n, k):
                act.wait_ge(sems["on_done"], n + 1)
                least(act, "out_done", n)
                act.activation(onT[:, :], B_[:, 0:P], ACT.Copy).then_inc(sems["onT_taken"], 1)

            def take_proj(n, k):
                act.wait_ge(sems["out_done"], n + 1)
                least(act, "sc_done", n)
                act.activation(os_[:, :], B_[:, 0:E], ACT.Copy).then_inc(sems["out_taken"], 1)

            def take_gated(n, k):
                act.wait_ge(sems["gt_done"], n + 1)
                least(act, "sc_done", n)
                act.activation(spread[:, :], B_[:, :], ACT.Copy).then_inc(sems["gt_taken"], 1)

            def body(n, k, loop=False):
                more, later = loop or n + 1 < TILES, loop or n + 2 < TILES
                before = loop or n > 0
                for u in range(NH):
                    exps(n, k, u)
                    if u == 9 and before:
                        take_norm(n - 1, k - 1)
                    if u == 8 and later:
                        take_xg(n + 2, k + 2)
                    if u == 13 and before:
                        take_proj(n - 1, k - 1)
                if more:
                    take_max(n + 1, k + 1)
                take_out(n, k)
                take_gated(n, k)

            take_xg(0, 0)
            take_xg(1, 1)
            take_max(0, 0)
            bodies(act, body)
            take_norm(TILES - 1, TILES - 1)
            take_proj(TILES - 1, TILES - 1)

        @block.vector
        def _(dve):
            for i in range(3):
                dve.memset(qs[i][:, :, :], 0.0)
                dve.memset(ks[i][2 * KQ:P, :, :], 1.0)
            dve.memset(mpart[:, :, :], 0.0)
            dve.memset(acc[1][:, :, :], 0.0)
            dve.wait_ge(sems["consts"], 16 * 6)
            dve.tensor_copy(identb[:, :], ident[:, :])
            dve.memset(O_[:, :], 0.0).then_inc(sems["cleared"], 1)

            def parts_q(n, k):
                dve.wait_ge(sems["q_done"], n + 1)
                least(dve, "q_stacked", 192 * n)
                dve.tensor_scalar(q[:, :], A_[:, 0:P], wq[k % 2][:, E:E + 1], SCALE, ALU.add, ALU.mult)\
                    .then_inc(sems["q_taken"], 1)
                dve.wait_ge(sems["q_taken"], n + 1)
                dve.tensor_copy(qpart[0][:, :], q[:, :]).then_inc(sems["q0"], 1)
                dve.wait_ge(sems["q0"], n + 1)
                dve.tensor_tensor(qrest[:, :], q[:, :], qpart[0][:, :], ALU.subtract).then_inc(sems["qr1"], 1)
                dve.wait_ge(sems["qr1"], n + 1)
                dve.tensor_copy(qpart[1][:, :], qrest[:, :]).then_inc(sems["q1"], 1)
                least(dve, "st_done", 16 * (n - 2))
                dve.wait_ge(sems["q1"], n + 1)
                dve.tensor_tensor(qpart[2][:, :], qrest[:, :], qpart[1][:, :], ALU.subtract).then_inc(sems["q_parts"], 1)

            def row_max(n, k, h):
                dve.wait_ge(sems["s_done"], 16 * n + h + 1)
                dve.tensor_reduce(nm[:, h:h + 1], SP_[h % 2][:, :], AX.X, ALU.max, negate=True).then_inc(sems["max_taken"], 1)

            def parts_max(n, k):
                dve.wait_ge(sems["max_taken"], 16 * (n + 1))
                least(dve, "mt_done", n)
                dve.tensor_copy(mpart[:, 0, :], nm[:, :]).then_inc(sems["nm0"], 1)
                dve.wait_ge(sems["nm0"], n + 1)
                dve.tensor_tensor(nmrest[:, :], nm[:, :], mpart[:, 0, :], ALU.subtract).then_inc(sems["nmr"], 1)
                dve.wait_ge(sems["nmr"], n + 1)
                dve.tensor_copy(mpart[:, 1, :], nmrest[:, :]).then_inc(sems["nm1"], 1)
                dve.wait_ge(sems["nm1"], n + 1)
                dve.tensor_tensor(mpart[:, 2, :], nmrest[:, :], mpart[:, 1, :], ALU.subtract).then_inc(sems["nm_parts"], 1)

            def normalise(n, k):
                dve.wait_ge(sems["tr_done"], n + 1)
                least(dve, "on_done", n)
                tr = B_[:, :].rearrange("p (g j r) -> p g j r", g=4, j=4)
                dve.reciprocal(rec[:, :, :], tr[:, :, :, HD]).then_inc(sems["rec_ready"], 1)
                dve.wait_ge(sems["rec_ready"], n + 1)
                dve.tensor_tensor(on[:, :, :].rearrange("p (g j) d -> p g j d", j=4), tr[:, :, :, 0:HD],
                                  bc(rec[:, :, :].unsqueeze(3), [P, 4, 4, HD]), ALU.mult).then_inc(sems["on_ready"], 1)

            def add_out(n, k):
                dve.wait_ge(sems["sc_done"], n + 1)
                least(dve, "acc_ready", n)
                stored = 16 * (uses(k, 2) - 1)
                if not isinstance(stored, int) or stored > 0:
                    dve.wait_ge(acc_stored[k % 2], stored)
                dve.scalar_tensor_tensor(acc[k % 2][:, :, :].rearrange("p c e -> p (c e)"),
                                         acc[(k + 1) % 2][:, :, :].rearrange("p c e -> p (c e)"),
                                         keep[:, bass.DynSlice(n, 1)], B_[:, :], ALU.mult, ALU.add)\
                    .then_inc(sems["acc_ready"], 1)

            def body(n, k, loop=False):
                more, later = loop or n + 1 < TILES, loop or n + 2 < TILES
                before = loop or n > 0
                for h in range(NH):
                    if more:
                        row_max(n + 1, k + 1, h)
                    if h == 5 and before:
                        normalise(n - 1, k - 1)
                    if h == 13 and later:
                        parts_q(n + 2, k + 2)
                if more:
                    parts_max(n + 1, k + 1)
                if before:
                    add_out(n - 1, k - 1)

            parts_q(0, 0)
            parts_q(1, 1)
            for h in range(NH):
                row_max(0, 0, h)
            parts_max(0, 0)
            bodies(dve, body)
            normalise(TILES - 1, TILES - 1)
            add_out(TILES - 1, TILES - 1)


def mlstm_phase(nc, d, xnT_dram, ml_dram):
    with ExitStack() as ctx:
        sb, ps, sem = tools(nc, ctx, "ml")
        CH = INNER // P
        KS = 4
        xT = sb("xT", [P, S])
        wup = sb("wup", [P, 2 * INNER])
        conv = sb("conv", [P, CH, KS + 1])
        bdq, bdk, bdv = (sb(n, [P, CH, P]) for n in ("bdq", "bdk", "bdv"))
        wg = sb("wg", [P, 2, 3 * CH, MH])
        bg = sb("bg", [MH, 2])
        chan = sb("chan", [P, CH, 2])
        wdn = sb("wdn", [P, CH, E])
        sel = sb("sel", [MH, MH, P])
        tri = sb("tri", [P, P])
        ident = sb("ident", [P, P])
        xm = sb("xm", [P, CH, S + KS - 1])
        pre = sb("pre", [P, 2 * CH, S])
        sg = sb("sg", [P, 2 * CH, S])
        qT, kT, vT = (sb(n, [P, CH, S]) for n in ("qT", "kT", "vT"))
        va = sb("va", [P, SC, MH, MD + 1])
        ig, fg, nf, ef, lnf, lf, lc, a, cm, nM, lm, em = (
            sb(n, [MH, S]) for n in ("ig", "fg", "nf", "ef", "lnf", "lf", "lc", "a", "cm", "nM", "lm", "em"))
        ones = sb("ones", [MH, S])
        cols = sb("cols", [P, 2, SC, MH])
        D = sb("D", [P, SC, S])
        C = sb("C", [P, SC, S])
        nd = sb("nd", [P, SC])
        hh = sb("hh", [P, SC, MH, MD])
        stats = sb("stats", [P, SC * MH, 6])
        mv = sb("mv", [P, SC * MH, 2])
        ve = sb("ve", [P, SC * MH])
        half = sb("half", [P, SC * MH])
        rstd = sb("rstd", [P, SC * MH])
        sx = sb("sx", [P, CH, S])
        hs = sb("hs", [P, CH, S])
        o = sb("o", [P, SC, E])
        bank = [ps(f"p{i}", [P, S]) for i in range(8)]
        names = ("consts half_set x_in up_done up_taken conv_done exp4 silu_done qk_done v_done qk_taken gate_done "
                 "gate_taken nf_ready ef_ready em_in em_ready cols_done cols_taken mb_done s_done d_ready d_exp "
                 "c_ready h_done h_taken var_ready rstd_ready hn_ready hT_done hs_ready o_done o_taken o_stored own stats_seen em_seen chain")
        z = {n: sem(n) for n in names.split()}
        block = ctx.enter_context(nc.Block())
        consts = [(wup[:, :], "w_up"), (conv[:, :, :], "conv"), (bdq[:, :, :], "bdq"), (bdk[:, :, :], "bdk"),
                  (bdv[:, :, :], "bdv"), (wg[:, :, :, :], "w_gates"), (bg[:, :], "b_gates"), (chan[:, :, :], "chan"),
                  (wdn[:, :, :], "w_down0"), (sel[:, :, :], "sel"), (tri[:, :], "tri"), (ident[:, :], "identity")]

        @block.sync
        def _(sp):
            for dst, name in consts:
                sp.dma_start(dst, d[name]).then_inc(z["consts"], 16)
            with sp.Fori(0, NB) as b:
                at = sp.snap(b * S)
                sp.wait_ge(z["up_done"], 4 * b + 4)
                sp.dma_start(xT[:, :], xnT_dram[:, bass.DynSlice(at, S)]).then_inc(z["x_in"], 16)
                to = sp.snap(b)
                sp.wait_ge(z["o_taken"], b + 1)
                sp.dma_start(ml_dram[bass.DynSlice(to, 1), :, :].rearrange("o (c p) e -> p (o c) e", p=P),
                             o[:, :, :]).then_inc(z["o_stored"], 16)
            sp.wait_ge(z["o_stored"], 16 * NB + 16)

        @block.gpsimd
        def _(pool):
            pool.memset(half[:, :], -0.5).then_inc(z["half_set"], 1)
            pool.memset(ones[:, :], 1.0).then_inc(z["half_set"], 1)
            pool.memset(va[:, :, :, :], 1.0).then_inc(z["half_set"], 1)
            pool.memset(xm[:, :, :], 0.0).then_inc(z["half_set"], 1)
            pool.wait_ge(z["half_set"], 4)
            with pool.Fori(0, NB) as b:
                pool.wait_ge(z["var_ready"], b + 1)
                pool.tensor_tensor(rstd[:, :], ve[:, :], half[:, :], ALU.pow).then_inc(z["rstd_ready"], 1)

        @block.tensor
        def _(pe):
            pe.wait_ge(z["consts"], 16 * len(consts))
            pe.wait_ge(z["half_set"], 4)
            pe.sem_inc(z["up_done"], 4)
            with pe.Fori(0, NB) as b:
                pe.wait_ge(z["x_in"], 16 * b + 16)
                for i in range(2 * CH):
                    pe.matmul(bank[i][:, :], wup[:, i * P:(i + 1) * P], xT[:, :], start=True, stop=True)\
                        .then_inc(z["up_done"], 1)
                pe.wait_ge(z["up_taken"], 4 * b + 4)
                for c in range(CH):
                    pe.matmul(bank[4 + c][:, :], bdv[:, c, :], xm[:, c, KS - 1:], start=True, stop=True)
                for t in range(SC):
                    for c in range(CH):
                        at = (t % 2) * INNER + c * P
                        last = pe.matmul(bank[6 + t // 2][:, at:at + P], xm[:, c, KS - 1 + t * P:KS - 1 + (t + 1) * P],
                                         bdv[:, c, :], start=True, stop=True)
                last.then_inc(z["v_done"], 1)
                pe.wait_ge(z["silu_done"], b + 1)
                for c in range(CH):
                    pe.matmul(bank[c][:, :], bdq[:, c, :], sg[:, c, :], start=True, stop=True)
                    last = pe.matmul(bank[2 + c][:, :], bdk[:, c, :], sg[:, c, :], start=True, stop=True)
                last.then_inc(z["qk_done"], 1)
                pe.wait_ge(z["qk_taken"], b + 1)
                src = [t[:, c, :] for t in (qT, kT, vT) for c in range(CH)]
                for i in range(2):
                    for c in range(3 * CH):
                        last = pe.matmul(bank[4 + i][0:MH, :], wg[:, i, c, :], src[c], start=(c == 0), stop=(c == 3 * CH - 1))
                last.then_inc(z["gate_done"], 1)
                pe.wait_ge(z["em_ready"], b + 1)
                pe.sem_inc(z["em_seen"], 1)
                for i, t in enumerate((a, em)):
                    for c in range(SC):
                        last = pe.transpose(bank[7][:, (i * SC + c) * MH:(i * SC + c + 1) * MH], t[:, c * P:(c + 1) * P],
                                            ident[0:MH, 0:MH])
                last.then_inc(z["cols_done"], 1)
                for h in range(MH):
                    m, r = h // 2, MD * (h % 2)
                    if h:
                        pe.wait_ge(z["d_ready"], 4 * (MH * b + h))
                    pe.matmul(bank[0][:, :], sel[:, h, :], nM[:, :], start=True, stop=True).then_inc(z["mb_done"], 1)
                    for t in range(SC):
                        if h:
                            pe.wait_ge(z["c_ready"], 4 * (MH * b + h - 1) + t + 1)
                        elif t == 3:
                            pe.wait_ge(z["gate_taken"], 2 * b + 2)
                        pe.matmul(bank[1 + t][:, 0:S - t * P], kT[r:r + MD, m, t * P:(t + 1) * P], qT[r:r + MD, m, t * P:],
                                  start=True, stop=True).then_inc(z["s_done"], 1)
                    if h >= 2:
                        pe.wait_ge(z["h_taken"], MH * b + h - 1)
                    for s in range(SC):
                        for t in range(s + 1):
                            if s == SC - 1 or t == s:
                                pe.wait_ge(z["c_ready"], 4 * (MH * b + h) + t + 1)
                            last = pe.matmul(bank[5 + h % 2][:, s * (MD + 1):(s + 1) * (MD + 1)],
                                             C[:, t, (s - t) * P:(s - t + 1) * P], va[:, t, h, :],
                                             start=(t == 0), stop=(t == s))
                    last.then_inc(z["h_done"], 1)
                pe.wait_ge(z["hn_ready"], b + 1)
                for s in range(SC):
                    for c in range(CH):
                        last = pe.transpose(bank[c][:, s * P:(s + 1) * P],
                                            hh[:, s, 2 * c:2 * c + 2, :].rearrange("p h d -> p (h d)"), ident[:, :])
                last.then_inc(z["hT_done"], 1)
                pe.wait_ge(z["hs_ready"], b + 1)
                for s in range(SC):
                    for c in range(CH):
                        last = pe.matmul(bank[2][:, s * P:(s + 1) * P], hs[:, c, s * P:(s + 1) * P], wdn[:, c, :],
                                         start=(c == 0), stop=(c == CH - 1))
                last.then_inc(z["o_done"], 1)
                pe.wait_ge(z["o_taken"], b + 1)

        @block.scalar
        def _(act):
            act.wait_ge(z["half_set"], 4)
            act.wait_ge(z["consts"], 16 * len(consts))
            act.sem_inc(z["o_stored"], 16)
            with act.Fori(0, NB) as b:
                for i in range(2 * CH):
                    act.wait_ge(z["up_done"], 4 * b + 5 + i)
                    dst = xm[:, i, KS - 1:] if i < CH else pre[:, i, :]
                    act.activation(dst, bank[i][:, :], ACT.Copy).then_inc(z["up_taken"], 1)
                act.wait_ge(z["conv_done"], b + 1)
                act.activation(sg[:, :, :], pre[:, :, :], ACT.Exp, scale=-1.0).then_inc(z["exp4"], 1)
                act.wait_ge(z["v_done"], b + 1)
                for c in range(CH):
                    act.activation(vT[:, c, :], bank[4 + c][:, :], ACT.Copy)
                for i in range(2):
                    act.activation(va[:, 2 * i:2 * i + 2, :, 0:MD],
                                   bank[6 + i][:, :].rearrange("p (t h e) -> p t h e", t=2, h=MH), ACT.Copy)
                act.wait_ge(z["qk_done"], b + 1)
                for c in range(CH):
                    act.activation(qT[:, c, :], bank[c][:, :], ACT.Copy)
                    last = act.activation(kT[:, c, :], bank[2 + c][:, :], ACT.Copy)
                last.then_inc(z["qk_taken"], 1)
                act.wait_ge(z["gate_done"], b + 1)
                act.activation(ig[:, :], bank[4][0:MH, :], ACT.Identity, bias=bg[:, 0:1]).then_inc(z["gate_taken"], 1)
                act.activation(fg[:, :], bank[5][0:MH, :], ACT.Identity, bias=bg[:, 1:2]).then_inc(z["gate_taken"], 1)
                act.wait_ge(z["nf_ready"], b + 1)
                act.activation(ef[:, :], nf[:, :], ACT.Exp).then_inc(z["own"], 1)
                act.wait_ge(z["own"], b + 1)
                act.activation(lnf[:, :], ef[:, :], ACT.Ln, bias=1.0).then_inc(z["ef_ready"], 1)
                act.wait_ge(z["em_in"], b + 1)
                act.activation(em[:, :], lm[:, :], ACT.Exp, scale=-1.0).then_inc(z["em_ready"], 1)
                for h in range(MH):
                    for t in range(SC):
                        act.wait_ge(z["d_ready"], 4 * (MH * b + h) + t + 1)
                        act.activation(D[:, t, 0:S - t * P], D[:, t, 0:S - t * P], ACT.Exp).then_inc(z["d_exp"], 1)
                act.wait_ge(z["o_done"], b + 1)
                act.wait_ge(z["o_stored"], 16 * b + 16)
                act.activation(o[:, :, :], bank[2][:, :].rearrange("p (c e) -> p c e", c=SC), ACT.Copy).then_inc(z["o_taken"], 1)

        @block.vector
        def _(dve):
            dve.wait_ge(z["consts"], 16 * len(consts))
            dve.wait_ge(z["half_set"], 4)
            chain = Chain(dve, z["chain"])
            PER = 60
            with dve.Fori(0, NB) as b:
                chain.base, chain.n = b * PER, 0
                dve.wait_ge(z["up_taken"], 4 * b + 2)
                for c in range(CH):
                    chain.add(dve.tensor_scalar(pre[:, c, :], xm[:, c, 0:S], conv[:, c, 0:1], conv[:, c, KS:KS + 1],
                                                ALU.mult, ALU.add))
                for k in range(1, KS):
                    chain.settle()
                    for c in range(CH):
                        chain.add(dve.scalar_tensor_tensor(pre[:, c, :], xm[:, c, k:k + S], conv[:, c, k:k + 1],
                                                           pre[:, c, :], ALU.mult, ALU.add))
                chain.settle()
                dve.wait_ge(z["up_taken"], 4 * b + 4)
                dve.sem_inc(z["conv_done"], 1)
                dve.wait_ge(z["exp4"], b + 1)
                chain.link(dve.tensor_scalar(sg[:, :, :], sg[:, :, :], 1.0, None, ALU.add))
                chain.link(dve.reciprocal(sg[:, :, :], sg[:, :, :]))
                dve.tensor_tensor(sg[:, :, :], sg[:, :, :], pre[:, :, :], ALU.mult).then_inc(z["silu_done"], 1)
                dve.wait_ge(z["silu_done"], b + 1)
                for c in range(CH):
                    chain.add(dve.tensor_scalar(sx[:, c, :], sg[:, c, :], chan[:, c, 1:2], None, ALU.mult))
                dve.wait_ge(z["gate_taken"], 2 * b + 2)
                dve.scalar_tensor_tensor(nf[:, :], fg[:, :], -1.0, fg[:, :], ALU.mult, ALU.min).then_inc(z["nf_ready"], 1)
                chain.link(dve.tensor_scalar(lf[:, :], fg[:, :], 0.0, None, ALU.min))
                dve.wait_ge(z["ef_ready"], b + 1)
                chain.link(dve.tensor_tensor(lf[:, :], lf[:, :], lnf[:, :], ALU.subtract))
                chain.link(dve.tensor_tensor_scan(lc[:, :], ones[:, :], lf[:, :], 0.0, ALU.mult, ALU.add))
                chain.link(dve.tensor_tensor(a[:, :], ig[:, :], lc[:, :], ALU.subtract))
                chain.link(dve.tensor_tensor_scan(cm[:, :], a[:, :], a[:, :], -3.0e38, ALU.max, ALU.max))
                chain.link(dve.tensor_scalar(nM[:, :], cm[:, :], -1.0, None, ALU.mult))
                dve.tensor_tensor(lm[:, :], lc[:, :], cm[:, :], ALU.add).then_inc(z["em_in"], 1)
                dve.wait_ge(z["cols_done"], b + 1)
                chain.link(dve.tensor_copy(cols[:, :, :, :], bank[7][:, 0:2 * SC * MH].rearrange("p (i c h) -> p i c h", i=2, c=SC)))
                for h in range(MH):
                    dve.wait_ge(z["mb_done"], MH * b + h + 1)
                    for t in range(SC):
                        dve.tensor_scalar(D[:, t, 0:S - t * P], bank[0][:, t * P:], cols[:, 0, t, h:h + 1], 0.0,
                                          ALU.add, ALU.min).then_inc(z["d_ready"], 1)
                    for t in range(SC):
                        n = 4 * (MH * b + h) + t + 1
                        dve.wait_ge(z["d_exp"], n)
                        dve.wait_ge(z["s_done"], n)
                        if h:
                            dve.wait_ge(z["h_done"], MH * b + h)
                        chain.link(dve.tensor_tensor(D[:, t, 0:P], D[:, t, 0:P], tri[:, :], ALU.mult))
                        dve.scalar_tensor_tensor(C[:, t, 0:S - t * P], bank[1 + t][:, 0:S - t * P], float(MD) ** -0.5,
                                                 D[:, t, 0:S - t * P], ALU.mult, ALU.mult).then_inc(z["c_ready"], 1)
                    dve.wait_ge(z["h_done"], MH * b + h + 1)
                    H = bank[5 + h % 2][:, 0:SC * (MD + 1)].rearrange("p (c e) -> p c e", c=SC)
                    chain.link(dve.tensor_scalar(nd[:, :], H[:, :, MD], -1.0, None, ALU.mult))
                    chain.link(dve.tensor_tensor(nd[:, :], nd[:, :], H[:, :, MD], ALU.max))
                    chain.link(dve.tensor_tensor(nd[:, :], nd[:, :], cols[:, 1, :, h], ALU.max))
                    chain.link(dve.tensor_scalar(nd[:, :], nd[:, :], 1e-6, None, ALU.add))
                    chain.link(dve.reciprocal(nd[:, :], nd[:, :]))
                    dve.tensor_tensor(hh[:, :, h, :], H[:, :, 0:MD], bc(nd[:, :].unsqueeze(2), [P, SC, MD]),
                                      ALU.mult).then_inc(z["h_taken"], 1)
                dve.wait_ge(z["h_taken"], MH * b + MH)
                hv = hh[:, :, :, :].rearrange("p c h d -> p (c h) d")
                last = None
                for i in range(SC * MH):
                    last = dve.bn_stats(stats[:, i, :], hv[:, i, :])
                chain.link(last)
                dve.sem_inc(z["stats_seen"], 1)
                for i in range(SC * MH):
                    last = dve.bn_aggr(mv[:, i, :], stats[:, i, :])
                chain.link(last)
                dve.tensor_scalar(ve[:, :], mv[:, :, 1], LN_EPS, None, ALU.add).then_inc(z["var_ready"], 1)
                wide = [P, SC * MH, MD]
                chain.link(dve.tensor_tensor(hv, hv, bc(mv[:, :, 0:1], wide), ALU.subtract))
                dve.wait_ge(z["rstd_ready"], b + 1)
                dve.tensor_tensor(hv, hv, bc(rstd[:, :].unsqueeze(2), wide), ALU.mult).then_inc(z["hn_ready"], 1)
                dve.wait_ge(z["hT_done"], b + 1)
                for c in range(CH):
                    chain.link(dve.scalar_tensor_tensor(sx[:, c, :], bank[c][:, :], chan[:, c, 0:1], sx[:, c, :],
                                                        ALU.mult, ALU.add))
                dve.tensor_tensor(hs[:, :, :], sx[:, :, :], sg[:, CH:, :], ALU.mult).then_inc(z["hs_ready"], 1)
                assert chain.n == PER, chain.n


def cross_phase(nc, d, xnT_dram, at_dram):
    with ExitStack() as ctx:
        sb, ps, sem = tools(nc, ctx, "cr")
        R = 8
        AH = 16
        AD = E // AH
        xnT = sb("xnT", [P, NCH * P])
        dirT = sb("dirT", [P, 2, E])
        kwT = sb("kwT", [P, E])
        lowA = sb("lowA", [R, 2, E])
        lowB = sb("lowB", [R, 2, E])
        mag = sb("mag", [P, 2])
        bias = sb("bias", [1, 4 * E])
        owT = sb("owT", [P, E])
        ident = sb("ident", [P, P])
        ones = sb("ones", [P, P])
        root = sb("root", [P, 2])
        w = sb("w", [P, 3, E])
        sq = sb("sq", [P, 2, E])
        ss = sb("ss", [P, 2])
        tot = sb("tot", [P, 2])
        nrm = sb("nrm", [P, 2])
        qkv = [sb(f"qkv{i}", [P, NB, 3, E]) for i in range(2)]
        prod = sb("prod", [P, NB, E])
        prod2 = sb("prod2", [P, E, NB])
        sc = sb("sc", [P, NB, NB, AH])
        pr = sb("pr", [P, NB, NB, AH])
        mx = sb("mx", [P, NB, AH])
        att = [sb(f"att{i}", [P, NB, E]) for i in range(2)]
        attT = sb("attT", [P, NB, P])
        o = sb("o", [P, NB, E])
        qp = [ps(f"qp{i}", [P, S]) for i in range(2)]
        tp = [ps(f"tp{i}", [P, S]) for i in range(2)]
        op = [ps(f"op{i}", [P, S]) for i in range(2)]
        wp = ps("wp", [P, S])
        z = {n: sem(n) for n in ("consts ones_set low_done sq_ready tot_done tot_ready root_ready w_ready q_done "
                                 "q_taken att_ready turned turned_taken o_done o_taken stored s_ready p_exp "
                                 "own").split()}
        clear(nc)
        block = ctx.enter_context(nc.Block())
        consts = [(xnT[:, :], xnT_dram[:, :]), (dirT[:, :, :], d["dirT"]), (kwT[:, :], d["k_wT"]), (lowA[:, :, :], d["lowA"]),
                  (lowB[:, :, :], d["lowB"]), (mag[:, :], d["mag"].partition_broadcast(P)), (bias[:, :], d["bias1"]),
                  (owT[:, :], d["out_wT"]), (ident[:, :], d["identity"])]
        at_v = at_dram.rearrange("b (c p) e -> c p b e", p=P)

        @block.sync
        def _(sp):
            for dst, src in consts:
                sp.dma_start(dst, src).then_inc(z["consts"], 16)
            for c in range(SC):
                sp.wait_ge(z["o_taken"], 2 * c + 2)
                sp.dma_start(at_v[c], o[:, :, :]).then_inc(z["stored"], 16)
            sp.wait_ge(z["stored"], 16 * SC)

        @block.gpsimd
        def _(pool):
            pool.memset(ones[:, :], 1.0).then_inc(z["ones_set"], 1)
            pool.memset(root[:, :], 0.5).then_inc(z["ones_set"], 1)
            pool.wait_ge(z["ones_set"], 2)
            pool.wait_ge(z["tot_ready"], 1)
            pool.tensor_tensor(nrm[:, :], tot[:, :], root[:, :], ALU.pow).then_inc(z["root_ready"], 1)

        @block.tensor
        def _(pe):
            pe.wait_ge(z["consts"], 16 * len(consts))
            pe.wait_ge(z["ones_set"], 2)
            for i in range(2):
                last = pe.matmul(wp[:, i * E:(i + 1) * E], lowA[:, i, :], lowB[:, i, :], start=True, stop=True)
            last.then_inc(z["low_done"], 1)
            pe.wait_ge(z["sq_ready"], 1)
            pe.matmul(wp[:, 2 * E:2 * E + 2], ones[:, :], ss[:, :], start=True, stop=True).then_inc(z["tot_done"], 1)
            pe.wait_ge(z["w_ready"], 3)
            for c in range(SC + 1):
                if c < SC:
                    for b in range(NB):
                        n = c * NB + b
                        if n >= 2:
                            pe.wait_ge(z["q_taken"], n - 1)
                        at = (b * SC + c) * P
                        pe.matmul(qp[n % 2][:, 0:3 * E], xnT[:, at:at + P], w[:, :, :].rearrange("p i e -> p (i e)"),
                                  start=True, stop=False)
                        pe.matmul(qp[n % 2][:, 0:3 * E], ones[0:1, :], bias[:, 0:3 * E], start=False, stop=True)\
                            .then_inc(z["q_done"], 1)
                if c:
                    m = c - 1
                    pe.wait_ge(z["att_ready"], m + 1)
                    for g in range(2):
                        if m:
                            pe.wait_ge(z["turned_taken"], 2 * m - 1 + g)
                        for b in range(4):
                            last = pe.transpose(tp[g][:, b * P:(b + 1) * P], att[m % 2][:, 4 * g + b, :], ident[:, :])
                        last.then_inc(z["turned"], 1)
                    for g in range(2):
                        pe.wait_ge(z["turned_taken"], 2 * m + g + 1)
                        if m:
                            pe.wait_ge(z["o_taken"], 2 * m - 1 + g)
                        for b in range(4):
                            pe.matmul(op[g][:, b * P:(b + 1) * P], attT[:, 4 * g + b, :], owT[:, :], start=True, stop=False)
                            last = pe.matmul(op[g][:, b * P:(b + 1) * P], ones[0:1, :], bias[:, 3 * E:], start=False, stop=True)
                        last.then_inc(z["o_done"], 1)

        @block.scalar
        def _(act):
            for c in range(SC + 2):
                if c < SC:
                    if c >= 2:
                        act.wait_ge(z["att_ready"], c - 1)
                    for b in range(NB):
                        act.wait_ge(z["q_done"], c * NB + b + 1)
                        act.activation(qkv[c % 2][:, b, :, :].rearrange("p i e -> p (i e)"), qp[b % 2][:, 0:3 * E],
                                       ACT.Copy).then_inc(z["q_taken"], 1)
                if 1 <= c <= SC:
                    act.wait_ge(z["s_ready"], c)
                    act.activation(pr[:, :, :, :], sc[:, :, :, :], ACT.Exp, scale=float(AD) ** -0.5).then_inc(z["p_exp"], 1)
                    m = c - 1
                    for g in range(2):
                        act.wait_ge(z["turned"], 2 * m + g + 1)
                        if m:
                            act.wait_ge(z["o_done"], 2 * m)
                        act.activation(attT[:, 4 * g:4 * g + 4, :], tp[g][:, :].rearrange("p (b s) -> p b s", b=4),
                                       ACT.Copy).then_inc(z["turned_taken"], 1)
                    for g in range(2):
                        act.wait_ge(z["o_done"], 2 * m + g + 1)
                        if m:
                            act.wait_ge(z["stored"], 16 * m)
                        act.activation(o[:, 4 * g:4 * g + 4, :], op[g][:, :].rearrange("p (b s) -> p b s", b=4),
                                       ACT.Copy).then_inc(z["o_taken"], 1)

        @block.vector
        def _(dve):
            chain = Chain(dve, z["own"])
            dve.wait_ge(z["consts"], 16 * len(consts))
            dve.wait_ge(z["ones_set"], 2)
            dve.wait_ge(z["low_done"], 1)
            low = wp[:, 0:2 * E].rearrange("p (i e) -> p i e", i=2)
            chain.link(dve.tensor_tensor(dirT[:, :, :], low, dirT[:, :, :], ALU.add))
            chain.link(dve.tensor_tensor(sq[:, :, :], dirT[:, :, :], dirT[:, :, :], ALU.mult))
            dve.tensor_reduce(ss[:, :], sq[:, :, :], AX.X, ALU.add).then_inc(z["sq_ready"], 1)
            dve.wait_ge(z["tot_done"], 1)
            dve.tensor_copy(tot[:, :], wp[:, 2 * E:2 * E + 2]).then_inc(z["tot_ready"], 1)
            dve.wait_ge(z["root_ready"], 1)
            chain.link(dve.tensor_scalar(nrm[:, :], nrm[:, :], 1e-8, None, ALU.add))
            chain.link(dve.reciprocal(nrm[:, :], nrm[:, :]))
            chain.link(dve.tensor_tensor(nrm[:, :], nrm[:, :], mag[:, :], ALU.mult))
            for i, at in ((0, 0), (1, 2)):
                dve.tensor_scalar(w[:, at, :], dirT[:, i, :], nrm[:, i:i + 1], None, ALU.mult).then_inc(z["w_ready"], 1)
            dve.tensor_copy(w[:, 1, :], kwT[:, :]).then_inc(z["w_ready"], 1)
            for c in range(SC):
                t = qkv[c % 2]
                dve.wait_ge(z["q_taken"], NB * (c + 1))
                for b in range(NB):
                    chain.link(dve.tensor_tensor(prod[:, :, :], t[:, :, 1, :], bc(t[:, b, 0, :].unsqueeze(1), [P, NB, E]), ALU.mult))
                    chain.link(dve.tensor_reduce(sc[:, b, :, :], prod[:, :, :].rearrange("p k (h e) -> p k h e", h=AH),
                                                 AX.X, ALU.add))
                chain.link(dve.tensor_reduce(mx[:, :, :], sc[:, :, :, :].rearrange("p q k h -> p q h k"), AX.X, ALU.max))
                for b in range(NB):
                    last = dve.tensor_tensor(sc[:, b, :, :], sc[:, b, :, :], bc(mx[:, b, :].unsqueeze(1), [P, NB, AH]),
                                             ALU.subtract)
                last.then_inc(z["s_ready"], 1)
                dve.wait_ge(z["p_exp"], c + 1)
                chain.link(dve.tensor_reduce(mx[:, :, :], pr[:, :, :, :].rearrange("p q k h -> p q h k"), AX.X, ALU.add))
                chain.link(dve.reciprocal(mx[:, :, :], mx[:, :, :]))
                if c >= 2:
                    dve.wait_ge(z["turned"], 2 * (c - 1))
                for b in range(NB):
                    chain.link(dve.tensor_tensor(prod2[:, :, :].rearrange("p (h e) k -> p h e k", h=AH),
                                                 bc(pr[:, b, :, :].rearrange("p k h -> p h k").unsqueeze(2), [P, AH, AD, NB]),
                                                 t[:, :, 2, :].rearrange("p k (h e) -> p h e k", h=AH), ALU.mult))
                    chain.link(dve.tensor_reduce(att[c % 2][:, b, :], prod2[:, :, :], AX.X, ALU.add))
                av = att[c % 2][:, :, :].rearrange("p b (h e) -> p (b h) e", h=AH)
                dve.tensor_tensor(av, av, bc(mx[:, :, :].rearrange("p b h -> p (b h)").unsqueeze(2), [P, NB * AH, AD]),
                                  ALU.mult).then_inc(z["att_ready"], 1)


def fp4(chain, act_abs, x, blocks, scale, inv, mag, big, small):
    dve = chain.eng
    shape = [P, blocks, QB]
    chain.link(dve.tensor_reduce(scale, x, AX.X, ALU.max, apply_absolute_value=True))
    chain.link(dve.tensor_scalar(scale, scale, 1.0 / 6.0, 1e-12, ALU.mult, ALU.max))
    chain.link(dve.reciprocal(inv, scale))
    act_abs(chain, dve.tensor_tensor(x, x, bc(inv.unsqueeze(2), shape), ALU.mult))
    chain.add(dve.tensor_scalar(inv, scale, 0.5, None, ALU.mult))
    chain.add(dve.tensor_scalar(big, mag, 5.0, 2.0, ALU.is_gt, ALU.mult))
    chain.link(dve.tensor_scalar(small, mag, 0.25, None, ALU.is_gt))
    chain.add(dve.scalar_tensor_tensor(big, mag, 2.5, big, ALU.is_gt, ALU.add))
    chain.link(dve.scalar_tensor_tensor(small, mag, 0.75, small, ALU.is_gt, ALU.add))
    chain.add(dve.scalar_tensor_tensor(big, mag, 3.5, big, ALU.is_gt, ALU.add))
    chain.link(dve.scalar_tensor_tensor(small, mag, 1.25, small, ALU.is_gt, ALU.add))
    chain.link(dve.scalar_tensor_tensor(small, mag, 1.75, small, ALU.is_gt, ALU.add))
    chain.link(dve.scalar_tensor_tensor(mag, big, 2.0, small, ALU.mult, ALU.add))
    chain.link(dve.tensor_tensor(mag, mag, bc(inv.unsqueeze(2), shape), ALU.mult))
    return dve.scalar_tensor_tensor(x.bitcast(U32), x.bitcast(U32), 0x80000000, mag.bitcast(U32),
                                    ALU.bitwise_and, ALU.bitwise_or)


def ffn_phase(nc, d, xn_dram, base_dram, at_dram, out_dram):
    with ExitStack() as ctx:
        sb, ps, sem = tools(nc, ctx, "ff")
        FB = FF // QB
        FK = 3
        WIDTH = [P, P, FF - 2 * P]
        STEPS = NCH // 2
        wgu = sb("wgu", [P, 2 * FK, E])
        wdn = sb("wdn", [P, FF])
        wguT = sb("wguT", [P, 2, FK * P])
        wdT = sb("wdT", [P, FK, E])
        ident = sb("ident", [P, P])
        x = [sb(f"x{i}", [P, 2, E]) for i in range(2)]
        base = [sb(f"base{i}", [P, 2, E]) for i in range(2)]
        at = [sb(f"at{i}", [P, 2, E]) for i in range(2)]
        xqT = sb("xqT", [P, 2, P])
        g = sb("g", [P, 2, FF])
        h = sb("h", [P, 2, FF])
        hT = sb("hT", [P, 2, FK, P])
        NBIG = 2 * FK * E
        mag = sb("mag", [P, NBIG])
        big = sb("big", [P, NBIG])
        small = sb("small", [P, NBIG])
        scale = sb("scale", [P, NBIG // QB])
        inv = sb("inv", [P, NBIG // QB])
        o = [sb(f"o{i}", [P, 2, E]) for i in range(2)]
        gp = [ps(f"gp{i}", [P, S]) for i in range(2)]
        up = [ps(f"up{i}", [P, S]) for i in range(2)]
        tx = ps("tx", [P, S])
        th = [ps(f"th{i}", [P, S]) for i in range(2)]
        op = ps("op", [P, S])
        z = {n: sem(n) for n in ("consts w_ready w_turned w_taken scaled absed xq_ready xq_done xq_taken gu_done "
                                 "g_exp h_open hq_ready h_done h_taken o_done o_added own").split()}
        loaded, stored = ([sem(f"{n}{i}") for i in range(2)] for n in ("loaded", "stored"))
        clear(nc)
        block = ctx.enter_context(nc.Block())
        pair = lambda t, n: t.rearrange("b (k c p) e -> (b k) p c e", p=P, c=2)[bass.DynSlice(n, 1)].rearrange("o p c e -> (o p) c e")

        def steps(eng, body):
            for u in range(2):
                body(u, u, 0)
            with eng.Fori(1, STEPS // 2) as i:
                for u in range(2):
                    body(2 * i + u, u, i)

        @block.sync
        def _(sp):
            for dst, name in ((wgu[:, :, :], "w_gu"), (wdn[:, :], "w_down1"), (ident[:, :], "identity")):
                sp.dma_start(dst, d[name]).then_inc(z["consts"], 16)

            def load(n, u):
                for dst, src in ((x, xn_dram), (base, base_dram), (at, at_dram)):
                    sp.dma_start(dst[u][:, :, :], pair(src, n)).then_inc(loaded[u], 16)

            load(0, 0)
            load(1, 1)

            def body(n, u, i):
                sp.wait_ge(z["o_added"], n + 1)
                sp.dma_start(pair(out_dram, n), o[u][:, :, :]).then_inc(stored[u], 16)
                if isinstance(n, int) and n < 2:
                    load(n + 2, u)

            for u in range(2):
                body(u, u, 0)
            with sp.Fori(1, STEPS // 2 - 1) as i:
                for u in range(2):
                    n = 2 * i + u
                    sp.wait_ge(z["o_added"], n + 1)
                    sp.dma_start(pair(out_dram, n), o[u][:, :, :]).then_inc(stored[u], 16)
                    load(n + 2, u)
            for u in range(2):
                body(STEPS - 2 + u, u, 0)
            for u in range(2):
                sp.wait_ge(stored[u], 16 * STEPS // 2)

        @block.tensor
        def _(pe):
            pe.wait_ge(z["consts"], 48)
            pe.wait_ge(z["w_ready"], 2)
            for i in range(2):
                for k in range(FK):
                    last = pe.transpose(gp[i][:, k * P:(k + 1) * P], wgu[:, FK * i + k, :], ident[:, :])
            for k in range(FK):
                last = pe.transpose(up[0][0:WIDTH[k], k * P:(k + 1) * P], wdn[:, k * P:k * P + WIDTH[k]], ident[:, :])
            last.then_inc(z["w_turned"], 1)
            pe.wait_ge(z["w_taken"], 1)

            def gate_up(n, u, i):
                pe.wait_ge(z["xq_ready"], n + 1)
                for c in range(2):
                    last = pe.transpose(tx[:, c * P:(c + 1) * P], x[u][:, c, :], ident[:, :])
                last.then_inc(z["xq_done"], 1)
                pe.wait_ge(z["xq_taken"], n + 1)
                if not isinstance(n, int) or n:
                    pe.wait_ge(z["h_open"], n)
                for c in range(2):
                    pe.matmul(gp[c][:, 0:FF], xqT[:, c, :], wguT[:, 0, 0:FF], start=True, stop=True)
                    last = pe.matmul(up[c][:, 0:FF], xqT[:, c, :], wguT[:, 1, 0:FF], start=True, stop=True)
                last.then_inc(z["gu_done"], 1)

            def down(n, u, i):
                pe.wait_ge(z["hq_ready"], n + 1)
                for c in range(2):
                    for k in range(FK):
                        last = pe.transpose(th[c][0:WIDTH[k], k * P:(k + 1) * P], h[:, c, k * P:k * P + WIDTH[k]], ident[:, :])
                last.then_inc(z["h_done"], 1)
                pe.wait_ge(z["h_taken"], n + 1)
                if not isinstance(n, int) or n:
                    pe.wait_ge(z["o_added"], n)
                for c in range(2):
                    for k in range(FK):
                        last = pe.matmul(op[:, c * P:(c + 1) * P], hT[0:WIDTH[k], c, k, :], wdT[0:WIDTH[k], k, :],
                                         start=(k == 0), stop=(k == FK - 1))
                last.then_inc(z["o_done"], 1)

            gate_up(0, 0, 0)
            for n in range(2):
                gate_up(n + 1, (n + 1) % 2, 0)
                down(n, n, 0)
            with pe.Fori(1, STEPS // 2 - 1) as i:
                for u in range(2):
                    gate_up(2 * i + u + 1, (u + 1) % 2, i)
                    down(2 * i + u, u, i)
            gate_up(STEPS - 1, 1, 0)
            down(STEPS - 2, 0, 0)
            down(STEPS - 1, 1, 0)

        @block.scalar
        def _(act):
            act.wait_ge(z["w_turned"], 1)
            for i in range(2):
                act.activation(wguT[:, i, :], gp[i][:, 0:FK * P], ACT.Copy)
            for k in range(FK):
                last = act.activation(wdT[0:WIDTH[k], k, :], up[0][0:WIDTH[k], k * P:(k + 1) * P], ACT.Copy)
            last.then_inc(z["w_taken"], 1)

            def early(n, u, i):
                act.wait_ge(z["xq_done"], n + 1)
                if not isinstance(n, int) or n:
                    act.wait_ge(z["gu_done"], n)
                act.activation(xqT[:, :, :], tx[:, 0:2 * P].rearrange("p (c t) -> p c t", c=2), ACT.Copy)\
                    .then_inc(z["xq_taken"], 1)
                act.wait_ge(z["gu_done"], n + 1)
                if not isinstance(n, int) or n:
                    act.wait_ge(z["h_open"], n)
                for c in range(2):
                    last = act.activation(g[:, c, :], gp[c][:, 0:FF], ACT.Exp, scale=-1.0)
                last.then_inc(z["g_exp"], 1)

            def late(n, u, i):
                act.wait_ge(z["h_done"], n + 1)
                if not isinstance(n, int) or n:
                    act.wait_ge(z["o_done"], n)
                for c in range(2):
                    for k in range(FK):
                        last = act.activation(hT[0:WIDTH[k], c, k, :], th[c][0:WIDTH[k], k * P:(k + 1) * P], ACT.Copy)
                last.then_inc(z["h_taken"], 1)

            early(0, 0, 0)
            for n in range(2):
                early(n + 1, (n + 1) % 2, 0)
                late(n, n, 0)
            with act.Fori(1, STEPS // 2 - 1) as i:
                for u in range(2):
                    early(2 * i + u + 1, (u + 1) % 2, i)
                    late(2 * i + u, u, i)
            early(STEPS - 1, 1, 0)
            late(STEPS - 2, 0, 0)
            late(STEPS - 1, 1, 0)

        @block.vector
        def _(dve):
            chain = Chain(dve, z["own"])

            def quant(x3, blocks):
                v = lambda t: t[:, 0:blocks * QB].rearrange("p (b q) -> p b q", q=QB)

                def magnitude(ch, ins):
                    ch.link(ins)
                    ch.link(dve.scalar_tensor_tensor(v(mag), x3, -1.0, x3, ALU.mult, ALU.max))
                return fp4(chain, magnitude, x3, blocks, scale[:, 0:blocks], inv[:, 0:blocks], v(mag), v(big), v(small))

            dve.wait_ge(z["consts"], 48)
            quant(wgu[:, :, :].rearrange("p k (b q) -> p (k b) q", q=QB), NBIG // QB).then_inc(z["w_ready"], 1)
            dve.wait_ge(z["w_ready"], 1)
            quant(wdn[:, :].rearrange("p (b q) -> p b q", q=QB), FB).then_inc(z["w_ready"], 1)
            dve.wait_ge(z["w_ready"], 2)

            def early(n, u, i):
                dve.wait_ge(loaded[u], 48 * i + 48)
                quant(x[u][:, :, :].rearrange("p c (b q) -> p (c b) q", q=QB), 2 * E // QB).then_inc(z["xq_ready"], 1)

            def late(n, u, i):
                dve.wait_ge(z["g_exp"], n + 1)
                if not isinstance(n, int) or n:
                    dve.wait_ge(z["h_done"], n)
                chain.link(dve.tensor_scalar(g[:, :, :], g[:, :, :], 1.0, None, ALU.add))
                chain.link(dve.reciprocal(g[:, :, :], g[:, :, :]))
                for c in range(2):
                    chain.add(dve.tensor_tensor(h[:, c, :], gp[c][:, 0:FF], g[:, c, :], ALU.mult))
                chain.settle()
                for c in range(2):
                    last = dve.tensor_tensor(h[:, c, :], up[c][:, 0:FF], h[:, c, :], ALU.mult)
                last.then_inc(z["h_open"], 1)
                dve.wait_ge(z["h_open"], n + 1)
                quant(h[:, :, :].rearrange("p c (b q) -> p (c b) q", q=QB), 2 * FB).then_inc(z["hq_ready"], 1)
                chain.link(dve.tensor_tensor(base[u][:, :, :], base[u][:, :, :], at[u][:, :, :], ALU.add))
                dve.wait_ge(z["o_done"], n + 1)
                if not isinstance(i, int) or i:
                    dve.wait_ge(stored[u], 16 * i)
                dve.tensor_tensor(o[u][:, :, :], op[:, 0:2 * P].rearrange("p (c e) -> p c e", c=2), base[u][:, :, :],
                                  ALU.add).then_inc(z["o_added"], 1)

            def body(n, u, i, more=True):
                if more:
                    early(n + 1, (u + 1) % 2, i + u)
                late(n, u, i)

            early(0, 0, 0)
            first = chain.n
            for n in range(2):
                body(n, n, 0)
            per = chain.n - first
            with dve.Fori(1, STEPS // 2 - 1) as i:
                chain.base, chain.n = i * per + first, 0
                for u in range(2):
                    body(2 * i + u, u, i)
                assert chain.n == per
            chain.base, chain.n = first + per * (STEPS // 2 - 1), 0
            body(STEPS - 2, 0, STEPS // 2 - 1)
            body(STEPS - 1, 1, STEPS // 2 - 1, more=False)


def layout_mlstm(g, o):
    import numpy as np

    f = np.float32
    CH = INNER // P
    o["w_up"] = g["L0_attn_w_up"].T
    o["conv"] = np.concatenate([g["L0_attn_conv_w"][:, 0, :], g["L0_attn_conv_b"][:, None]], 1).reshape(CH, P, 5).transpose(1, 0, 2)
    for n in "qkv":
        w = g[f"L0_attn_w_{n}"]
        blk = w.shape[1]
        full = np.zeros((P, CH, P), f)
        for j in range(w.shape[0]):
            c, r = divmod(j * blk, P)
            full[r:r + blk, c, r:r + blk] = w[j].T
        o["bd" + n] = full
    gates = np.stack([g["L0_attn_w_ig"], g["L0_attn_w_fg"]])
    o["w_gates"] = gates.reshape(2, MH, 3 * CH, P).transpose(3, 0, 2, 1)
    o["b_gates"] = np.stack([g["L0_attn_b_ig"], g["L0_attn_b_fg"]], 1)
    o["chan"] = np.stack([g["L0_attn_ln_w"].reshape(-1), g["L0_attn_skip"]], 1).reshape(CH, P, 2).transpose(1, 0, 2)
    o["w_down0"] = g["L0_attn_w_down"].T.reshape(CH, P, E).transpose(1, 0, 2)
    sel = np.zeros((MH, MH, P), f)
    for h in range(MH):
        sel[h, h] = 1
    o["sel"] = sel
    o["tri"] = np.triu(np.ones((P, P), f))


def layout_layer1(g, o):
    import numpy as np

    f = np.float32
    o["dirT"] = np.stack([g["L1_attn_dir_q"].T, g["L1_attn_dir_v"].T], 1)
    o["k_wT"] = g["L1_attn_k_w"].T
    o["lowA"] = np.stack([g["L1_attn_A_q"], g["L1_attn_A_v"]], 1)
    o["lowB"] = np.stack([g["L1_attn_B_q"].T, g["L1_attn_B_v"].T], 1)
    o["mag"] = np.stack([g["L1_attn_mag_q"].reshape(()), g["L1_attn_mag_v"].reshape(())])
    o["bias1"] = np.concatenate([g[f"L1_attn_{n}"] for n in ("bias_q", "k_b", "bias_v", "out_b")])[None]
    o["out_wT"] = g["L1_attn_out_w"].T
    wgu = np.zeros((2, 3 * P, E), f)
    wgu[0, :FF] = g["L1_ffn_w_gate"]
    wgu[1, :FF] = g["L1_ffn_w_up"]
    o["w_gu"] = wgu.reshape(6, P, E).transpose(1, 0, 2)
    o["w_down1"] = g["L1_ffn_w_down"]


def layout(inp):
    import numpy as np

    f = np.float32
    g = {n: np.ascontiguousarray(np.asarray(a)) for n, a in inp.items()}
    perm = np.array([(2 * p + s) * HD + dd for s in range(2) for dd in range(HD) for p in range(NH // 2)])
    o = {"x": g["L0_attn_x"]}
    o["rW1T"] = g["L0_ffn_rW1"].T
    o["rb1"] = g["L0_ffn_rb1"][None]
    o["rW2T"] = g["L0_ffn_rW2"].T
    o["rb2"] = g["L0_ffn_rb2"][None]
    o["ln_g"] = g["L0_ffn_ln_g"]
    o["ln_b"] = g["L0_ffn_ln_b"]
    kT = g["L0_ffn_kW"].transpose(0, 2, 1)[:, :, perm]
    o["wkv"] = np.concatenate([kT, g["L0_ffn_vW"].transpose(0, 2, 1), g["L0_ffn_kb"][:, perm, None]], 2)
    o["vb"] = g["L0_ffn_vb"]
    o["wq"] = np.concatenate([g["L0_ffn_qW"].transpose(0, 2, 1)[:, :, perm], g["L0_ffn_qb"][:, perm, None]], 2)
    o["wo"] = g["L0_ffn_oW"].transpose(0, 2, 1)
    o["ob"] = g["L0_ffn_ob"]
    o["identity"] = np.eye(P, dtype=f)
    o["lower"] = np.triu(np.ones((P, P), f), 1)
    o["iota"] = np.broadcast_to(np.arange(P, dtype=f), (P, P))
    o["iota8"] = np.broadcast_to(np.arange(NE, dtype=f), (P, NE))
    tile = np.arange(TILES)
    o["tile_start"] = np.broadcast_to((np.arange(NT) * P).astype(f), (P, NT))
    o["first_slot"] = np.broadcast_to((tile % NT * P).astype(f), (P, TILES))
    o["keep"] = np.broadcast_to((tile % NT > 0).astype(f), (P, TILES))
    o["batch_start"] = np.broadcast_to((tile // NT * NE).astype(f), (P, TILES))
    o["tile_batch"] = (tile // NT).astype(np.int32)[None]
    layout_mlstm(g, o)
    layout_layer1(g, o)
    return o


def build(nc, d, out):
    def scratch(name, shape, dt=F32):
        return nc.dram_tensor(name, shape, dt).ap()

    xn0 = scratch("xn0", [NB, S, E])
    xn0T = scratch("xn0T", [P, NB * S])
    route = scratch("route", [P, NB * NE, 2 * SC])
    texp = scratch("texp", [1, 2 * TILES], I32)
    kst = scratch("kst", [NB * NE, 2 * KQ, NH // 2, S], BF16)
    v = scratch("v", [NB * NE, P, SC, NH, HD + 1])
    moe = scratch("moe", [TILES, P, SC, E])
    ml = scratch("ml", [NB, S, E])
    x1 = scratch("x1", [NB, S, E])
    xn1 = scratch("xn1", [NB, S, E])
    xn1T = scratch("xn1T", [P, NB * S])
    at = scratch("at", [NB, S, E])
    norm_phase(nc, "n0", d["x"], xn0, xn0T, d["identity"])
    router_phase(nc, d, xn0T, route, texp)
    kv_phase(nc, d, xn0T, kst, v)
    experts_phase(nc, d, xn0, kst, v, route, texp, moe)
    mlstm_phase(nc, d, xn0T, ml)
    norm_phase(nc, "n1", d["x"], xn1, xn1T, d["identity"], sum_dram=x1,
               adds=(lambda b: ml[b].rearrange("(c p) e -> p c e", p=P), lambda b: moe[b * NT + NT - 1]))
    cross_phase(nc, d, xn1T, at)
    ffn_phase(nc, d, xn1, x1, at, out)


def kernel(**inputs):
    import numpy as _np
    import concourse.bacc as _bacc
    from concourse.bass_utils import run_bass_kernel_spmd as _run

    nc = _bacc.Bacc("TRN2", target_bir_lowering=False, num_devices=1)
    arrays = {f"in_{n}": _np.ascontiguousarray(a) for n, a in layout(inputs).items()}
    d = {n[3:]: nc.dram_tensor(n, a.shape, mybir.dt.from_np(a.dtype), kind="ExternalInput").ap()
         for n, a in arrays.items()}
    out = nc.dram_tensor("out", (NB, S, E), F32, kind="ExternalOutput").ap()
    build(nc, d, out)
    r = _run(nc, [arrays], core_ids=[0])
    return r.results[0]["out"]
```

```python
from contextlib import ExitStack

import concourse.bass as bass
from concourse import mybir

F32 = mybir.dt.float32
BF16 = mybir.dt.bfloat16
I32 = mybir.dt.int32
U32 = mybir.dt.uint32
ACT = mybir.ActivationFunctionType
ALU = mybir.AluOpType
AX = mybir.AxisListType

P = 128
NB, S, E = 8, 512, 128
SC = S // P
NCH = NB * SC
NE, NH, HD = 8, 16, 8
NT = 15
TILES = NB * NT
LN_EPS = 1e-5
KQ = 48
QPART = (0, 0, 1, 0, 1, 2)
KPART = (0, 1, 0, 2, 1, 0)
INNER, MH, MD = 256, 4, 64
FF = 352
QB = 16


class Chain:

    def __init__(self, eng, sem, base=0):
        self.eng, self.sem, self.base, self.n = eng, sem, base, 0

    def add(self, ins):
        self.n += 1
        ins.then_inc(self.sem, 1)

    def settle(self):
        self.eng.wait_ge(self.sem, self.base + self.n)

    def link(self, ins):
        self.add(ins)
        self.settle()


def tools(nc, ctx, tag):
    def sb(name, shape, dt=F32):
        return ctx.enter_context(nc.sbuf_tensor(f"{tag}_{name}", shape, dt))

    def ps(name, shape, dt=F32):
        return ctx.enter_context(nc.psum_tensor(f"{tag}_{name}", shape, dt))

    def sem(name):
        s = ctx.enter_context(nc.semaphore(f"{tag}_{name}"))
        MADE.append(s)
        return s

    MADE.clear()
    return sb, ps, sem


MADE = []


def clear(nc):
    with nc.Block() as block:
        @block.sync
        def _(sp):
            for s in MADE:
                sp.sem_clear(s)




def bc(ap, shape):
    return ap.to_broadcast(shape)


def norm_phase(nc, tag, x_dram, xn_dram, xnT_dram, identity, adds=(), sum_dram=None):
    x_v = x_dram.rearrange("b (c p) e -> p (b c) e", p=P)
    xn_v = xn_dram.rearrange("b (c p) e -> p (b c) e", p=P)
    with ExitStack() as ctx:
        sb, ps, sem = tools(nc, ctx, tag)
        x = sb("x", [P, NCH, E])
        xn = sb("xn", [P, NCH, E])
        xnT = sb("xnT", [P, NCH * P])
        ident = sb("ident", [P, P])
        stats = sb("stats", [P, NCH, 6])
        mv = sb("mv", [P, NCH, 2])
        ve = sb("ve", [P, NCH])
        half = sb("half", [P, NCH])
        rstd = sb("rstd", [P, NCH])
        tp = [ps(f"tp{i}", [P, SC * P]) for i in range(2)]
        more = [sb(f"more{i}", [P, NCH, E]) for i in range(len(adds))]
        loaded, ident_loaded, half_set, var_ready, rstd_ready, xn_ready, turned, taken, stored, own = (
            sem(n) for n in ("loaded", "ident_loaded", "half_set", "var_ready", "rstd_ready", "xn_ready",
                             "turned", "taken", "stored", "own"))
        if adds:
            clear(nc)
        block = ctx.enter_context(nc.Block())

        @block.sync
        def _(sp):
            for b in range(NB):
                sp.dma_start(x[:, b * SC:(b + 1) * SC, :], x_v[:, b * SC:(b + 1) * SC, :]).then_inc(loaded, 16)
                for t, source in zip(more, adds):
                    sp.dma_start(t[:, b * SC:(b + 1) * SC, :], source(b)).then_inc(loaded, 16)
                if b == 0:
                    sp.dma_start(ident[:, :], identity).then_inc(ident_loaded, 16)
            for b in range(NB):
                sp.wait_ge(xn_ready, (b + 1) * SC)
                if adds:
                    sp.dma_start(sum_dram.rearrange("b (c p) e -> p (b c) e", p=P)[:, b * SC:(b + 1) * SC, :],
                                 x[:, b * SC:(b + 1) * SC, :]).then_inc(stored, 16)
                sp.dma_start(xn_v[:, b * SC:(b + 1) * SC, :], xn[:, b * SC:(b + 1) * SC, :]).then_inc(stored, 16)
                sp.wait_ge(taken, b + 1)
                sp.dma_start(xnT_dram[:, b * S:(b + 1) * S], xnT[:, b * S:(b + 1) * S]).then_inc(stored, 16)
            sp.wait_ge(stored, (48 if adds else 32) * NB)

        @block.gpsimd
        def _(pool):
            pool.memset(half[:, :], -0.5).then_inc(half_set, 1)
            pool.wait_ge(half_set, 1)
            pool.wait_ge(var_ready, 1)
            pool.tensor_tensor(rstd[:, :], ve[:, :], half[:, :], ALU.pow).then_inc(rstd_ready, 1)

        @block.vector
        def _(dve):
            chain = Chain(dve, own)
            dve.wait_ge(loaded, 16 * NB * (1 + len(adds)))
            for t in more:
                chain.link(dve.tensor_tensor(x[:, :, :], x[:, :, :], t[:, :, :], ALU.add))
            for c in range(NCH):
                chain.add(dve.bn_stats(stats[:, c, :], x[:, c, :]))
            chain.settle()
            for c in range(NCH):
                chain.add(dve.bn_aggr(mv[:, c, :], stats[:, c, :]))
            chain.settle()
            dve.tensor_scalar(ve[:, :], mv[:, :, 1], LN_EPS, None, ALU.add).then_inc(var_ready, 1)
            dve.wait_ge(rstd_ready, 1)
            for c in range(NCH):
                dve.tensor_scalar(xn[:, c, :], x[:, c, :], mv[:, c, 0:1], rstd[:, c:c + 1],
                                  ALU.subtract, ALU.mult).then_inc(xn_ready, 1)

        @block.tensor
        def _(pe):
            pe.wait_ge(ident_loaded, 16)
            for b in range(NB):
                pe.wait_ge(xn_ready, (b + 1) * SC)
                if b >= 2:
                    pe.wait_ge(taken, b - 1)
                for c in range(SC):
                    last = pe.transpose(tp[b % 2][:, c * P:(c + 1) * P], xn[:, b * SC + c, :], ident[:, :])
                last.then_inc(turned, 1)

        @block.scalar
        def _(act):
            for b in range(NB):
                act.wait_ge(turned, b + 1)
                act.activation(xnT[:, b * S:(b + 1) * S], tp[b % 2][:, :], ACT.Copy).then_inc(taken, 1)


def router_phase(nc, d, xnT_dram, route_dram, texp_dram):
    with ExitStack() as ctx:
        sb, ps, sem = tools(nc, ctx, "rt")
        R = 64
        xnT = sb("xnT", [P, NCH * P])
        w1 = sb("w1", [P, R])
        b1 = sb("b1", [1, R])
        w2 = sb("w2", [R, NE])
        b2 = sb("b2", [1, NE])
        gain = sb("gain", [P, R])
        shift = sb("shift", [P, R])
        ident = sb("ident", [P, P])
        lower = sb("lower", [P, P])
        ones = sb("ones", [P, P])
        iota8 = sb("iota8", [P, NE])
        tstart = sb("tstart", [P, NT])
        bstart = sb("bstart", [P, TILES])
        h = sb("h", [P, NCH, R])
        stats = sb("stats", [P, NCH, 6])
        mv = sb("mv", [P, NCH, 2])
        ve = sb("ve", [P, NCH])
        half = sb("half", [P, NCH])
        rstd = sb("rstd", [P, NCH])
        hT = sb("hT", [R, NCH * P])
        lg = sb("lg", [P, NCH, NE])
        mx = sb("mx", [P, NCH])
        sm = sb("sm", [P, NCH])
        top = sb("top", [P, NCH, 8])
        idx = sb("idx", [P, NCH, 8], U32)
        idf = sb("idf", [P, NCH, 2])
        m1 = sb("m1", [P, NCH, NE])
        m2 = sb("m2", [P, NCH, NE])
        g1 = sb("g1", [P, NCH, NE])
        g2 = sb("g2", [P, NCH, NE])
        den = sb("den", [P, NCH])
        w = sb("w", [P, NCH, 2])
        rank = sb("rank", [P, NB, SC, NE])
        tot = sb("tot", [P, NB, SC, NE])
        cnt = sb("cnt", [P, NB, NE])
        pc = sb("pc", [P, NB, NE])
        tmp = sb("tmp", [P, NB, NE])
        off = sb("off", [P, NB, NE])
        end = sb("end", [P, NB, NE])
        cmp = sb("cmp", [P, NB, NT, NE])
        tx = sb("tx", [P, 2, TILES])
        txi = sb("txi", [P, 2, TILES], I32)
        route = sb("route", [P, NB * NE, 2 * SC])
        hp = [ps(f"hp{i}", [P, 8 * R]) for i in range(2)]
        tp = [ps(f"tp{i}", [P, 4 * P]) for i in range(2)]
        lp = ps("lp", [P, NCH * NE])
        rp = ps("rp", [P, 2 * NCH * NE])
        loaded, half_set, h_ready, h_taken, var_ready, rstd_ready, act_ready, turned, hT_taken, lg_ready, \
            sub_ready, exp_ready, mask_ready, rank_ready, table_ready, stored, own = (
                sem(n) for n in ("loaded", "half_set", "h_ready", "h_taken", "var_ready", "rstd_ready",
                                 "act_ready", "turned", "hT_taken", "lg_ready", "sub_ready", "exp_ready",
                                 "mask_ready", "rank_ready", "table_ready", "stored", "own"))
        block = ctx.enter_context(nc.Block())
        G = NCH // 8

        @block.sync
        def _(sp):
            loads = [(xnT[:, :], xnT_dram[:, :]), (w1[:, :], d["rW1T"]), (b1[:, :], d["rb1"]), (w2[:, :], d["rW2T"]),
                     (b2[:, :], d["rb2"]), (gain[:, :], d["ln_g"].partition_broadcast(P)),
                     (shift[:, :], d["ln_b"].partition_broadcast(P)), (ident[:, :], d["identity"]),
                     (lower[:, :], d["lower"]), (iota8[:, :], d["iota8"]), (tstart[:, :], d["tile_start"]),
                     (bstart[:, :], d["batch_start"])]
            for dst, src in loads:
                sp.dma_start(dst, src).then_inc(loaded, 16)
            sp.wait_ge(table_ready, 1)
            sp.dma_start(route_dram[:, :, :], route[:, :, :]).then_inc(stored, 16)
            sp.dma_start(texp_dram[:, :], txi[0:1, :, :].rearrange("p i t -> p (i t)")).then_inc(stored, 16)
            sp.wait_ge(stored, 32)

        @block.gpsimd
        def _(pool):
            pool.memset(half[:, :], -0.5).then_inc(half_set, 1)
            pool.memset(ones[:, :], 1.0).then_inc(half_set, 1)
            pool.wait_ge(half_set, 2)
            pool.wait_ge(var_ready, 1)
            pool.tensor_tensor(rstd[:, :], ve[:, :], half[:, :], ALU.pow).then_inc(rstd_ready, 1)

        @block.tensor
        def _(pe):
            pe.wait_ge(loaded, 16 * 12)
            pe.wait_ge(half_set, 2)
            for g in range(G):
                if g >= 2:
                    pe.wait_ge(h_taken, g - 1)
                for i in range(8):
                    o = hp[g % 2][:, i * R:(i + 1) * R]
                    pe.matmul(o, xnT[:, (8 * g + i) * P:(8 * g + i + 1) * P], w1[:, :], start=True, stop=False)
                    last = pe.matmul(o, ones[0:1, :], b1[:, :], start=False, stop=True)
                last.then_inc(h_ready, 1)
            for g in range(NCH // 4):
                if g == 0:
                    pe.wait_ge(act_ready, 1)
                if g >= 2:
                    pe.wait_ge(hT_taken, g - 1)
                for i in range(4):
                    last = pe.transpose(tp[g % 2][0:R, i * P:(i + 1) * P], h[:, 4 * g + i, :], ident[:, :])
                last.then_inc(turned, 1)
            pe.wait_ge(hT_taken, NCH // 4)
            for c in range(NCH):
                o = lp[:, c * NE:(c + 1) * NE]
                pe.matmul(o, hT[:, c * P:(c + 1) * P], w2[:, :], start=True, stop=False)
                last = pe.matmul(o, ones[0:1, :], b2[:, :], start=False, stop=True)
            last.then_inc(lg_ready, 1)
            pe.wait_ge(mask_ready, 1)
            mask = m1[:, :, :].rearrange("p c e -> p (c e)")
            pe.matmul(rp[:, 0:NCH * NE], lower[:, :], mask, start=True, stop=True)
            pe.matmul(rp[:, NCH * NE:2 * NCH * NE], ones[:, :], mask, start=True, stop=True).then_inc(rank_ready, 1)

        @block.scalar
        def _(act):
            for g in range(G):
                act.wait_ge(h_ready, g + 1)
                act.activation(h[:, 8 * g:8 * g + 8, :], hp[g % 2][:, :].rearrange("p (c r) -> p c r", c=8),
                               ACT.Copy).then_inc(h_taken, 1)
            for g in range(NCH // 4):
                act.wait_ge(turned, g + 1)
                act.activation(hT[:, 4 * g * P:4 * (g + 1) * P], tp[g % 2][0:R, :], ACT.Copy).then_inc(hT_taken, 1)
            act.wait_ge(sub_ready, 1)
            act.activation(g1[:, :, :], lg[:, :, :], ACT.Exp).then_inc(exp_ready, 1)

        @block.vector
        def _(dve):
            chain = Chain(dve, own)
            dve.wait_ge(loaded, 16 * 12)
            dve.wait_ge(h_taken, G)
            for c in range(NCH):
                chain.add(dve.bn_stats(stats[:, c, :], h[:, c, :]))
            chain.settle()
            for c in range(NCH):
                chain.add(dve.bn_aggr(mv[:, c, :], stats[:, c, :]))
            chain.settle()
            dve.tensor_scalar(ve[:, :], mv[:, :, 1], LN_EPS, None, ALU.add).then_inc(var_ready, 1)
            dve.wait_ge(rstd_ready, 1)
            wide = [P, NCH, R]
            chain.link(dve.tensor_tensor(h[:, :, :], h[:, :, :], bc(mv[:, :, 0:1], wide), ALU.subtract))
            chain.link(dve.tensor_tensor(h[:, :, :], h[:, :, :], bc(rstd[:, :].unsqueeze(2), wide), ALU.mult))
            chain.link(dve.tensor_tensor(h[:, :, :], h[:, :, :], bc(gain[:, :].unsqueeze(1), wide), ALU.mult))
            chain.link(dve.tensor_tensor(h[:, :, :], h[:, :, :], bc(shift[:, :].unsqueeze(1), wide), ALU.add))
            dve.tensor_scalar(h[:, :, :], h[:, :, :], 0.0, None, ALU.max).then_inc(act_ready, 1)
            dve.wait_ge(lg_ready, 1)
            lp_v = lp[:, :].rearrange("p (c e) -> p c e", e=NE)
            each = [P, NCH, NE]
            chain.link(dve.tensor_reduce(mx[:, :], lp_v, AX.X, ALU.max))
            dve.tensor_tensor(lg[:, :, :], lp_v, bc(mx[:, :].unsqueeze(2), each), ALU.subtract).then_inc(sub_ready, 1)
            dve.wait_ge(exp_ready, 1)
            chain.link(dve.tensor_reduce(sm[:, :], g1[:, :, :], AX.X, ALU.add))
            chain.link(dve.reciprocal(mx[:, :], sm[:, :]))
            chain.link(dve.tensor_tensor(g1[:, :, :], g1[:, :, :], bc(mx[:, :].unsqueeze(2), each), ALU.mult))
            for c in range(NCH):
                chain.add(dve.max(top[:, c, :], g1[:, c, :]))
            chain.settle()
            for c in range(NCH):
                chain.add(dve.max_index(idx[:, c, :], top[:, c, :], g1[:, c, :]))
            chain.settle()
            chain.link(dve.tensor_copy(idf[:, :, :], idx[:, :, 0:2]))
            chain.link(dve.tensor_tensor(den[:, :], top[:, :, 0], top[:, :, 1], ALU.add))
            chain.link(dve.reciprocal(sm[:, :], den[:, :]))
            chain.link(dve.tensor_tensor(w[:, :, :], top[:, :, 0:2], bc(sm[:, :].unsqueeze(2), [P, NCH, 2]), ALU.mult))
            iota_b = bc(iota8[:, :].unsqueeze(1), each)
            chain.link(dve.tensor_tensor(m1[:, :, :], iota_b, bc(idf[:, :, 0:1], each), ALU.is_equal))
            chain.link(dve.tensor_tensor(m2[:, :, :], iota_b, bc(idf[:, :, 1:2], each), ALU.is_equal))
            chain.link(dve.tensor_tensor(g1[:, :, :], m1[:, :, :], bc(w[:, :, 0:1], each), ALU.mult))
            chain.link(dve.tensor_tensor(g2[:, :, :], m2[:, :, :], bc(w[:, :, 1:2], each), ALU.mult))
            chain.link(dve.tensor_tensor(g1[:, :, :], g1[:, :, :], g2[:, :, :], ALU.add))
            dve.tensor_tensor(m1[:, :, :], m1[:, :, :], m2[:, :, :], ALU.add).then_inc(mask_ready, 1)
            dve.wait_ge(mask_ready, 1)
            dve.wait_ge(rank_ready, 1)
            four = "p (b c e) -> p b c e"
            chain.link(dve.tensor_copy(rank[:, :, :, :], rp[:, 0:NCH * NE].rearrange(four, b=NB, c=SC)))
            chain.link(dve.tensor_copy(tot[:, :, :, :], rp[:, NCH * NE:].rearrange(four, b=NB, c=SC)))
            chain.link(dve.tensor_copy(cnt[:, :, :], tot[:, :, 0, :]))
            for c in range(1, SC):
                chain.link(dve.tensor_tensor(rank[:, :, c, :], rank[:, :, c, :], cnt[:, :, :], ALU.add))
                chain.link(dve.tensor_tensor(cnt[:, :, :], cnt[:, :, :], tot[:, :, c, :], ALU.add))
            chain.link(dve.tensor_scalar(pc[:, :, :], cnt[:, :, :], 0.0, float(P), ALU.is_gt, ALU.mult))
            for k in range(1, SC):
                chain.link(dve.tensor_scalar(tmp[:, :, :], cnt[:, :, :], float(P * k), float(P), ALU.is_gt, ALU.mult))
                chain.link(dve.tensor_tensor(pc[:, :, :], pc[:, :, :], tmp[:, :, :], ALU.add))
            chain.link(dve.memset(off[:, :, 0:1], 0.0))
            for e in range(1, NE):
                chain.link(dve.tensor_tensor(off[:, :, e:e + 1], off[:, :, e - 1:e], pc[:, :, e - 1:e], ALU.add))
            chain.link(dve.tensor_tensor(end[:, :, :], off[:, :, :], pc[:, :, :], ALU.add))
            for c in range(SC):
                chain.add(dve.tensor_tensor(rank[:, :, c, :], rank[:, :, c, :], off[:, :, :], ALU.add))
            chain.settle()
            rank_v = rank[:, :, :, :].rearrange("p b c e -> p (b c) e")
            chain.link(dve.tensor_scalar(rank_v, rank_v, 1.0, None, ALU.add))
            chain.link(dve.tensor_tensor(rank_v, rank_v, m1[:, :, :], ALU.mult))
            route_v = route[:, :, :].rearrange("p (b e) k -> p b e k", e=NE)
            g_v = g1[:, :, :].rearrange("p (b c) e -> p b c e", c=SC)
            for c in range(SC):
                chain.add(dve.tensor_scalar(route_v[:, :, :, c], rank[:, :, c, :], -1.0, None, ALU.add))
                chain.add(dve.tensor_copy(route_v[:, :, :, SC + c], g_v[:, :, c, :]))
            for b in range(NB):
                chain.add(dve.tensor_tensor(cmp[:, b, :, :], bc(end[:, b, :].unsqueeze(1), [P, NT, NE]),
                                            bc(tstart[:, :].unsqueeze(2), [P, NT, NE]), ALU.is_le))
            chain.settle()
            chain.link(dve.tensor_reduce(tx[:, 0, :], cmp[:, :, :, :].rearrange("p b t e -> p (b t) e"), AX.X, ALU.add))
            chain.link(dve.tensor_scalar(tx[:, 1, :], tx[:, 0, :], float(NE - 1), None, ALU.min))
            chain.link(dve.tensor_tensor(tx[:, 0, :], tx[:, 1, :], bstart[:, :], ALU.add))
            dve.tensor_copy(txi[:, :, :], tx[:, :, :]).then_inc(table_ready, 1)


def kv_phase(nc, d, xnT_dram, kst_dram, v_dram):
    with ExitStack() as ctx:
        sb, ps, sem = tools(nc, ctx, "kv")
        J = len(KPART)
        xT = [sb(f"xT{i}", [P, S]) for i in range(2)]
        w = sb("w", [P, NE, 2 * E + 1])
        vb = sb("vb", [1, NE, E])
        ones = sb("ones", [1, P])
        key = [sb(f"key{i}", [P, S]) for i in range(2)]
        rest = [sb(f"rest{i}", [P, S]) for i in range(2)]
        part = [sb(f"part{i}", [P, J, S], BF16) for i in range(2)]
        v = [sb(f"v{i}", [P, SC, NH, HD + 1]) for i in range(2)]
        kp = [ps(f"kp{i}", [P, S]) for i in range(2)]
        vp = [ps(f"vp{i}", [P, S]) for i in range(2)]
        ones_set, k_done, v_done, k_taken, v_taken, part0, rest_ready, part1, parts = (
            sem(n) for n in ("ones_set", "k_done", "v_done", "k_taken", "v_taken", "part0", "rest_ready", "part1", "parts"))
        loaded, stored, v_stored = ([sem(f"{n}{i}") for i in range(2)] for n in ("loaded", "stored", "v_stored"))
        w_loaded = sem("w_loaded")
        block = ctx.enter_context(nc.Block())
        STEPS = NB * NE
        LOOP = 2 * NE

        def steps(eng, body):
            for k in range(LOOP):
                body(k, k, 0)
            with eng.Fori(1, STEPS // LOOP) as i:
                for k in range(LOOP):
                    body(LOOP * i + k, k, i)

        def least(eng, s, value):
            if not isinstance(value, int) or value > 0:
                eng.wait_ge(s, value)

        @block.sync
        def _(sp):
            sp.dma_start(w[:, :, :], d["wkv"].rearrange("e p n -> p e n")).then_inc(w_loaded, 16)
            sp.dma_start(vb[:, :, :], d["vb"].rearrange("(o e) n -> o e n", o=1)).then_inc(w_loaded, 16)

            def load(b, u):
                sp.dma_start(xT[u][:, :], xnT_dram[:, bass.DynSlice(b * S, S)]).then_inc(loaded[u], 16)

            load(0, 0)
            load(1, 1)

            def body(n, k, i):
                u, j = k % 2, i * (LOOP // 2) + k // 2
                sp.wait_ge(parts, n + 1)
                for s in range(2):
                    row = KQ * s
                    sp.dma_start(kst_dram[bass.DynSlice(n, 1), row:row + KQ, :, :].rearrange("o (j d) p t -> (o d p) j t", d=HD),
                                 part[u][64 * s:64 * s + 64, :, :]).then_inc(stored[u], 16)

            def next_x(b, u):
                sp.wait_ge(v_taken, NE * (b - 1))
                load(b, u)

            for k in range(LOOP):
                body(k, k, 0)
                if k == LOOP - 1:
                    next_x(2, 0)
            with sp.Fori(1, STEPS // LOOP - 1) as i:
                for k in range(LOOP):
                    if k == 3:
                        next_x(2 * i + 1, 1)
                    body(LOOP * i + k, k, i)
                next_x(2 * i + 2, 0)
            i = STEPS // LOOP - 1
            for k in range(LOOP):
                if k == 3:
                    next_x(2 * i + 1, 1)
                body(LOOP * i + k, k, i)
            for u in range(2):
                sp.wait_ge(stored[u], 32 * STEPS // 2)

        @block.gpsimd
        def _(pool):
            for i in range(2):
                pool.memset(v[i][:, :, :, :], 1.0).then_inc(ones_set, 1)
            pool.memset(ones[:, :], 1.0).then_inc(ones_set, 1)

            def body(n, k, i):
                pool.wait_ge(v_taken, n + 1)
                pool.dma_start(v_dram[bass.DynSlice(n, 1), :, :, :, :].rearrange("o p c h d -> (o p) (c h d)"),
                               v[k % 2][:, :, :, :].rearrange("p c h d -> p (c h d)")).then_inc(v_stored[k % 2], 16)

            steps(pool, body)
            for u in range(2):
                pool.wait_ge(v_stored[u], 16 * STEPS // 2)

        @block.tensor
        def _(pe):
            pe.wait_ge(ones_set, 3)
            pe.wait_ge(w_loaded, 32)

            def body(n, k, i):
                u, e, x = k % 2, k % NE, xT[k // NE]
                pe.wait_ge(loaded[k // NE], 16 * i + 16)
                least(pe, k_taken, n - 1)
                pe.matmul(kp[u][:, :], w[:, e, 0:E], x[:, :], start=True, stop=True).then_inc(k_done, 1)
                least(pe, v_taken, n - 1)
                for c in range(SC):
                    o = vp[u][:, c * P:(c + 1) * P]
                    pe.matmul(o, x[:, c * P:(c + 1) * P], w[:, e, E:2 * E], start=True, stop=False)
                    last = pe.matmul(o, ones[:, :], vb[:, e, :], start=False, stop=True)
                last.then_inc(v_done, 1)

            steps(pe, body)

        @block.scalar
        def _(act):
            act.wait_ge(ones_set, 3)
            act.wait_ge(w_loaded, 32)

            def body(n, k, i):
                u, j = k % 2, i * (LOOP // 2) + k // 2
                act.wait_ge(k_done, n + 1)
                least(act, rest_ready, n - 1)
                act.activation(key[u][:, :], kp[u][:, :], ACT.Identity, bias=w[:, k % NE, 2 * E:2 * E + 1]).then_inc(k_taken, 1)
                act.wait_ge(v_done, n + 1)
                least(act, v_stored[u], 16 * j)
                act.activation(v[u][:, :, :, 0:HD], vp[u][:, :].rearrange("p (c h d) -> p c h d", c=SC, h=NH),
                               ACT.Copy).then_inc(v_taken, 1)

            steps(act, body)

        @block.vector
        def _(dve):
            def body(n, k, i):
                u, j = k % 2, i * (LOOP // 2) + k // 2
                dve.wait_ge(k_taken, n + 1)
                least(dve, stored[u], 32 * j)
                dve.tensor_copy(part[u][:, 0, :], key[u][:, :]).then_inc(part0, 1)
                dve.wait_ge(part0, n + 1)
                dve.tensor_tensor(rest[u][:, :], key[u][:, :], part[u][:, 0, :], ALU.subtract).then_inc(rest_ready, 1)
                dve.wait_ge(rest_ready, n + 1)
                dve.tensor_copy(part[u][:, 1, :], rest[u][:, :]).then_inc(part1, 1)
                dve.wait_ge(part1, n + 1)
                for to, at in enumerate(KPART[3:]):
                    if at < 2:
                        dve.tensor_copy(part[u][:, 3 + to, :], part[u][:, at, :])
                dve.tensor_copy(part[u][:, 2, :], part[u][:, KPART[2], :])
                dve.tensor_tensor(part[u][:, KPART.index(2), :], rest[u][:, :], part[u][:, 1, :], ALU.subtract).then_inc(parts, 1)

            steps(dve, body)


def experts_phase(nc, d, xn_dram, kst_dram, v_dram, route_dram, texp_dram, moe_dram):
    with ExitStack() as ctx:
        sb, ps, sem = tools(nc, ctx, "ex")
        M3 = 3 * NH
        SCALE = float(HD) ** -0.5
        Q_STACK = 16 * 2 * len(QPART)
        ks = [sb(f"ks{i}", [P, NH // 2, S], BF16) for i in range(3)]
        qs = [sb(f"qs{i}", [P, NH, P], BF16) for i in range(3)]
        v = [sb(f"v{i}", [P, SC, NH, HD + 1]) for i in range(2)]
        wo = [sb(f"wo{i}", [P, E]) for i in range(3)]
        ob = [sb(f"ob{i}", [1, E]) for i in range(3)]
        wq = [sb(f"wq{i}", [P, E + 1]) for i in range(2)]
        xn = [sb(f"xn{i}", [P, SC, E]) for i in range(2)]
        rt = [sb(f"rt{i}", [P, 2 * SC]) for i in range(2)]
        rel = sb("rel", [P, SC])
        hot = [sb(f"hot{i}", [P, SC, P]) for i in range(2)]
        gated = [sb(f"gated{i}", [P, SC, P]) for i in range(6)]
        xg = sb("xg", [P, P])
        q = sb("q", [P, P])
        qrest = sb("qrest", [P, P])
        qpart = sb("qpart", [P, len(QPART), P], BF16)
        nm = sb("nm", [P, NH])
        nmrest = sb("nmrest", [P, NH])
        mpart = sb("mpart", [P, P // NH, NH], BF16)
        mT = sb("mT", [M3, P], BF16)
        ex = sb("ex", [P, 8, S])
        oT = sb("oT", [P, 4 * P])
        rec = sb("rec", [P, 4, 4])
        on = sb("on", [P, NH, HD])
        onT = sb("onT", [P, P])
        os_ = sb("os", [P, E])
        spread = sb("spread", [P, SC * P])
        acc = [sb(f"acc{i}", [P, SC, E]) for i in range(2)]
        ident = sb("ident", [P, P])
        identb = sb("identb", [P, P], BF16)
        iota = sb("iota", [P, P])
        first_slot = sb("first_slot", [P, TILES])
        keep = sb("keep", [P, TILES])
        ones = sb("ones", [1, P])
        texp = sb("texp", [1, 2 * TILES], I32)
        SP_ = [ps(f"s{i}", [P, S]) for i in range(2)]
        ST_ = [ps(f"st{i}", [P, S]) for i in range(3)]
        O_ = ps("o", [P, 4 * P])
        A_ = ps("a", [P, 4 * P])
        B_ = ps("b", [P, 4 * P])
        names = ("consts cleared rel_ready rel_seen hot_ready gated_ready xg_done "
                 "xg_taken q_done q_taken q0 qr1 q1 q_parts q_stacked s_done max_taken nm0 nmr nm1 nm_parts mt_done mt_taken "
                 "m_stacked st_done exp_done pv_done o_taken tr_done rec_ready on_ready on_done onT_taken out_done "
                 "out_taken gt_done gt_taken sc_done acc_ready")
        sems = {n: sem(n) for n in names.split()}
        kv_loaded, wo_loaded = ([sem(f"{n}{i}") for i in range(3)] for n in ("kv_loaded", "wo_loaded"))
        v_loaded, in_loaded, acc_stored = ([sem(f"{n}{i}") for i in range(2)] for n in ("v_loaded", "in_loaded", "acc_stored"))
        block = ctx.enter_context(nc.Block())

        def least(eng, name, value):
            if not isinstance(value, int) or value > 0:
                eng.wait_ge(sems[name], value)

        now = {"i": 0}

        def uses(k, ring):
            return now["i"] * (6 // ring) + k // ring + 1

        def bodies(eng, body):
            now["i"] = 0
            for n in range(3):
                body(n, n)
            with eng.Fori(0, (TILES - 6) // 6) as i:
                now["i"] = i
                for k in range(3, 9):
                    body(6 * i + k, k, loop=True)
            now["i"] = 0
            for n in range(TILES - 3, TILES):
                body(n, n)

        @block.sync
        def _(sp):
            for dst, src in [(ident[:, :], d["identity"]), (iota[:, :], d["iota"]), (first_slot[:, :], d["first_slot"]),
                             (keep[:, :], d["keep"]), (texp[:, :], texp_dram[:, :])]:
                sp.dma_start(dst, src).then_inc(sems["consts"], 16)

            def value(n):
                return n if isinstance(n, int) else sp.snap(n)

            def wait(s, v):
                if not isinstance(v, int) or v > 0:
                    sp.wait_ge(s, v)

            def be_of(n):
                return sp.value_load(texp[0:1, bass.DynSlice(n, 1)], min_val=0, max_val=NB * NE - 1)

            def expert_of(be):
                return sp.snap(be % NE)

            def load_kv(n, k):
                be, scored = be_of(n), value(16 * (n - 2))
                wait(sems["st_done"], scored)
                sp.dma_start(ks[k % 3][0:2 * KQ, :, :].rearrange("p h t -> p (h t)"),
                             kst_dram[bass.DynSlice(be, 1), :, :, :].rearrange("o r p t -> (o r) (p t)"))\
                    .then_inc(kv_loaded[k % 3], 16)

            def load_v(n, k):
                be, multiplied, projected = be_of(n), value(4 * (n - 1)), value(n - 2)
                e = expert_of(be)
                wait(sems["pv_done"], multiplied)
                sp.dma_start(v[k % 2][:, :, :, :].rearrange("p c h d -> p (c h d)"),
                             v_dram[bass.DynSlice(be, 1), :, :, :, :].rearrange("o p c h d -> (o p) (c h d)"))\
                    .then_inc(v_loaded[k % 2], 16)
                wait(sems["out_done"], projected)
                sp.dma_start(wo[k % 3][:, :], d["wo"][bass.DynSlice(e, 1), :, :].rearrange("o p n -> (o p) n"))\
                    .then_inc(wo_loaded[k % 3], 16)
                sp.dma_start(ob[k % 3][:, :], d["ob"][bass.DynSlice(e, 1), :]).then_inc(wo_loaded[k % 3], 16)

            def load_in(n, k):
                i, be, before = k % 2, be_of(n), value(n - 1)
                e, b = expert_of(be), sp.snap(be // NE)
                wait(sems["q_taken"], before)
                sp.dma_start(xn[i][:, :, :], xn_dram[bass.DynSlice(b, 1), :, :].rearrange("o (c p) e -> p (o c) e", p=P))\
                    .then_inc(in_loaded[i], 16)
                sp.dma_start(wq[i][:, :], d["wq"][bass.DynSlice(e, 1), :, :].rearrange("o p n -> (o p) n"))\
                    .then_inc(in_loaded[i], 16)
                wait(sems["gated_ready"], before)
                sp.dma_start(rt[i][:, :], route_dram[:, bass.DynSlice(be, 1), :].rearrange("p o k -> p (o k)"))\
                    .then_inc(in_loaded[i], 16)

            def stack_q(n, k):
                sp.wait_ge(sems["q_parts"], n + 1)
                for s in range(2):
                    for j in range(len(QPART)):
                        row = KQ * s + HD * j
                        sp.dma_start(qs[k % 3][row:row + HD, s::2, :], qpart[64 * s:64 * s + 64, j, :])\
                            .then_inc(sems["q_stacked"], 16)

            def stack_m(n, k):
                sp.wait_ge(sems["mt_taken"], n + 1)
                sp.dma_start(qs[k % 3][2 * KQ:2 * KQ + 3, :, :], mT[:, :]).then_inc(sems["m_stacked"], 16)

            def store(n, k):
                tile, added = value(n), value(n + 1)
                sp.wait_ge(sems["acc_ready"], added)
                sp.dma_start(moe_dram[bass.DynSlice(tile, 1), :, :, :].rearrange("o p c e -> (o p) (c e)"),
                             acc[k % 2][:, :, :].rearrange("p c e -> p (c e)")).then_inc(acc_stored[k % 2], 16)

            def body(n, k, loop=False):
                if loop or n + 3 < TILES:
                    load_in(n + 3, k + 3)
                if loop or n + 1 < TILES:
                    load_v(n + 1, k + 1)
                if loop or n + 2 < TILES:
                    load_kv(n + 2, k + 2)
                    stack_q(n + 2, k + 2)
                if loop or n + 1 < TILES:
                    stack_m(n + 1, k + 1)
                if loop or n > 0:
                    store(n - 1, k - 1)

            sp.wait_ge(sems["consts"], 16 * 5)
            load_in(0, 0)
            load_in(1, 1)
            sp.wait_ge(sems["cleared"], 2)
            load_kv(0, 0)
            load_kv(1, 1)
            load_v(0, 0)
            stack_q(0, 0)
            load_in(2, 2)
            stack_q(1, 1)
            stack_m(0, 0)
            bodies(sp, body)
            store(TILES - 1, TILES - 1)
            for i in range(2):
                sp.wait_ge(acc_stored[i], 16 * TILES // 2)

        @block.gpsimd
        def _(pool):
            pool.memset(ones[:, :], 1.0).then_inc(sems["cleared"], 1)
            pool.wait_ge(sems["consts"], 16 * 5)

            def one_hot(n, k):
                pool.wait_ge(in_loaded[k % 2], 48 * uses(k, 2))
                least(pool, "gated_ready", n)
                least(pool, "xg_done", n - 1)
                least(pool, "gt_done", n - 4)
                pool.tensor_tensor(rel[:, :], rt[k % 2][:, 0:SC], bc(first_slot[:, bass.DynSlice(n, 1)], [P, SC]),
                                   ALU.subtract).then_inc(sems["rel_ready"], 1)
                pool.wait_ge(sems["rel_ready"], n + 1)
                pool.sem_inc(sems["rel_seen"], 1)
                for c in range(SC):
                    last = pool.tensor_scalar(hot[k % 2][:, c, :], iota[:, :], rel[:, c:c + 1], None, ALU.is_equal)
                last.then_inc(sems["hot_ready"], 1)
                for c in range(SC):
                    last = pool.tensor_scalar(gated[k % 6][:, c, :], iota[:, :], rel[:, c:c + 1],
                                              rt[k % 2][:, SC + c:SC + c + 1], ALU.is_equal, ALU.mult)
                last.then_inc(sems["gated_ready"], 1)

            def body(n, k, loop=False):
                if loop or n + 2 < TILES:
                    one_hot(n + 2, k + 2)

            one_hot(0, 0)
            one_hot(1, 1)
            bodies(pool, body)

        @block.tensor
        def _(pe):
            def gather(n, k):
                pe.wait_ge(sems["hot_ready"], n + 1)
                pe.wait_ge(in_loaded[k % 2], 48 * uses(k, 2))
                least(pe, "mt_taken", n - 1)
                least(pe, "q_taken", n)
                for c in range(SC):
                    last = pe.matmul(A_[:, 0:P], xn[k % 2][:, c, :], hot[k % 2][:, c, :], start=(c == 0), stop=(c == SC - 1))
                last.then_inc(sems["xg_done"], 1)

            def query(n, k):
                pe.wait_ge(sems["xg_taken"], n + 1)
                pe.matmul(A_[:, 0:P], wq[k % 2][:, 0:E], xg[:, :], start=True, stop=True).then_inc(sems["q_done"], 1)

            def max_T(n, k):
                pe.wait_ge(sems["nm_parts"], n + 1)
                least(pe, "q_taken", n + 2 if not isinstance(n, int) or n + 2 <= TILES else TILES)
                pe.transpose(A_[:, 0:P // 2].bitcast(BF16), mpart[:, :, :].rearrange("p i h -> p (i h)"), identb[:, :])\
                    .then_inc(sems["mt_done"], 1)

            def score(n, k, h):
                if h == 0:
                    pe.wait_ge(sems["q_stacked"], Q_STACK * (n + 1))
                    pe.wait_ge(kv_loaded[k % 3], 16 * uses(k, 3))
                least(pe, "max_taken", 16 * n + h - 1)
                pe.matmul(SP_[h % 2][:, :], qs[k % 3][0:2 * KQ, h, :], ks[k % 3][0:2 * KQ, h // 2, :],
                          start=True, stop=True).then_inc(sems["s_done"], 1)

            def score_T(n, k, u):
                if u == 0:
                    pe.wait_ge(sems["m_stacked"], 16 * (n + 1))
                least(pe, "exp_done", 16 * n + u - 2)
                bank = ST_[(k + u) % 3]
                for i in range(2):
                    c = 2 * (u % 2) + i
                    last = pe.matmul(bank[:, i * 2 * P:(i + 1) * 2 * P],
                                     ks[k % 3][0:2 * KQ + 3, u // 2, c * P:(c + 1) * P],
                                     qs[k % 3][0:2 * KQ + 3, u // 2 * 2:u // 2 * 2 + 2, :], start=True, stop=True)
                last.then_inc(sems["st_done"], 1)

            def values(n, k, g, c):
                if c == 0:
                    pe.wait_ge(sems["exp_done"], 16 * n + 4 * g + 4)
                    if g == 0:
                        pe.wait_ge(v_loaded[k % 2], 16 * uses(k, 2))
                        least(pe, "o_taken", n)
                for j in range(4):
                    unit = (4 * g + 2 * (j // 2) + c // 2) % 8
                    at = (c % 2) * 2 * P + (j % 2) * P
                    last = pe.matmul(O_[32 * j:32 * j + HD + 1, g * P:(g + 1) * P], v[k % 2][:, c, 4 * g + j, :],
                                     ex[:, unit, at:at + P], start=(c == 0), stop=(c == SC - 1), skip_group_check=True)
                if c == SC - 1:
                    last.then_inc(sems["pv_done"], 1)

            def turn_out(n, k):
                pe.wait_ge(sems["o_taken"], n + 1)
                least(pe, "gt_taken", n + 1)
                for g in range(4):
                    last = pe.transpose(B_[:, g * P:(g + 1) * P], oT[:, g * P:(g + 1) * P], ident[:, :])
                last.then_inc(sems["tr_done"], 1)

            def turn_norm(n, k):
                pe.wait_ge(sems["on_ready"], n + 1)
                pe.transpose(B_[:, 0:P], on[:, :, :].rearrange("p h d -> p (h d)"), ident[:, :]).then_inc(sems["on_done"], 1)

            def project(n, k):
                pe.wait_ge(sems["onT_taken"], n + 1)
                pe.wait_ge(wo_loaded[k % 3], 32 * uses(k, 3))
                pe.matmul(B_[:, 0:E], onT[:, :], wo[k % 3][:, :], start=True, stop=False)
                pe.matmul(B_[:, 0:E], ones[:, :], ob[k % 3][:, :], start=False, stop=True).then_inc(sems["out_done"], 1)

            def scatter(n, k):
                pe.wait_ge(sems["out_taken"], n + 1)
                pe.wait_ge(sems["gt_taken"], n + 1)
                for c in range(SC):
                    last = pe.matmul(B_[:, c * P:(c + 1) * P], spread[:, c * P:(c + 1) * P], os_[:, :], start=True, stop=True)
                last.then_inc(sems["sc_done"], 1)

            def turn_gated(n, k):
                pe.wait_ge(sems["gated_ready"], n + 1)
                least(pe, "acc_ready", n)
                for c in range(SC):
                    last = pe.transpose(B_[:, c * P:(c + 1) * P], gated[k % 6][:, c, :], ident[:, :])
                last.then_inc(sems["gt_done"], 1)

            def body(n, k, loop=False):
                more, later = loop or n + 1 < TILES, loop or n + 2 < TILES
                before = loop or n > 0
                for g in range(4):
                    for i in range(4):
                        u = 4 * g + i
                        score_T(n, k, u)
                        if more:
                            for h in range(min(NH, NH * u // 11), min(NH, NH * (u + 1) // 11)):
                                score(n + 1, k + 1, h)
                        if g:
                            values(n, k, g - 1, i)
                        if u == 1 and later:
                            gather(n + 2, k + 2)
                        if u == 3 and later:
                            query(n + 2, k + 2)
                        if u == 14 and more:
                            max_T(n + 1, k + 1)
                    if g == 0 and before:
                        turn_out(n - 1, k - 1)
                    if g == 1 and before:
                        turn_norm(n - 1, k - 1)
                    if g == 2 and before:
                        project(n - 1, k - 1)
                    if g == 3 and before:
                        scatter(n - 1, k - 1)
                for i in range(4):
                    values(n, k, 3, i)
                turn_gated(n, k)

            pe.wait_ge(sems["consts"], 16 * 5)
            pe.wait_ge(sems["cleared"], 2)
            gather(0, 0)
            query(0, 0)
            gather(1, 1)
            query(1, 1)
            for h in range(NH):
                score(0, 0, h)
            max_T(0, 0)
            bodies(pe, body)
            n, k = TILES - 1, TILES - 1
            turn_out(n, k)
            turn_norm(n, k)
            project(n, k)
            scatter(n, k)

        @block.scalar
        def _(act):
            def take_xg(n, k):
                act.wait_ge(sems["xg_done"], n + 1)
                least(act, "q_done", n)
                act.activation(xg[:, :], A_[:, 0:P], ACT.Copy).then_inc(sems["xg_taken"], 1)

            def take_max(n, k):
                act.wait_ge(sems["mt_done"], n + 1)
                least(act, "m_stacked", 16 * n)
                act.activation(mT[:, :], A_[0:M3, 0:P // 2].bitcast(BF16), ACT.Copy).then_inc(sems["mt_taken"], 1)

            def exps(n, k, u):
                act.wait_ge(sems["st_done"], 16 * n + u + 1)
                if u % 4 == 0:
                    least(act, "pv_done", 4 * n + u // 4 - 1)
                act.activation(ex[:, u % 8, :], ST_[(k + u) % 3][:, :], ACT.Exp).then_inc(sems["exp_done"], 1)

            def take_out(n, k):
                act.wait_ge(sems["pv_done"], 4 * n + 4)
                least(act, "tr_done", n)
                act.activation(oT[:, :], O_[:, :], ACT.Copy).then_inc(sems["o_taken"], 1)

            def take_norm(n, k):
                act.wait_ge(sems["on_done"], n + 1)
                least(act, "out_done", n)
                act.activation(onT[:, :], B_[:, 0:P], ACT.Copy).then_inc(sems["onT_taken"], 1)

            def take_proj(n, k):
                act.wait_ge(sems["out_done"], n + 1)
                least(act, "sc_done", n)
                act.activation(os_[:, :], B_[:, 0:E], ACT.Copy).then_inc(sems["out_taken"], 1)

            def take_gated(n, k):
                act.wait_ge(sems["gt_done"], n + 1)
                least(act, "sc_done", n)
                act.activation(spread[:, :], B_[:, :], ACT.Copy).then_inc(sems["gt_taken"], 1)

            def body(n, k, loop=False):
                more, later = loop or n + 1 < TILES, loop or n + 2 < TILES
                before = loop or n > 0
                for u in range(NH):
                    exps(n, k, u)
                    if u == 1 and before:
                        take_out(n - 1, k - 1)
                        take_gated(n - 1, k - 1)
                    if u == 2 and later:
                        take_xg(n + 2, k + 2)
                    if u == 9 and before:
                        take_norm(n - 1, k - 1)
                    if u == 13 and before:
                        take_proj(n - 1, k - 1)
                    if u == 14 and more:
                        take_max(n + 1, k + 1)

            take_xg(0, 0)
            take_xg(1, 1)
            take_max(0, 0)
            bodies(act, body)
            take_out(TILES - 1, TILES - 1)
            take_gated(TILES - 1, TILES - 1)
            take_norm(TILES - 1, TILES - 1)
            take_proj(TILES - 1, TILES - 1)

        @block.vector
        def _(dve):
            for i in range(3):
                dve.memset(qs[i][:, :, :], 0.0)
                dve.memset(ks[i][2 * KQ:P, :, :], 1.0)
            dve.memset(mpart[:, :, :], 0.0)
            dve.memset(acc[1][:, :, :], 0.0)
            dve.wait_ge(sems["consts"], 16 * 5)
            dve.tensor_copy(identb[:, :], ident[:, :])
            dve.memset(O_[:, :], 0.0).then_inc(sems["cleared"], 1)

            def parts_q(n, k):
                dve.wait_ge(sems["q_done"], n + 1)
                least(dve, "q_stacked", Q_STACK * n)
                dve.tensor_scalar(q[:, :], A_[:, 0:P], wq[k % 2][:, E:E + 1], SCALE, ALU.add, ALU.mult)\
                    .then_inc(sems["q_taken"], 1)
                dve.wait_ge(sems["q_taken"], n + 1)
                dve.tensor_copy(qpart[:, 0, :], q[:, :]).then_inc(sems["q0"], 1)
                dve.wait_ge(sems["q0"], n + 1)
                dve.tensor_tensor(qrest[:, :], q[:, :], qpart[:, 0, :], ALU.subtract).then_inc(sems["qr1"], 1)
                dve.wait_ge(sems["qr1"], n + 1)
                dve.tensor_copy(qpart[:, 2, :], qrest[:, :]).then_inc(sems["q1"], 1)
                least(dve, "st_done", 16 * (n - 2))
                dve.wait_ge(sems["q1"], n + 1)
                for to, at in ((1, 0), (3, 0), (4, 2)):
                    dve.tensor_copy(qpart[:, to, :], qpart[:, at, :])
                dve.tensor_tensor(qpart[:, 5, :], qrest[:, :], qpart[:, 2, :], ALU.subtract).then_inc(sems["q_parts"], 1)

            def row_max(n, k, h):
                dve.wait_ge(sems["s_done"], 16 * n + h + 1)
                dve.tensor_reduce(nm[:, h:h + 1], SP_[h % 2][:, :], AX.X, ALU.max, negate=True).then_inc(sems["max_taken"], 1)

            def parts_max(n, k):
                dve.wait_ge(sems["max_taken"], 16 * (n + 1))
                least(dve, "mt_done", n)
                dve.tensor_copy(mpart[:, 0, :], nm[:, :]).then_inc(sems["nm0"], 1)
                dve.wait_ge(sems["nm0"], n + 1)
                dve.tensor_tensor(nmrest[:, :], nm[:, :], mpart[:, 0, :], ALU.subtract).then_inc(sems["nmr"], 1)
                dve.wait_ge(sems["nmr"], n + 1)
                dve.tensor_copy(mpart[:, 1, :], nmrest[:, :]).then_inc(sems["nm1"], 1)
                dve.wait_ge(sems["nm1"], n + 1)
                dve.tensor_tensor(mpart[:, 2, :], nmrest[:, :], mpart[:, 1, :], ALU.subtract).then_inc(sems["nm_parts"], 1)

            def normalise(n, k):
                dve.wait_ge(sems["tr_done"], n + 1)
                least(dve, "on_done", n)
                tr = B_[:, :].rearrange("p (g j r) -> p g j r", g=4, j=4)
                dve.reciprocal(rec[:, :, :], tr[:, :, :, HD]).then_inc(sems["rec_ready"], 1)
                dve.wait_ge(sems["rec_ready"], n + 1)
                dve.tensor_tensor(on[:, :, :].rearrange("p (g j) d -> p g j d", j=4), tr[:, :, :, 0:HD],
                                  bc(rec[:, :, :].unsqueeze(3), [P, 4, 4, HD]), ALU.mult).then_inc(sems["on_ready"], 1)

            def add_out(n, k):
                dve.wait_ge(sems["sc_done"], n + 1)
                least(dve, "acc_ready", n)
                stored = 16 * (uses(k, 2) - 1)
                if not isinstance(stored, int) or stored > 0:
                    dve.wait_ge(acc_stored[k % 2], stored)
                dve.scalar_tensor_tensor(acc[k % 2][:, :, :].rearrange("p c e -> p (c e)"),
                                         acc[(k + 1) % 2][:, :, :].rearrange("p c e -> p (c e)"),
                                         keep[:, bass.DynSlice(n, 1)], B_[:, :], ALU.mult, ALU.add)\
                    .then_inc(sems["acc_ready"], 1)

            def body(n, k, loop=False):
                more, later = loop or n + 1 < TILES, loop or n + 2 < TILES
                before = loop or n > 0
                for h in range(NH):
                    if more:
                        row_max(n + 1, k + 1, h)
                    if h == 5 and before:
                        normalise(n - 1, k - 1)
                    if h == 7 and later:
                        parts_q(n + 2, k + 2)
                if more:
                    parts_max(n + 1, k + 1)
                if before:
                    add_out(n - 1, k - 1)

            parts_q(0, 0)
            parts_q(1, 1)
            for h in range(NH):
                row_max(0, 0, h)
            parts_max(0, 0)
            bodies(dve, body)
            normalise(TILES - 1, TILES - 1)
            add_out(TILES - 1, TILES - 1)


def mlstm_phase(nc, d, xnT_dram, ml_dram):
    with ExitStack() as ctx:
        sb, ps, sem = tools(nc, ctx, "ml")
        CH = INNER // P
        FROW = 32
        KS = 4
        xT = [sb(f"xT{i}", [P, S]) for i in range(2)]
        wup = sb("wup", [P, 2 * INNER])
        conv = sb("conv", [P, CH, KS + 1])
        bdq, bdk, bdv = (sb(n, [P, CH, P]) for n in ("bdq", "bdk", "bdv"))
        wg = sb("wg", [P, 3 * CH, FROW + MH])
        bg = sb("bg", [MH, 2])
        chan = sb("chan", [P, CH, 2])
        wdn = sb("wdn", [P, CH, E])
        sel = sb("sel", [MH, MH, P])
        tri = sb("tri", [P, P])
        ident = sb("ident", [P, P])
        xm = sb("xm", [P, CH, S + KS - 1])
        pre = sb("pre", [P, 2 * CH, S])
        sg = [sb(f"sg{i}", [P, 2 * CH, S]) for i in range(2)]
        qT, kT = ([sb(f"{n}{i}", [P, CH, S]) for i in range(2)] for n in ("qT", "kT"))
        vT = sb("vT", [P, CH, S])
        va = [sb(f"va{i}", [P, SC, MH, MD + 1]) for i in range(2)]
        ig, fg, nf, ef, lnf, lf, lc, a, cm, nM, lm, em = (
            sb(n, [MH, S]) for n in ("ig", "fg", "nf", "ef", "lnf", "lf", "lc", "a", "cm", "nM", "lm", "em"))
        ones = sb("ones", [MH, S])
        cols = [sb(f"cols{i}", [P, 2, SC, MH]) for i in range(2)]
        D = sb("D", [P, 2, SC, S])
        C = sb("C", [P, SC, S])
        nd = sb("nd", [P, SC])
        hh = sb("hh", [P, SC, MH, MD])
        stats = sb("stats", [P, SC * MH, 6])
        mv = sb("mv", [P, SC * MH, 2])
        ve = sb("ve", [P, SC * MH])
        half = sb("half", [P, SC * MH])
        rstd = sb("rstd", [P, SC * MH])
        sx = [sb(f"sx{i}", [P, CH, S]) for i in range(2)]
        hs = sb("hs", [P, CH, S])
        o = sb("o", [P, SC, E])
        bank = [ps(f"p{i}", [P, S]) for i in range(8)]
        UP, V_T, V, QK, GATES, COLS, FRONT = 0, 4, 6, 8, 12, 13, 14
        turned, down = (bank[5], bank[7]), bank[6]
        H = bank[5][:, 0:SC * (MD + 1)].rearrange("p (c e) -> p c e", c=SC)
        names = ("consts half_set front_done front_taken conv_done silu_done nf_ready ln_ready em_in em_ready em_seen "
                 "mb_done s_done d_ready d_exp c_ready h_done h_taken var_ready rstd_ready hn_ready hT_done hs_ready "
                 "o_done o_taken o_stored own stats_seen nm_ready chain")
        z = {n: sem(n) for n in names.split()}
        x_in = [sem(f"x_in{i}") for i in range(2)]
        block = ctx.enter_context(nc.Block())
        consts = [(wup[:, :], "w_up"), (conv[:, :, :], "conv"), (bdq[:, :, :], "bdq"), (bdk[:, :, :], "bdk"),
                  (bdv[:, :, :], "bdv"), (wg[:, :, :], "w_gates"), (bg[:, :], "b_gates"), (chan[:, :, :], "chan"),
                  (wdn[:, :, :], "w_down0"), (sel[:, :, :], "sel"), (tri[:, :], "tri"), (ident[:, :], "identity")]

        def batches(eng, front, step):
            front(0, 0, 0)
            with eng.Fori(0, NB // 2 - 1) as i:
                step(2 * i, 0, lambda part: front(2 * i + 1, 1, i, part), i)
                step(2 * i + 1, 1, lambda part: front(2 * i + 2, 0, i + 1, part), i)
            step(NB - 2, 0, lambda part: front(NB - 1, 1, NB // 2 - 1, part), NB // 2 - 1)
            step(NB - 1, 1, lambda part: None, NB // 2 - 1)

        @block.sync
        def _(sp):
            for dst, name in consts:
                sp.dma_start(dst, d[name]).then_inc(z["consts"], 16)

            def load(b, u):
                sp.dma_start(xT[u][:, :], xnT_dram[:, bass.DynSlice(b * S, S)]).then_inc(x_in[u], 16)

            def store(b):
                to = b if isinstance(b, int) else sp.snap(b)
                sp.wait_ge(z["o_taken"], b + 1)
                sp.dma_start(ml_dram[bass.DynSlice(to, 1), :, :].rearrange("o (c p) e -> p (o c) e", p=P),
                             o[:, :, :]).then_inc(z["o_stored"], 16)

            load(0, 0)
            load(1, 1)
            with sp.Fori(0, NB // 2 - 1) as i:
                for u in range(2):
                    b = sp.snap(2 * i + u)
                    at = sp.snap((b + 2) * S)
                    sp.wait_ge(z["front_done"], FRONT * b + V_T)
                    sp.dma_start(xT[u][:, :], xnT_dram[:, bass.DynSlice(at, S)]).then_inc(x_in[u], 16)
                    store(b)
            for u in range(2):
                store(NB - 2 + u)
            sp.wait_ge(z["o_stored"], 16 * NB + 16)

        @block.gpsimd
        def _(pool):
            pool.memset(half[:, :], -0.5).then_inc(z["half_set"], 1)
            pool.memset(ones[:, :], 1.0).then_inc(z["half_set"], 1)
            for i in range(2):
                pool.memset(va[i][:, :, :, :], 1.0).then_inc(z["half_set"], 1)
            pool.memset(xm[:, :, :], 0.0).then_inc(z["half_set"], 1)
            pool.wait_ge(z["half_set"], 5)
            with pool.Fori(0, NB) as b:
                pool.wait_ge(z["var_ready"], b + 1)
                pool.tensor_tensor(rstd[:, :], ve[:, :], half[:, :], ALU.pow).then_inc(z["rstd_ready"], 1)

        @block.tensor
        def _(pe):
            pe.wait_ge(z["consts"], 16 * len(consts))
            pe.wait_ge(z["half_set"], 5)

            def spread_max(b, u, h):
                if h or not isinstance(b, int) or b:
                    pe.wait_ge(z["d_ready"], 4 * (MH * b + h))
                pe.matmul(bank[0][:, :], sel[:, h, :], nM[:, :], start=True, stop=True).then_inc(z["mb_done"], 1)

            def scores(b, u, h):
                m, r = h // 2, MD * (h % 2)
                for t in range(SC):
                    if h or not isinstance(b, int) or b:
                        pe.wait_ge(z["c_ready"], 4 * (MH * b + h - 1) + t + 1)
                    pe.matmul(bank[1 + t][:, 0:S - t * P], kT[u][r:r + MD, m, t * P:(t + 1) * P],
                              qT[u][r:r + MD, m, t * P:], start=True, stop=True).then_inc(z["s_done"], 1)

            def front(b, u, uses, part=None):
                def free(j):
                    if j >= 2 or not isinstance(b, int) or b:
                        pe.wait_ge(z["front_taken"], FRONT * b + j - 1)
                    return bank[6 + j % 2]

                if part in (None, "up"):
                    pe.wait_ge(x_in[u], 16 * uses + 16)
                    for i in range(2 * CH):
                        pe.matmul(free(UP + i)[:, :], wup[:, i * P:(i + 1) * P], xT[u][:, :], start=True, stop=True)\
                            .then_inc(z["front_done"], 1)
                if part in (None, "v"):
                    for c in range(CH):
                        pe.matmul(free(V_T + c)[:, :], bdv[:, c, :], xm[:, c, KS - 1:], start=True, stop=True)\
                            .then_inc(z["front_done"], 1)
                    for i in range(2):
                        o_ = free(V + i)
                        for t in range(2 * i, 2 * i + 2):
                            for c in range(CH):
                                at = (t % 2) * INNER + c * P
                                last = pe.matmul(o_[:, at:at + P], xm[:, c, KS - 1 + t * P:KS - 1 + (t + 1) * P],
                                                 bdv[:, c, :], start=True, stop=True)
                        last.then_inc(z["front_done"], 1)
                if part in (None, "qk"):
                    pe.wait_ge(z["silu_done"], b + 1)
                    for c in range(CH):
                        for i, w in enumerate((bdq, bdk)):
                            pe.matmul(free(QK + 2 * c + i)[:, :], w[:, c, :], sg[u][:, c, :], start=True, stop=True)\
                                .then_inc(z["front_done"], 1)
                if part in (None, "gates"):
                    pe.wait_ge(z["front_taken"], FRONT * b + GATES)
                    src = [t[:, c, :] for t in (qT[u], kT[u], vT) for c in range(CH)]
                    for c in range(3 * CH):
                        last = pe.matmul(bank[6][0:FROW + MH, :], wg[:, c, :], src[c], start=(c == 0), stop=(c == 3 * CH - 1))
                    last.then_inc(z["front_done"], 1)
                if part in (None, "cols"):
                    pe.wait_ge(z["em_ready"], b + 1)
                    pe.sem_inc(z["em_seen"], 1)
                    for i, t in enumerate((a, em)):
                        for c in range(SC):
                            last = pe.transpose(bank[7][:, (i * SC + c) * MH:(i * SC + c + 1) * MH], t[:, c * P:(c + 1) * P],
                                                ident[0:MH, 0:MH])
                    last.then_inc(z["front_done"], 1)
                if part in (None, "head 0"):
                    pe.wait_ge(z["nm_ready"], b + 1)
                    spread_max(b, u, 0)
                    scores(b, u, 0)

            def step(b, u, next_front, i):
                def outputs(h):
                    if h:
                        pe.wait_ge(z["h_taken"], MH * b + h)
                    for s in range(SC):
                        for t in range(s + 1):
                            if s == SC - 1 or t == s:
                                pe.wait_ge(z["c_ready"], 4 * (MH * b + h) + t + 1)
                            last = pe.matmul(bank[5][:, s * (MD + 1):(s + 1) * (MD + 1)],
                                             C[:, t, (s - t) * P:(s - t + 1) * P], va[u][:, t, h, :],
                                             start=(t == 0), stop=(t == s))
                    last.then_inc(z["h_done"], 1)

                next_front("up")
                spread_max(b, u, 1)
                for h, parts in enumerate((("v",), ("qk", "gates"), ("cols",), ())):
                    outputs(h)
                    if h + 1 < MH:
                        scores(b, u, h + 1)
                    if h + 2 < MH:
                        spread_max(b, u, h + 2)
                    for part in parts:
                        next_front(part)
                next_front("head 0")
                pe.wait_ge(z["hn_ready"], b + 1)
                done = min(b + 2, NB) if isinstance(b, int) else b + 2
                pe.wait_ge(z["front_taken"], FRONT * done)
                for s in range(SC):
                    for c in range(CH):
                        last = pe.transpose(turned[c][:, s * P:(s + 1) * P],
                                            hh[:, s, 2 * c:2 * c + 2, :].rearrange("p h d -> p (h d)"), ident[:, :])
                last.then_inc(z["hT_done"], 1)
                pe.wait_ge(z["hs_ready"], b + 1)
                for s in range(SC):
                    for c in range(CH):
                        last = pe.matmul(down[:, s * P:(s + 1) * P], hs[:, c, s * P:(s + 1) * P], wdn[:, c, :],
                                         start=(c == 0), stop=(c == CH - 1))
                last.then_inc(z["o_done"], 1)
                pe.wait_ge(z["o_taken"], b + 1)

            batches(pe, front, step)

        @block.scalar
        def _(act):
            act.wait_ge(z["half_set"], 5)
            act.wait_ge(z["consts"], 16 * len(consts))
            act.sem_inc(z["o_stored"], 16)

            def front(b, u, uses, part=None):
                def take(j, dst, rows=P, source=lambda t: t):
                    act.wait_ge(z["front_done"], FRONT * b + j + 1)
                    act.activation(dst, source(bank[6 + j % 2][0:rows, :]), ACT.Copy).then_inc(z["front_taken"], 1)

                if part in (None, "up"):
                    for i in range(2 * CH):
                        take(UP + i, xm[:, i, KS - 1:] if i < CH else pre[:, i, :])
                if part in (None, "v"):
                    act.wait_ge(z["conv_done"], b + 1)
                    act.activation(sg[u][:, :, :], pre[:, :, :], ACT.Silu).then_inc(z["silu_done"], 1)
                    for c in range(CH):
                        take(V_T + c, vT[:, c, :])
                    for i in range(2):
                        take(V + i, va[u][:, 2 * i:2 * i + 2, :, 0:MD],
                             source=lambda t: t.rearrange("p (t h e) -> p t h e", t=2, h=MH))
                if part in (None, "qk"):
                    for c in range(CH):
                        take(QK + 2 * c, qT[u][:, c, :])
                        take(QK + 2 * c + 1, kT[u][:, c, :])
                if part in (None, "gates"):
                    act.wait_ge(z["front_done"], FRONT * b + GATES + 1)
                    act.activation(ig[:, :], bank[6][0:MH, :], ACT.Identity, bias=bg[:, 0:1])
                    act.activation(fg[:, :], bank[6][FROW:FROW + MH, :], ACT.Identity, bias=bg[:, 1:2])\
                        .then_inc(z["front_taken"], 1)
                    act.wait_ge(z["nf_ready"], b + 1)
                    act.activation(ef[:, :], nf[:, :], ACT.Exp).then_inc(z["own"], 1)
                    act.wait_ge(z["own"], b + 1)
                    act.activation(lnf[:, :], ef[:, :], ACT.Ln, bias=1.0).then_inc(z["ln_ready"], 1)
                if part in (None, "cols"):
                    act.wait_ge(z["em_in"], b + 1)
                    act.activation(em[:, :], lm[:, :], ACT.Exp, scale=-1.0).then_inc(z["em_ready"], 1)
                    take(COLS, cols[u][:, :, :, :],
                         source=lambda t: t[:, 0:2 * SC * MH].rearrange("p (i c h) -> p i c h", i=2, c=SC))

            def step(b, u, next_front, i):
                def exps(h):
                    for t in range(SC):
                        act.wait_ge(z["d_ready"], 4 * (MH * b + h) + t + 1)
                        act.activation(D[:, h % 2, t, 0:S - t * P], D[:, h % 2, t, 0:S - t * P], ACT.Exp).then_inc(z["d_exp"], 1)

                exps(0)
                next_front("up")
                exps(1)
                next_front("v")
                exps(2)
                next_front("qk")
                next_front("gates")
                exps(3)
                next_front("cols")
                act.wait_ge(z["o_done"], b + 1)
                act.wait_ge(z["o_stored"], 16 * b + 16)
                act.activation(o[:, :, :], down[:, :].rearrange("p (c e) -> p c e", c=SC), ACT.Copy).then_inc(z["o_taken"], 1)

            batches(act, front, step)

        @block.vector
        def _(dve):
            dve.wait_ge(z["consts"], 16 * len(consts))
            dve.wait_ge(z["half_set"], 5)
            chain = Chain(dve, z["chain"])
            IN_FRONT, IN_BACK = 15, 41

            def front(b, u, uses, part=None):
                if part in (None, "conv"):
                    dve.wait_ge(z["front_taken"], FRONT * b + CH)
                    for c in range(CH):
                        chain.add(dve.tensor_scalar(pre[:, c, :], xm[:, c, 0:S], conv[:, c, 0:1], conv[:, c, KS:KS + 1],
                                                    ALU.mult, ALU.add))
                    for k in range(1, KS):
                        chain.settle()
                        for c in range(CH):
                            chain.add(dve.scalar_tensor_tensor(pre[:, c, :], xm[:, c, k:k + S], conv[:, c, k:k + 1],
                                                               pre[:, c, :], ALU.mult, ALU.add))
                    chain.settle()
                    dve.wait_ge(z["front_taken"], FRONT * b + V_T)
                    dve.sem_inc(z["conv_done"], 1)
                if part in (None, "gates"):
                    dve.wait_ge(z["silu_done"], b + 1)
                    for c in range(CH):
                        chain.add(dve.tensor_scalar(sx[u][:, c, :], sg[u][:, c, :], chan[:, c, 1:2], None, ALU.mult))
                    dve.wait_ge(z["front_taken"], FRONT * b + GATES + 1)
                    dve.scalar_tensor_tensor(nf[:, :], fg[:, :], -1.0, fg[:, :], ALU.mult, ALU.min).then_inc(z["nf_ready"], 1)
                    chain.link(dve.tensor_scalar(lf[:, :], fg[:, :], 0.0, None, ALU.min))
                if part in (None, "scan"):
                    dve.wait_ge(z["ln_ready"], b + 1)
                    chain.link(dve.tensor_tensor(lf[:, :], lf[:, :], lnf[:, :], ALU.subtract))
                    chain.link(dve.tensor_tensor_scan(lc[:, :], ones[:, :], lf[:, :], 0.0, ALU.mult, ALU.add))
                    chain.link(dve.tensor_tensor(a[:, :], ig[:, :], lc[:, :], ALU.subtract))
                    chain.link(dve.tensor_tensor_scan(cm[:, :], a[:, :], a[:, :], -3.0e38, ALU.max, ALU.max))
                    dve.tensor_tensor(lm[:, :], lc[:, :], cm[:, :], ALU.add).then_inc(z["em_in"], 1)
                    dve.tensor_scalar(nM[:, :], cm[:, :], -1.0, None, ALU.mult).then_inc(z["nm_ready"], 1)

            def step(b, u, next_front, i):
                def decay(h):
                    dve.wait_ge(z["mb_done"], MH * b + h + 1)
                    if h == 0:
                        dve.wait_ge(z["front_taken"], FRONT * b + FRONT)
                    for t in range(SC):
                        dve.tensor_scalar(D[:, h % 2, t, 0:S - t * P], bank[0][:, t * P:], cols[u][:, 0, t, h:h + 1], 0.0,
                                          ALU.add, ALU.min).then_inc(z["d_ready"], 1)

                def weigh(h):
                    for t in range(SC):
                        n = 4 * (MH * b + h) + t + 1
                        dve.wait_ge(z["d_exp"], n)
                        dve.wait_ge(z["s_done"], n)
                        Dt = D[:, h % 2, t, :]
                        chain.link(dve.tensor_tensor(Dt[:, 0:P], Dt[:, 0:P], tri[:, :], ALU.mult))
                        dve.scalar_tensor_tensor(C[:, t, 0:S - t * P], bank[1 + t][:, 0:S - t * P], float(MD) ** -0.5,
                                                 Dt[:, 0:S - t * P], ALU.mult, ALU.mult).then_inc(z["c_ready"], 1)

                def divide(h):
                    dve.wait_ge(z["h_done"], MH * b + h + 1)
                    if h:
                        dve.wait_ge(z["h_taken"], MH * b + h)
                    chain.link(dve.tensor_scalar(nd[:, :], H[:, :, MD], -1.0, None, ALU.mult))
                    chain.link(dve.tensor_tensor(nd[:, :], nd[:, :], H[:, :, MD], ALU.max))
                    chain.link(dve.tensor_tensor(nd[:, :], nd[:, :], cols[u][:, 1, :, h], ALU.max))
                    chain.link(dve.tensor_scalar(nd[:, :], nd[:, :], 1e-6, None, ALU.add))
                    chain.link(dve.reciprocal(nd[:, :], nd[:, :]))
                    dve.tensor_tensor(hh[:, :, h, :], H[:, :, 0:MD], bc(nd[:, :].unsqueeze(2), [P, SC, MD]),
                                      ALU.mult).then_inc(z["h_taken"], 1)

                decay(0)
                decay(1)
                weigh(0)
                next_front("conv")
                decay(2)
                divide(0)
                weigh(1)
                decay(3)
                divide(1)
                weigh(2)
                next_front("gates")
                next_front("scan")
                divide(2)
                weigh(3)
                divide(3)
                dve.wait_ge(z["h_taken"], MH * b + MH)
                hv = hh[:, :, :, :].rearrange("p c h d -> p (c h) d")
                for k in range(SC * MH):
                    last = dve.bn_stats(stats[:, k, :], hv[:, k, :])
                chain.link(last)
                dve.sem_inc(z["stats_seen"], 1)
                for k in range(SC * MH):
                    last = dve.bn_aggr(mv[:, k, :], stats[:, k, :])
                chain.link(last)
                dve.tensor_scalar(ve[:, :], mv[:, :, 1], LN_EPS, None, ALU.add).then_inc(z["var_ready"], 1)
                wide = [P, SC * MH, MD]
                chain.link(dve.tensor_tensor(hv, hv, bc(mv[:, :, 0:1], wide), ALU.subtract))
                dve.wait_ge(z["rstd_ready"], b + 1)
                dve.tensor_tensor(hv, hv, bc(rstd[:, :].unsqueeze(2), wide), ALU.mult).then_inc(z["hn_ready"], 1)
                dve.wait_ge(z["hT_done"], b + 1)
                for c in range(CH):
                    chain.link(dve.scalar_tensor_tensor(sx[u][:, c, :], turned[c][:, :], chan[:, c, 0:1], sx[u][:, c, :],
                                                        ALU.mult, ALU.add))
                dve.tensor_tensor(hs[:, :, :], sx[u][:, :, :], sg[u][:, CH:, :], ALU.mult).then_inc(z["hs_ready"], 1)

            def counted(b, u, next_front, i):
                chain.base, chain.n = IN_FRONT + (IN_FRONT + IN_BACK) * b, 0
                step(b, u, next_front, i)
                assert chain.n == IN_BACK + (0 if isinstance(b, int) and b == NB - 1 else IN_FRONT), chain.n

            batches(dve, front, counted)


def cross_phase(nc, d, xnT_dram, at_dram):
    with ExitStack() as ctx:
        sb, ps, sem = tools(nc, ctx, "cr")
        R = 8
        AH = 16
        AD = E // AH
        xnT = sb("xnT", [P, NCH * P])
        dirT = sb("dirT", [P, 2, E])
        kwT = sb("kwT", [P, E])
        lowA = sb("lowA", [R, 2, E])
        lowB = sb("lowB", [R, 2, E])
        mag = sb("mag", [P, 2])
        bias = sb("bias", [1, 4 * E])
        owT = sb("owT", [P, E])
        ident = sb("ident", [P, P])
        ones = sb("ones", [P, P])
        root = sb("root", [P, 2])
        w = sb("w", [P, 3, E])
        sq = sb("sq", [P, 2, E])
        ss = sb("ss", [P, 2])
        tot = sb("tot", [P, 2])
        nrm = sb("nrm", [P, 2])
        qkv = [sb(f"qkv{i}", [P, NB, 3, E]) for i in range(2)]
        prod = sb("prod", [P, NB, E])
        prod2 = sb("prod2", [P, E, NB])
        sc = sb("sc", [P, NB, NB, AH])
        pr = sb("pr", [P, NB, NB, AH])
        mx = sb("mx", [P, NB, AH])
        att = [sb(f"att{i}", [P, NB, E]) for i in range(2)]
        attT = sb("attT", [P, NB, P])
        o = sb("o", [P, NB, E])
        qp = [ps(f"qp{i}", [P, S]) for i in range(2)]
        tp = [ps(f"tp{i}", [P, S]) for i in range(2)]
        op = [ps(f"op{i}", [P, S]) for i in range(2)]
        wp = ps("wp", [P, S])
        z = {n: sem(n) for n in ("consts ones_set low_done sq_ready tot_done tot_ready root_ready w_ready q_done "
                                 "q_taken att_ready turned turned_taken o_done o_taken stored s_ready p_exp "
                                 "own").split()}
        clear(nc)
        block = ctx.enter_context(nc.Block())
        consts = [(xnT[:, :], xnT_dram[:, :]), (dirT[:, :, :], d["dirT"]), (kwT[:, :], d["k_wT"]), (lowA[:, :, :], d["lowA"]),
                  (lowB[:, :, :], d["lowB"]), (mag[:, :], d["mag"].partition_broadcast(P)), (bias[:, :], d["bias1"]),
                  (owT[:, :], d["out_wT"]), (ident[:, :], d["identity"])]
        at_v = at_dram.rearrange("b (c p) e -> c p b e", p=P)

        @block.sync
        def _(sp):
            for dst, src in consts:
                sp.dma_start(dst, src).then_inc(z["consts"], 16)
            for c in range(SC):
                sp.wait_ge(z["o_taken"], 2 * c + 2)
                sp.dma_start(at_v[c], o[:, :, :]).then_inc(z["stored"], 16)
            sp.wait_ge(z["stored"], 16 * SC)

        @block.gpsimd
        def _(pool):
            pool.memset(ones[:, :], 1.0).then_inc(z["ones_set"], 1)
            pool.memset(root[:, :], 0.5).then_inc(z["ones_set"], 1)
            pool.wait_ge(z["ones_set"], 2)
            pool.wait_ge(z["tot_ready"], 1)
            pool.tensor_tensor(nrm[:, :], tot[:, :], root[:, :], ALU.pow).then_inc(z["root_ready"], 1)

        @block.tensor
        def _(pe):
            pe.wait_ge(z["consts"], 16 * len(consts))
            pe.wait_ge(z["ones_set"], 2)
            for i in range(2):
                last = pe.matmul(wp[:, i * E:(i + 1) * E], lowA[:, i, :], lowB[:, i, :], start=True, stop=True)
            last.then_inc(z["low_done"], 1)
            pe.wait_ge(z["sq_ready"], 1)
            pe.matmul(wp[:, 2 * E:2 * E + 2], ones[:, :], ss[:, :], start=True, stop=True).then_inc(z["tot_done"], 1)
            pe.wait_ge(z["w_ready"], 3)
            for c in range(SC + 1):
                if c < SC:
                    for b in range(NB):
                        n = c * NB + b
                        if n >= 2:
                            pe.wait_ge(z["q_taken"], n - 1)
                        at = (b * SC + c) * P
                        pe.matmul(qp[n % 2][:, 0:3 * E], xnT[:, at:at + P], w[:, :, :].rearrange("p i e -> p (i e)"),
                                  start=True, stop=False)
                        pe.matmul(qp[n % 2][:, 0:3 * E], ones[0:1, :], bias[:, 0:3 * E], start=False, stop=True)\
                            .then_inc(z["q_done"], 1)
                if c:
                    m = c - 1
                    pe.wait_ge(z["att_ready"], m + 1)
                    for g in range(2):
                        if m:
                            pe.wait_ge(z["turned_taken"], 2 * m - 1 + g)
                        for b in range(4):
                            last = pe.transpose(tp[g][:, b * P:(b + 1) * P], att[m % 2][:, 4 * g + b, :], ident[:, :])
                        last.then_inc(z["turned"], 1)
                    for g in range(2):
                        pe.wait_ge(z["turned_taken"], 2 * m + g + 1)
                        if m:
                            pe.wait_ge(z["o_taken"], 2 * m - 1 + g)
                        for b in range(4):
                            pe.matmul(op[g][:, b * P:(b + 1) * P], attT[:, 4 * g + b, :], owT[:, :], start=True, stop=False)
                            last = pe.matmul(op[g][:, b * P:(b + 1) * P], ones[0:1, :], bias[:, 3 * E:], start=False, stop=True)
                        last.then_inc(z["o_done"], 1)

        @block.scalar
        def _(act):
            for c in range(SC + 2):
                if c < SC:
                    if c >= 2:
                        act.wait_ge(z["att_ready"], c - 1)
                    for b in range(NB):
                        act.wait_ge(z["q_done"], c * NB + b + 1)
                        act.activation(qkv[c % 2][:, b, :, :].rearrange("p i e -> p (i e)"), qp[b % 2][:, 0:3 * E],
                                       ACT.Copy).then_inc(z["q_taken"], 1)
                if 1 <= c <= SC:
                    act.wait_ge(z["s_ready"], c)
                    act.activation(pr[:, :, :, :], sc[:, :, :, :], ACT.Exp, scale=float(AD) ** -0.5).then_inc(z["p_exp"], 1)
                    m = c - 1
                    for g in range(2):
                        act.wait_ge(z["turned"], 2 * m + g + 1)
                        if m:
                            act.wait_ge(z["o_done"], 2 * m)
                        act.activation(attT[:, 4 * g:4 * g + 4, :], tp[g][:, :].rearrange("p (b s) -> p b s", b=4),
                                       ACT.Copy).then_inc(z["turned_taken"], 1)
                    for g in range(2):
                        act.wait_ge(z["o_done"], 2 * m + g + 1)
                        if m:
                            act.wait_ge(z["stored"], 16 * m)
                        act.activation(o[:, 4 * g:4 * g + 4, :], op[g][:, :].rearrange("p (b s) -> p b s", b=4),
                                       ACT.Copy).then_inc(z["o_taken"], 1)

        @block.vector
        def _(dve):
            chain = Chain(dve, z["own"])
            dve.wait_ge(z["consts"], 16 * len(consts))
            dve.wait_ge(z["ones_set"], 2)
            dve.wait_ge(z["low_done"], 1)
            low = wp[:, 0:2 * E].rearrange("p (i e) -> p i e", i=2)
            chain.link(dve.tensor_tensor(dirT[:, :, :], low, dirT[:, :, :], ALU.add))
            chain.link(dve.tensor_tensor(sq[:, :, :], dirT[:, :, :], dirT[:, :, :], ALU.mult))
            dve.tensor_reduce(ss[:, :], sq[:, :, :], AX.X, ALU.add).then_inc(z["sq_ready"], 1)
            dve.wait_ge(z["tot_done"], 1)
            dve.tensor_copy(tot[:, :], wp[:, 2 * E:2 * E + 2]).then_inc(z["tot_ready"], 1)
            dve.wait_ge(z["root_ready"], 1)
            chain.link(dve.tensor_scalar(nrm[:, :], nrm[:, :], 1e-8, None, ALU.add))
            chain.link(dve.reciprocal(nrm[:, :], nrm[:, :]))
            chain.link(dve.tensor_tensor(nrm[:, :], nrm[:, :], mag[:, :], ALU.mult))
            for i, at in ((0, 0), (1, 2)):
                dve.tensor_scalar(w[:, at, :], dirT[:, i, :], nrm[:, i:i + 1], None, ALU.mult).then_inc(z["w_ready"], 1)
            dve.tensor_copy(w[:, 1, :], kwT[:, :]).then_inc(z["w_ready"], 1)
            for c in range(SC):
                t = qkv[c % 2]
                dve.wait_ge(z["q_taken"], NB * (c + 1))
                for b in range(NB):
                    chain.link(dve.tensor_tensor(prod[:, :, :], t[:, :, 1, :], bc(t[:, b, 0, :].unsqueeze(1), [P, NB, E]), ALU.mult))
                    chain.link(dve.tensor_reduce(sc[:, b, :, :], prod[:, :, :].rearrange("p k (h e) -> p k h e", h=AH),
                                                 AX.X, ALU.add))
                chain.link(dve.tensor_reduce(mx[:, :, :], sc[:, :, :, :].rearrange("p q k h -> p q h k"), AX.X, ALU.max))
                for b in range(NB):
                    last = dve.tensor_tensor(sc[:, b, :, :], sc[:, b, :, :], bc(mx[:, b, :].unsqueeze(1), [P, NB, AH]),
                                             ALU.subtract)
                last.then_inc(z["s_ready"], 1)
                dve.wait_ge(z["p_exp"], c + 1)
                chain.link(dve.tensor_reduce(mx[:, :, :], pr[:, :, :, :].rearrange("p q k h -> p q h k"), AX.X, ALU.add))
                chain.link(dve.reciprocal(mx[:, :, :], mx[:, :, :]))
                if c >= 2:
                    dve.wait_ge(z["turned"], 2 * (c - 1))
                for b in range(NB):
                    chain.link(dve.tensor_tensor(prod2[:, :, :].rearrange("p (h e) k -> p h e k", h=AH),
                                                 bc(pr[:, b, :, :].rearrange("p k h -> p h k").unsqueeze(2), [P, AH, AD, NB]),
                                                 t[:, :, 2, :].rearrange("p k (h e) -> p h e k", h=AH), ALU.mult))
                    chain.link(dve.tensor_reduce(att[c % 2][:, b, :], prod2[:, :, :], AX.X, ALU.add))
                av = att[c % 2][:, :, :].rearrange("p b (h e) -> p (b h) e", h=AH)
                dve.tensor_tensor(av, av, bc(mx[:, :, :].rearrange("p b h -> p (b h)").unsqueeze(2), [P, NB * AH, AD]),
                                  ALU.mult).then_inc(z["att_ready"], 1)


def fp4(chain, act_abs, x, blocks, scale, inv, mag, big, small):
    dve = chain.eng
    shape = [P, blocks, QB]
    chain.link(dve.tensor_reduce(scale, x, AX.X, ALU.max, apply_absolute_value=True))
    chain.link(dve.tensor_scalar(scale, scale, 1.0 / 6.0, 1e-12, ALU.mult, ALU.max))
    chain.link(dve.reciprocal(inv, scale))
    act_abs(chain, dve.tensor_tensor(x, x, bc(inv.unsqueeze(2), shape), ALU.mult))
    chain.add(dve.tensor_scalar(inv, scale, 0.5, None, ALU.mult))
    chain.add(dve.tensor_scalar(big, mag, 5.0, 2.0, ALU.is_gt, ALU.mult))
    chain.link(dve.tensor_scalar(small, mag, 0.25, None, ALU.is_gt))
    chain.add(dve.scalar_tensor_tensor(big, mag, 2.5, big, ALU.is_gt, ALU.add))
    chain.link(dve.scalar_tensor_tensor(small, mag, 0.75, small, ALU.is_gt, ALU.add))
    chain.add(dve.scalar_tensor_tensor(big, mag, 3.5, big, ALU.is_gt, ALU.add))
    chain.link(dve.scalar_tensor_tensor(small, mag, 1.25, small, ALU.is_gt, ALU.add))
    chain.link(dve.scalar_tensor_tensor(small, mag, 1.75, small, ALU.is_gt, ALU.add))
    chain.link(dve.scalar_tensor_tensor(mag, big, 2.0, small, ALU.mult, ALU.add))
    chain.link(dve.tensor_tensor(mag, mag, bc(inv.unsqueeze(2), shape), ALU.mult))
    return dve.scalar_tensor_tensor(x.bitcast(U32), x.bitcast(U32), 0x80000000, mag.bitcast(U32),
                                    ALU.bitwise_and, ALU.bitwise_or)


def ffn_phase(nc, d, xn_dram, base_dram, at_dram, out_dram):
    with ExitStack() as ctx:
        sb, ps, sem = tools(nc, ctx, "ff")
        FB = FF // QB
        FK = 3
        WIDTH = [P, P, FF - 2 * P]
        STEPS = NCH // 2
        wgu = sb("wgu", [P, 2 * FK, E])
        wdn = sb("wdn", [P, FF])
        wguT = sb("wguT", [P, 2, FK * P])
        wdT = sb("wdT", [P, FK, E])
        ident = sb("ident", [P, P])
        x = [sb(f"x{i}", [P, 2, E]) for i in range(2)]
        base = [sb(f"base{i}", [P, 2, E]) for i in range(2)]
        at = [sb(f"at{i}", [P, 2, E]) for i in range(2)]
        xqT = sb("xqT", [P, 2, P])
        g = sb("g", [P, 2, FF])
        h = sb("h", [P, 2, FF])
        hT = sb("hT", [P, 2, FK, P])
        NBIG = 2 * FK * E
        mag = sb("mag", [P, NBIG])
        big = sb("big", [P, NBIG])
        small = sb("small", [P, NBIG])
        scale = sb("scale", [P, NBIG // QB])
        inv = sb("inv", [P, NBIG // QB])
        o = [sb(f"o{i}", [P, 2, E]) for i in range(2)]
        gp = [ps(f"gp{i}", [P, S]) for i in range(2)]
        up = [ps(f"up{i}", [P, S]) for i in range(2)]
        tx = ps("tx", [P, S])
        th = [ps(f"th{i}", [P, S]) for i in range(2)]
        op = ps("op", [P, S])
        z = {n: sem(n) for n in ("consts w_ready w_turned w_taken scaled absed xq_ready xq_done xq_taken gu_done "
                                 "g_ready h_open hq_ready h_done h_taken o_done o_added own").split()}
        loaded, stored = ([sem(f"{n}{i}") for i in range(2)] for n in ("loaded", "stored"))
        clear(nc)
        block = ctx.enter_context(nc.Block())
        pair = lambda t, n: t.rearrange("b (k c p) e -> (b k) p c e", p=P, c=2)[bass.DynSlice(n, 1)].rearrange("o p c e -> (o p) c e")

        def steps(eng, body):
            for u in range(2):
                body(u, u, 0)
            with eng.Fori(1, STEPS // 2) as i:
                for u in range(2):
                    body(2 * i + u, u, i)

        @block.sync
        def _(sp):
            for dst, name in ((wgu[:, :, :], "w_gu"), (wdn[:, :], "w_down1"), (ident[:, :], "identity")):
                sp.dma_start(dst, d[name]).then_inc(z["consts"], 16)

            def load(n, u):
                for dst, src in ((x, xn_dram), (base, base_dram), (at, at_dram)):
                    sp.dma_start(dst[u][:, :, :], pair(src, n)).then_inc(loaded[u], 16)

            load(0, 0)
            load(1, 1)

            def body(n, u, i):
                sp.wait_ge(z["o_added"], n + 1)
                sp.dma_start(pair(out_dram, n), o[u][:, :, :]).then_inc(stored[u], 16)
                if isinstance(n, int) and n < 2:
                    load(n + 2, u)

            for u in range(2):
                body(u, u, 0)
            with sp.Fori(1, STEPS // 2 - 1) as i:
                for u in range(2):
                    n = 2 * i + u
                    sp.wait_ge(z["o_added"], n + 1)
                    sp.dma_start(pair(out_dram, n), o[u][:, :, :]).then_inc(stored[u], 16)
                    load(n + 2, u)
            for u in range(2):
                body(STEPS - 2 + u, u, 0)
            for u in range(2):
                sp.wait_ge(stored[u], 16 * STEPS // 2)

        @block.tensor
        def _(pe):
            pe.wait_ge(z["consts"], 48)
            pe.wait_ge(z["w_ready"], 2)
            for i in range(2):
                for k in range(FK):
                    last = pe.transpose(gp[i][:, k * P:(k + 1) * P], wgu[:, FK * i + k, :], ident[:, :])
            for k in range(FK):
                last = pe.transpose(up[0][0:WIDTH[k], k * P:(k + 1) * P], wdn[:, k * P:k * P + WIDTH[k]], ident[:, :])
            last.then_inc(z["w_turned"], 1)
            pe.wait_ge(z["w_taken"], 1)

            def gate_up(n, u, i):
                pe.wait_ge(z["xq_ready"], n + 1)
                for c in range(2):
                    last = pe.transpose(tx[:, c * P:(c + 1) * P], x[u][:, c, :], ident[:, :])
                last.then_inc(z["xq_done"], 1)
                pe.wait_ge(z["xq_taken"], n + 1)
                if not isinstance(n, int) or n:
                    pe.wait_ge(z["h_open"], n)
                for c in range(2):
                    pe.matmul(gp[c][:, 0:FF], xqT[:, c, :], wguT[:, 0, 0:FF], start=True, stop=True)
                    last = pe.matmul(up[c][:, 0:FF], xqT[:, c, :], wguT[:, 1, 0:FF], start=True, stop=True)
                last.then_inc(z["gu_done"], 1)

            def down(n, u, i):
                pe.wait_ge(z["hq_ready"], n + 1)
                for c in range(2):
                    for k in range(FK):
                        last = pe.transpose(th[c][0:WIDTH[k], k * P:(k + 1) * P], h[:, c, k * P:k * P + WIDTH[k]], ident[:, :])
                last.then_inc(z["h_done"], 1)
                pe.wait_ge(z["h_taken"], n + 1)
                if not isinstance(n, int) or n:
                    pe.wait_ge(z["o_added"], n)
                for c in range(2):
                    for k in range(FK):
                        last = pe.matmul(op[:, c * P:(c + 1) * P], hT[0:WIDTH[k], c, k, :], wdT[0:WIDTH[k], k, :],
                                         start=(k == 0), stop=(k == FK - 1))
                last.then_inc(z["o_done"], 1)

            gate_up(0, 0, 0)
            for n in range(2):
                gate_up(n + 1, (n + 1) % 2, 0)
                down(n, n, 0)
            with pe.Fori(1, STEPS // 2 - 1) as i:
                for u in range(2):
                    gate_up(2 * i + u + 1, (u + 1) % 2, i)
                    down(2 * i + u, u, i)
            gate_up(STEPS - 1, 1, 0)
            down(STEPS - 2, 0, 0)
            down(STEPS - 1, 1, 0)

        @block.scalar
        def _(act):
            act.wait_ge(z["w_turned"], 1)
            for i in range(2):
                act.activation(wguT[:, i, :], gp[i][:, 0:FK * P], ACT.Copy)
            for k in range(FK):
                last = act.activation(wdT[0:WIDTH[k], k, :], up[0][0:WIDTH[k], k * P:(k + 1) * P], ACT.Copy)
            last.then_inc(z["w_taken"], 1)

            def early(n, u, i):
                act.wait_ge(z["xq_done"], n + 1)
                if not isinstance(n, int) or n:
                    act.wait_ge(z["gu_done"], n)
                act.activation(xqT[:, :, :], tx[:, 0:2 * P].rearrange("p (c t) -> p c t", c=2), ACT.Copy)\
                    .then_inc(z["xq_taken"], 1)
                act.wait_ge(z["gu_done"], n + 1)
                if not isinstance(n, int) or n:
                    act.wait_ge(z["h_open"], n)
                for c in range(2):
                    last = act.activation(g[:, c, :], gp[c][:, 0:FF], ACT.Silu)
                last.then_inc(z["g_ready"], 1)

            def late(n, u, i):
                act.wait_ge(z["h_done"], n + 1)
                if not isinstance(n, int) or n:
                    act.wait_ge(z["o_done"], n)
                for c in range(2):
                    for k in range(FK):
                        last = act.activation(hT[0:WIDTH[k], c, k, :], th[c][0:WIDTH[k], k * P:(k + 1) * P], ACT.Copy)
                last.then_inc(z["h_taken"], 1)

            early(0, 0, 0)
            for n in range(2):
                early(n + 1, (n + 1) % 2, 0)
                late(n, n, 0)
            with act.Fori(1, STEPS // 2 - 1) as i:
                for u in range(2):
                    early(2 * i + u + 1, (u + 1) % 2, i)
                    late(2 * i + u, u, i)
            early(STEPS - 1, 1, 0)
            late(STEPS - 2, 0, 0)
            late(STEPS - 1, 1, 0)

        @block.vector
        def _(dve):
            chain = Chain(dve, z["own"])

            def quant(x3, blocks):
                v = lambda t: t[:, 0:blocks * QB].rearrange("p (b q) -> p b q", q=QB)

                def magnitude(ch, ins):
                    ch.link(ins)
                    ch.link(dve.scalar_tensor_tensor(v(mag), x3, -1.0, x3, ALU.mult, ALU.max))
                return fp4(chain, magnitude, x3, blocks, scale[:, 0:blocks], inv[:, 0:blocks], v(mag), v(big), v(small))

            dve.wait_ge(z["consts"], 48)
            quant(wgu[:, :, :].rearrange("p k (b q) -> p (k b) q", q=QB), NBIG // QB).then_inc(z["w_ready"], 1)
            dve.wait_ge(z["w_ready"], 1)
            quant(wdn[:, :].rearrange("p (b q) -> p b q", q=QB), FB).then_inc(z["w_ready"], 1)
            dve.wait_ge(z["w_ready"], 2)

            def early(n, u, i):
                dve.wait_ge(loaded[u], 48 * i + 48)
                quant(x[u][:, :, :].rearrange("p c (b q) -> p (c b) q", q=QB), 2 * E // QB).then_inc(z["xq_ready"], 1)

            def late(n, u, i):
                dve.wait_ge(z["g_ready"], n + 1)
                if not isinstance(n, int) or n:
                    dve.wait_ge(z["h_done"], n)
                for c in range(2):
                    last = dve.tensor_tensor(h[:, c, :], up[c][:, 0:FF], g[:, c, :], ALU.mult)
                last.then_inc(z["h_open"], 1)
                dve.wait_ge(z["h_open"], n + 1)
                quant(h[:, :, :].rearrange("p c (b q) -> p (c b) q", q=QB), 2 * FB).then_inc(z["hq_ready"], 1)
                chain.link(dve.tensor_tensor(base[u][:, :, :], base[u][:, :, :], at[u][:, :, :], ALU.add))
                dve.wait_ge(z["o_done"], n + 1)
                if not isinstance(i, int) or i:
                    dve.wait_ge(stored[u], 16 * i)
                dve.tensor_tensor(o[u][:, :, :], op[:, 0:2 * P].rearrange("p (c e) -> p c e", c=2), base[u][:, :, :],
                                  ALU.add).then_inc(z["o_added"], 1)

            def body(n, u, i, more=True):
                if more:
                    early(n + 1, (u + 1) % 2, i + u)
                late(n, u, i)

            early(0, 0, 0)
            first = chain.n
            for n in range(2):
                body(n, n, 0)
            per = chain.n - first
            with dve.Fori(1, STEPS // 2 - 1) as i:
                chain.base, chain.n = i * per + first, 0
                for u in range(2):
                    body(2 * i + u, u, i)
                assert chain.n == per
            chain.base, chain.n = first + per * (STEPS // 2 - 1), 0
            body(STEPS - 2, 0, STEPS // 2 - 1)
            body(STEPS - 1, 1, STEPS // 2 - 1, more=False)


def layout_mlstm(g, o):
    import numpy as np

    f = np.float32
    CH = INNER // P
    o["w_up"] = g["L0_attn_w_up"].T
    o["conv"] = np.concatenate([g["L0_attn_conv_w"][:, 0, :], g["L0_attn_conv_b"][:, None]], 1).reshape(CH, P, 5).transpose(1, 0, 2)
    for n in "qkv":
        w = g[f"L0_attn_w_{n}"]
        blk = w.shape[1]
        full = np.zeros((P, CH, P), f)
        for j in range(w.shape[0]):
            c, r = divmod(j * blk, P)
            full[r:r + blk, c, r:r + blk] = w[j].T
        o["bd" + n] = full
    gates = np.stack([g["L0_attn_w_ig"], g["L0_attn_w_fg"]])
    gates = gates.reshape(2, MH, 3 * CH, P).transpose(3, 2, 0, 1)
    gap = np.zeros((P, 3 * CH, 32 - MH), f)
    o["w_gates"] = np.concatenate([gates[:, :, 0], gap, gates[:, :, 1]], 2)
    o["b_gates"] = np.stack([g["L0_attn_b_ig"], g["L0_attn_b_fg"]], 1)
    o["chan"] = np.stack([g["L0_attn_ln_w"].reshape(-1), g["L0_attn_skip"]], 1).reshape(CH, P, 2).transpose(1, 0, 2)
    o["w_down0"] = g["L0_attn_w_down"].T.reshape(CH, P, E).transpose(1, 0, 2)
    sel = np.zeros((MH, MH, P), f)
    for h in range(MH):
        sel[h, h] = 1
    o["sel"] = sel
    o["tri"] = np.triu(np.ones((P, P), f))


def layout_layer1(g, o):
    import numpy as np

    f = np.float32
    o["dirT"] = np.stack([g["L1_attn_dir_q"].T, g["L1_attn_dir_v"].T], 1)
    o["k_wT"] = g["L1_attn_k_w"].T
    o["lowA"] = np.stack([g["L1_attn_A_q"], g["L1_attn_A_v"]], 1)
    o["lowB"] = np.stack([g["L1_attn_B_q"].T, g["L1_attn_B_v"].T], 1)
    o["mag"] = np.stack([g["L1_attn_mag_q"].reshape(()), g["L1_attn_mag_v"].reshape(())])
    o["bias1"] = np.concatenate([g[f"L1_attn_{n}"] for n in ("bias_q", "k_b", "bias_v", "out_b")])[None]
    o["out_wT"] = g["L1_attn_out_w"].T
    wgu = np.zeros((2, 3 * P, E), f)
    wgu[0, :FF] = g["L1_ffn_w_gate"]
    wgu[1, :FF] = g["L1_ffn_w_up"]
    o["w_gu"] = wgu.reshape(6, P, E).transpose(1, 0, 2)
    o["w_down1"] = g["L1_ffn_w_down"]


def layout(inp):
    import numpy as np

    f = np.float32
    g = {n: np.ascontiguousarray(np.asarray(a)) for n, a in inp.items()}
    perm = np.array([(2 * p + s) * HD + dd for s in range(2) for dd in range(HD) for p in range(NH // 2)])
    o = {"x": g["L0_attn_x"]}
    o["rW1T"] = g["L0_ffn_rW1"].T
    o["rb1"] = g["L0_ffn_rb1"][None]
    o["rW2T"] = g["L0_ffn_rW2"].T
    o["rb2"] = g["L0_ffn_rb2"][None]
    o["ln_g"] = g["L0_ffn_ln_g"]
    o["ln_b"] = g["L0_ffn_ln_b"]
    kT = g["L0_ffn_kW"].transpose(0, 2, 1)[:, :, perm]
    o["wkv"] = np.concatenate([kT, g["L0_ffn_vW"].transpose(0, 2, 1), g["L0_ffn_kb"][:, perm, None]], 2)
    o["vb"] = g["L0_ffn_vb"]
    o["wq"] = np.concatenate([g["L0_ffn_qW"].transpose(0, 2, 1)[:, :, perm], g["L0_ffn_qb"][:, perm, None]], 2)
    o["wo"] = g["L0_ffn_oW"].transpose(0, 2, 1)
    o["ob"] = g["L0_ffn_ob"]
    o["identity"] = np.eye(P, dtype=f)
    o["lower"] = np.triu(np.ones((P, P), f), 1)
    o["iota"] = np.broadcast_to(np.arange(P, dtype=f), (P, P))
    o["iota8"] = np.broadcast_to(np.arange(NE, dtype=f), (P, NE))
    tile = np.arange(TILES)
    o["tile_start"] = np.broadcast_to((np.arange(NT) * P).astype(f), (P, NT))
    o["first_slot"] = np.broadcast_to((tile % NT * P).astype(f), (P, TILES))
    o["keep"] = np.broadcast_to((tile % NT > 0).astype(f), (P, TILES))
    o["batch_start"] = np.broadcast_to((tile // NT * NE).astype(f), (P, TILES))
    layout_mlstm(g, o)
    layout_layer1(g, o)
    return o


def build(nc, d, out):
    def scratch(name, shape, dt=F32):
        return nc.dram_tensor(name, shape, dt).ap()

    xn0 = scratch("xn0", [NB, S, E])
    xn0T = scratch("xn0T", [P, NB * S])
    route = scratch("route", [P, NB * NE, 2 * SC])
    texp = scratch("texp", [1, 2 * TILES], I32)
    kst = scratch("kst", [NB * NE, 2 * KQ, NH // 2, S], BF16)
    v = scratch("v", [NB * NE, P, SC, NH, HD + 1])
    moe = scratch("moe", [TILES, P, SC, E])
    ml = scratch("ml", [NB, S, E])
    x1 = scratch("x1", [NB, S, E])
    xn1 = scratch("xn1", [NB, S, E])
    xn1T = scratch("xn1T", [P, NB * S])
    at = scratch("at", [NB, S, E])
    norm_phase(nc, "n0", d["x"], xn0, xn0T, d["identity"])
    router_phase(nc, d, xn0T, route, texp)
    kv_phase(nc, d, xn0T, kst, v)
    experts_phase(nc, d, xn0, kst, v, route, texp, moe)
    mlstm_phase(nc, d, xn0T, ml)
    norm_phase(nc, "n1", d["x"], xn1, xn1T, d["identity"], sum_dram=x1,
               adds=(lambda b: ml[b].rearrange("(c p) e -> p c e", p=P), lambda b: moe[b * NT + NT - 1]))
    cross_phase(nc, d, xn1T, at)
    ffn_phase(nc, d, xn1, x1, at, out)


def kernel(**inputs):
    import numpy as _np
    import concourse.bacc as _bacc
    from concourse.bass_utils import run_bass_kernel_spmd as _run

    nc = _bacc.Bacc("TRN2", target_bir_lowering=False, num_devices=1)
    arrays = {f"in_{n}": _np.ascontiguousarray(a) for n, a in layout(inputs).items()}
    d = {n[3:]: nc.dram_tensor(n, a.shape, mybir.dt.from_np(a.dtype), kind="ExternalInput").ap()
         for n, a in arrays.items()}
    out = nc.dram_tensor("out", (NB, S, E), F32, kind="ExternalOutput").ap()
    build(nc, d, out)
    r = _run(nc, [arrays], core_ids=[0])
    return r.results[0]["out"]
```
